# Optimizing a Trainium2 kernel written in Bass

```python
import numpy as np
import jax
import jax.numpy as jnp

def _softmax(x, axis=-1):
    return jax.nn.softmax(x, axis=axis)

def _gelu(x):
    return jax.nn.gelu(x, approximate=True)

def _silu(x):
    return jax.nn.silu(x)

def _sigmoid(x):
    return jax.nn.sigmoid(x)

def _layernorm(x, axis=-1, eps=1e-05):
    m = jnp.mean(x, axis=axis, keepdims=True)
    v = jnp.var(x, axis=axis, keepdims=True)
    return (x - m) / jnp.sqrt(v + eps)

def _scatter_add(tgt, idx, src, axis=0):
    return tgt.at[idx].add(src)

def _segment_sum(src, seg, n):
    return jax.ops.segment_sum(src, seg, n)
kernel_name = 'mk_adaln_d1_jaxref_r4_191584'

def setup_inputs(seed: int=0):
    np.random.seed(seed)
    _w = jnp.asarray

    def _L0_attn_setup():
        import jax, jax.numpy as jnp
        import numpy as np
        D_MODEL = 256
        N_HEADS = 16
        D_HEAD = D_MODEL // N_HEADS
        EPS = 1e-06

        def _phi(x):
            return jax.nn.elu(x) + 1.0
        key = jax.random.key(seed)
        k1, k2, k3 = jax.random.split(key, 3)
        x = jax.random.normal(k1, (4, 1024, D_MODEL), dtype=jnp.float32)
        s = 1.0 / np.sqrt(D_MODEL)
        w_qkv = jax.random.uniform(k2, (3 * D_MODEL, D_MODEL), minval=-s, maxval=s, dtype=jnp.float32)
        w_out = jax.random.uniform(k3, (D_MODEL, D_MODEL), minval=-s, maxval=s, dtype=jnp.float32)
        return {'x': x, 'w_qkv': w_qkv, 'w_out': w_out}
    _L0_attn_in = _L0_attn_setup()

    def _L0_ffn_setup():
        import math
        import jax, jax.numpy as jnp
        import numpy as np
        D_MODEL = 256
        D_HIDDEN = 512
        N_EXPERTS = 8
        TOP_K = 2
        CAPACITY_FACTOR = 1.25

        def _moe_forward(x, w_router, w_gate, w_down):
            B, T, D = x.shape
            N = B * T
            xf = x.reshape(N, D)
            logits = xf.astype(jnp.float32) @ w_router.T
            gates = jax.nn.softmax(logits, axis=-1)
            topk_gates, topk_idx = jax.lax.top_k(gates, TOP_K)
            expert_mask = jax.nn.one_hot(topk_idx, N_EXPERTS, dtype=jnp.int32).sum(axis=1)
            capacity = math.ceil(N / N_EXPERTS * CAPACITY_FACTOR)
            position_in_expert = jnp.cumsum(expert_mask, axis=0) - 1
            expert_mask = expert_mask * (position_in_expert < capacity)
            keep = jnp.take_along_axis(expert_mask, topk_idx, axis=1) > 0
            topk_gates = topk_gates * keep
            topk_gates = topk_gates / (topk_gates.sum(axis=-1, keepdims=True) + 1e-06)
            hidden = jax.nn.silu(xf @ w_gate.T)
            combine = (topk_gates[:, :, None] * jax.nn.one_hot(topk_idx, N_EXPERTS, dtype=topk_gates.dtype)).sum(axis=1)
            y = jnp.zeros((N, D), dtype=x.dtype)
            for e in range(N_EXPERTS):
                y = y + combine[:, e:e + 1] * (hidden @ w_down[e].T)
            return y.reshape(B, T, D)
        key = jax.random.key(seed)
        k0, k1, k2, k3 = jax.random.split(key, 4)
        B, T = (2, 512)
        x = jax.random.normal(k0, (B, T, D_MODEL), dtype=jnp.float32)
        w_router = jax.random.normal(k1, (N_EXPERTS, D_MODEL), dtype=jnp.float32) * 0.02
        w_gate = jax.random.normal(k2, (D_HIDDEN, D_MODEL), dtype=jnp.float32) * 0.02
        w_down = jax.random.normal(k3, (N_EXPERTS, D_MODEL, D_HIDDEN), dtype=jnp.float32) * 0.02
        return {'x': x, 'w_router': w_router, 'w_gate': w_gate, 'w_down': w_down}
    _L0_ffn_in = _L0_ffn_setup()
    _L0_c = _w((lambda *s: np.random.randn(*s).astype(np.float32) * 0.05)(4, 256))
    _L0_wmod = _w((lambda *s: np.random.randn(*s).astype(np.float32) * 0.05)(256, 6 * 256) * 256 ** (-0.5))
    _d = {'L0_attn_x': _L0_attn_in['x'], 'L0_attn_w_qkv': _L0_attn_in['w_qkv'], 'L0_attn_w_out': _L0_attn_in['w_out'], 'L0_ffn_w_router': _L0_ffn_in['w_router'], 'L0_ffn_w_gate': _L0_ffn_in['w_gate'], 'L0_ffn_w_down': _L0_ffn_in['w_down'], 'L0_c': _L0_c, 'L0_wmod': _L0_wmod}
    _x0 = _d['L0_attn_x']
    _d['L0_attn_x'] = jax.random.normal(jax.random.fold_in(jax.random.key(seed), 1), (4, 2048, 256), dtype=_x0.dtype)
    del _x0
    return _d

def reference(L0_attn_x, L0_attn_w_qkv, L0_attn_w_out, L0_ffn_w_router, L0_ffn_w_gate, L0_ffn_w_down, L0_c, L0_wmod):

    def _L0_attn_ref(x, w_qkv, w_out):
        import jax, jax.numpy as jnp
        import numpy as np
        D_MODEL = 256
        N_HEADS = 16
        D_HEAD = D_MODEL // N_HEADS
        EPS = 1e-06

        def _phi(x):
            return jax.nn.elu(x) + 1.0
        B, L, D = x.shape
        H, dh = (N_HEADS, D_HEAD)
        qkv = jnp.einsum('bld,ed->ble', x, w_qkv)
        qkv = qkv.reshape(B, L, 3, H, dh).transpose(2, 0, 3, 1, 4)
        q, k, v = (_phi(qkv[0]), _phi(qkv[1]), qkv[2])
        qT = q.transpose(2, 0, 1, 3)
        kT = k.transpose(2, 0, 1, 3)
        vT = v.transpose(2, 0, 1, 3)
        S0 = jnp.zeros((B, H, dh, dh), dtype=x.dtype)
        z0 = jnp.zeros((B, H, dh), dtype=x.dtype)

        def step(carry, inp):
            S, z = carry
            q_t, k_t, v_t = inp
            S = S + k_t[..., :, None] * v_t[..., None, :]
            z = z + k_t
            num = jnp.einsum('bhde,bhd->bhe', S, q_t)
            den = jnp.maximum(jnp.sum(z * q_t, axis=-1, keepdims=True), EPS)
            return ((S, z), num / den)
        _, out = jax.lax.scan(step, (S0, z0), (qT, kT, vT))
        out = out.transpose(1, 0, 2, 3).reshape(B, L, D)
        return jnp.einsum('bld,ed->ble', out, w_out)

    def _L0_ffn_ref(x, w_router, w_gate, w_down):
        import math
        import jax, jax.numpy as jnp
        import numpy as np
        D_MODEL = 256
        D_HIDDEN = 512
        N_EXPERTS = 8
        TOP_K = 2
        CAPACITY_FACTOR = 1.25

        def _moe_forward(x, w_router, w_gate, w_down):
            B, T, D = x.shape
            N = B * T
            xf = x.reshape(N, D)
            logits = xf.astype(jnp.float32) @ w_router.T
            gates = jax.nn.softmax(logits, axis=-1)
            topk_gates, topk_idx = jax.lax.top_k(gates, TOP_K)
            expert_mask = jax.nn.one_hot(topk_idx, N_EXPERTS, dtype=jnp.int32).sum(axis=1)
            capacity = math.ceil(N / N_EXPERTS * CAPACITY_FACTOR)
            position_in_expert = jnp.cumsum(expert_mask, axis=0) - 1
            expert_mask = expert_mask * (position_in_expert < capacity)
            keep = jnp.take_along_axis(expert_mask, topk_idx, axis=1) > 0
            topk_gates = topk_gates * keep
            topk_gates = topk_gates / (topk_gates.sum(axis=-1, keepdims=True) + 1e-06)
            hidden = jax.nn.silu(xf @ w_gate.T)
            combine = (topk_gates[:, :, None] * jax.nn.one_hot(topk_idx, N_EXPERTS, dtype=topk_gates.dtype)).sum(axis=1)
            y = jnp.zeros((N, D), dtype=x.dtype)
            for e in range(N_EXPERTS):
                y = y + combine[:, e:e + 1] * (hidden @ w_down[e].T)
            return y.reshape(B, T, D)
        return _moe_forward(x, w_router, w_gate, w_down)
    x = L0_attn_x
    mod = (_silu(L0_c) @ L0_wmod).reshape(L0_c.shape[0], 6, 1, -1)
    sa, ca, ga, sb, cb, gb = (mod[:, 0], mod[:, 1], mod[:, 2], mod[:, 3], mod[:, 4], mod[:, 5])
    ga = (2 * (ga >= 0) - 1) * jnp.maximum(jnp.abs(ga), 0.25)
    gb = (2 * (gb >= 0) - 1) * jnp.maximum(jnp.abs(gb), 0.25)
    h = _layernorm(x, axis=-1) * (1 + ca) + sa
    x = x + ga * _L0_attn_ref(h, L0_attn_w_qkv, L0_attn_w_out)
    h = _layernorm(x, axis=-1) * (1 + cb) + sb
    x = x + gb * _L0_ffn_ref(h, L0_ffn_w_router, L0_ffn_w_gate, L0_ffn_w_down)
    return x

_drawn_inputs = setup_inputs


def setup_inputs(seed=0):
    import zlib

    import numpy as np

    out = dict(_drawn_inputs(seed))
    spreads = {}
    factors = {'L0_attn_w_qkv': 8.0,
     'L0_attn_w_out': 8.0,
     'L0_ffn_w_router': 5.86,
     'L0_ffn_w_gate': 5.214,
     'L0_ffn_w_down': 5.135,
     'L0_c': 4.64,
     'L0_wmod': 4.574}
    for name, (base, spread) in spreads.items():
        noise = np.random.default_rng([zlib.crc32(name.encode()), seed]).standard_normal(out[name].shape)
        drawn = base * np.exp(spread * noise) if base else spread * noise
        out[name] = jnp.asarray(drawn.astype(out[name].dtype))
    for name, factor in factors.items():
        out[name] = (out[name] * factor).astype(out[name].dtype)
    return out
```

```python
from contextlib import ExitStack

import concourse.bass as bass
from concourse import mybir

F32 = mybir.dt.float32
BF16 = mybir.dt.bfloat16
I32 = mybir.dt.int32
ALU = mybir.AluOpType
ACT = mybir.ActivationFunctionType
AX_X = mybir.AxisListType.X

P = 128
D = 256
DC = D // P
H = 16
DH = D // H
HC = H // DC
VW = 32
SW = DH + 1
BATCH = 4
SEQ = 2048
TOK = BATCH * SEQ
TILES = TOK // P
GT = 4
GROUPS = TILES // GT
GW = GT * P
E = 8
F = 512
FC = F // P
CAP = 1280
SLOTS = E * CAP
ROW = D + 4
BW = 256
BS = CAP // BW
BIG = 1.0e5
LN_EPS = 1e-5
DEN_EPS = 1e-6
NR = 29


def adaln_block(nc, x, wqkv, wo, wr, wg, wd, c, wmod, out, xe, ybuf):
    with ExitStack() as ctx:
        def sb(name, shape, dt=F32):
            return ctx.enter_context(nc.sbuf_tensor(name, shape, dt))

        def ps(name):
            return ctx.enter_context(nc.psum_tensor(name, [P, 512], F32))

        def sem(name):
            return ctx.enter_context(nc.semaphore(name))

        X = sb("X", [P, TILES, D])
        Sm = sb("Sm", [P, 2, H, P])
        QT = sb("QT", [P, 2, DC, GW])
        QM = sb("QM", [P, 2, 2, DC, GW])
        KT = sb("KT", [P, 2, DC, GW])
        VA = sb("VA", [P, 2, GT, H, VW])
        hT = sb("hT", [P, DC, GW])
        N1 = sb("N1", [P, GT, D])
        N2 = sb("N2", [P, GT, D])
        Hrow = sb("Hrow", [P, 2, GT, ROW])
        h2T = sb("h2T", [P, DC, GW])
        EX = sb("EX", [P, 4, GW])
        Kn = sb("Kn", [P, 2, D])
        Sbd = sb("Sbd", [P, H, VW])
        OTs = sb("OTs", [P, GT, P])
        An = sb("An", [P, H, DH])
        ATs = sb("ATs", [P, DC, P])
        og = sb("og", [P, D])
        w_qkv = sb("w_qkv", [P, DC, 3 * D])
        w_o = sb("w_o", [P, DC, D])
        w_r = sb("w_r", [P, DC, E])
        w_g = sb("w_g", [P, DC, F])
        cT = sb("cT", [P, DC, BATCH])
        cS = sb("cS", [P, DC, BATCH])
        saca = sb("saca", [P, 2 * DC, BATCH])
        MB = sb("MB", [P, BATCH, 4, D])
        ident = sb("ident", [P, P])
        tri = sb("tri", [P, P])
        before = sb("before", [P, P], BF16)
        ones = sb("ones", [P, P], BF16)
        headmask = sb("headmask", [P, H, SW])
        pairmask = sb("pairmask", [P, GT])
        parity = sb("parity", [P, 2])
        rev = sb("rev", [P, E])
        base = sb("base", [P, E])
        eid = sb("eid", [P, E])
        tokf = sb("tokf", [P, GT])
        carry = sb("carry", [P, 4, 2])
        mhalf = sb("mhalf", [P, GT])
        idle = sb("idle", [P, 5])
        zrow = sb("zrow", [P, 1, D])
        erow = sb("erow", [P, 1, ROW])
        st1 = sb("st1", [P, GT, 6])
        mv1 = sb("mv1", [P, GT, 2])
        vp1 = sb("vp1", [P, GT])
        rs1 = sb("rs1", [P, GT])
        st2 = sb("st2", [P, GT, 6])
        mv2 = sb("mv2", [P, GT, 2])
        vp2 = sb("vp2", [P, GT])
        rs2 = sb("rs2", [P, GT])
        den = sb("den", [P, H])
        rden = sb("rden", [P, H])
        lg = sb("lg", [P, GT, E])
        pos = sb("pos", [P, GT, E])
        lmax = sb("lmax", [P, GT])
        lp = sb("lp", [P, GT, E])
        lp2 = sb("lp2", [P, GT, E])
        cand = sb("cand", [P, GT, E])
        rk = sb("rk", [P, 2, GT])
        oh = sb("oh", [P, 2, GT, E])
        m2 = sb("m2", [P, GT])
        mask = sb("mask", [P, GT, E], BF16)
        msum = sb("msum", [P, E])
        macc = sb("macc", [P, E], BF16)
        drop = sb("drop", [P, GT, E])
        pbase = sb("pbase", [P, GT, E])
        pick = sb("pick", [P, 2, GT, E])
        slot = sb("slot", [P, 2, GT])
        sloti = sb("sloti", [P, 2, GT], I32)
        keep = sb("keep", [P, 2, GT])
        ee = sb("ee", [P, GT, E])
        e12 = sb("e12", [P, 2, GT])
        esum = sb("esum", [P, GT])
        gk = sb("gk", [P, 2, GT])
        Smf = Sm[:].rearrange("p a h i -> p (a h i)")
        wmod_sb = Smf[:, 0:DC * 6 * D].rearrange("p (a n) -> p a n", a=DC)
        KTf = KT[:].rearrange("p a c n -> p (a c n)")
        QTf = QT[:].rearrange("p a c n -> p (a c n)")
        EXf = EX[:].rearrange("p a n -> p (a n)")
        hid = [Smf[:, i * 1024:(i + 1) * 1024].rearrange("p (f n) -> p f n", f=FC) for i in range(2)]
        WD = [Smf[:, 2048 + i * 1024:3072 + i * 1024].rearrange("p (f n) -> p f n", f=FC) for i in range(2)]
        Xr = [Hrow[:, i // 2, (i % 2) * 2:(i % 2) * 2 + 2, :] for i in range(4)]
        Xr.append(QTf[:, 0:2 * ROW].rearrange("p (a r) -> p a r", a=2))
        XT = [KTf[:, i * 512:(i + 1) * 512].rearrange("p (c n) -> p c n", c=DC) for i in range(2)]
        Ys = [KTf[:, 1024 + i * 512:1536 + i * 512].rearrange("p (a n) -> p a n", a=2) for i in range(2)]
        bs = [EXf[:, i * 32:(i + 1) * 32] for i in range(2)]
        desti = [sb(f"desti{i}", [P, 2], I32) for i in range(2)]
        QMf = QM[:].rearrange("p a b c n -> p (a b c n)")
        YC = [QMf[:, i * 2048:(i + 1) * 2048].rearrange("p (k t d) -> p k t d", k=2, t=GT) for i in range(2)]

        PJ = [ps("PJ0"), ps("PJ1")]
        SC = [ps("SC0"), ps("SC1")]
        OB = ps("OB")
        SB = ps("SB")
        MA = ps("MA")
        MD = ps("MD")

        x_in = [sem("x_in0"), sem("x_in1")]
        w_in = sem("w_in")
        c_in = sem("c_in")
        init_out = sem("init_out")
        fills = sem("fills")
        consts = sem("consts")
        wipe = sem("wipe")
        c_silu = sem("c_silu")
        mod_mm = sem("mod_mm")
        mod_ev = sem("mod_ev")
        mb_ev = sem("mb_ev")
        gate_fix = sem("gate_fix")
        dve_setup = sem("dve_setup")
        bn1 = sem("bn1")
        ag1 = sem("ag1")
        vpe1 = sem("vpe1")
        rstd1 = sem("rstd1")
        n1_ready = sem("n1_ready")
        pj_full = sem("pj_full")
        pj_read = sem("pj_read")
        phi_done = sem("phi_done")
        qm_done = sem("qm_done")
        sc_full = sem("sc_full")
        sm_done = sem("sm_done")
        knt_full = sem("knt_full")
        kn_done = sem("kn_done")
        state_full = sem("state_full")
        sbd_done = sem("sbd_done")
        av_done = sem("av_done")
        ot_done = sem("ot_done")
        on_full = sem("on_full")
        den_done = sem("den_done")
        rden_done = sem("rden_done")
        an_done = sem("an_done")
        at_full = sem("at_full")
        at_done = sem("at_done")
        op_full = sem("op_full")
        og_done = sem("og_done")
        x1_done = sem("x1_done")
        bn2 = sem("bn2")
        ag2 = sem("ag2")
        vpe2 = sem("vpe2")
        rstd2 = sem("rstd2")
        n2_ready = sem("n2_ready")
        h2_scaled = sem("h2_scaled")
        h2_done = sem("h2_done")
        h2t_full = sem("h2t_full")
        h2t_done = sem("h2t_done")
        lg_full = sem("lg_full")
        taken = sem("taken")
        route = sem("route")
        gexp = sem("gexp")
        pos_full = sem("pos_full")
        breath = sem("breath")
        sent = [sem("sent0"), sem("sent1")]
        rows_in = [sem(f"rows_in{i}") for i in range(BS)]
        wd_in = [sem("wd_in0"), sem("wd_in1")]
        xt_full = sem("xt_full")
        xt_done = sem("xt_done")
        gate_full = sem("gate_full")
        hid_done = sem("hid_done")
        y_full = sem("y_full")
        meta = sem("meta")
        ys_done = sem("ys_done")
        y_sent = [sem("y_sent0"), sem("y_sent1")]
        yc_in = [sem("yc_in0"), sem("yc_in1")]
        comb = sem("comb")
        stored = sem("stored")

        N_CONST = 16
        block = ctx.enter_context(nc.Block())

        def at_least(eng, s, n):
            if not (isinstance(n, int) and n <= 0):
                eng.wait_ge(s, n)

        def run_slots(eng, slot):
            for it in (-1, 0, 1):
                for j in range(8):
                    slot(it, j, it * 8 + j)
            with eng.Fori(2, TILES // 8 - 1) as it:
                for j in range(8):
                    slot(it, j, 24 + j)
            for it in (TILES // 8 - 1, TILES // 8):
                for j in range(8):
                    slot(it, j, it * 8 + j)
            for j in range(2):
                slot(TILES // 8 + 1, j, TILES + 8 + j)

        def tile_ok(n):
            return 0 <= n < TILES

        def group_ok(n):
            return 0 <= n < GROUPS

        def halves(it, back):
            return (it - back) // 2 if isinstance(it, int) else (it - back) // 2

        def headslot(r):
            return [2 * r, 2 * r + 1]

        @block.sync
        def _(sp):
            xg = x.rearrange("(g t p) d -> g p t d", t=GT, p=P)
            sp.dma_start(X[:, 0:GT, :], xg[0]).then_inc(x_in[0], 16)
            sp.dma_start(X[:, GT:2 * GT, :], xg[1]).then_inc(x_in[1], 16)
            with sp.Fori(1, GROUPS // 2) as i:
                for k in range(2):
                    sp.wait_ge(x_in[k], i * 16)
                    sp.dma_start(X[:, bass.ds(i * (2 * GT) + k * GT, GT), :],
                                 x[bass.ds((i * 2 + k) * GW, GW), :].rearrange("(t p) d -> p t d", p=P)
                                 ).then_inc(x_in[k], 16)
            for k in range(2):
                sp.wait_ge(sent[k], 128 * (GROUPS // 2))
            sp.wait_ge(av_done, TILES)
            sp.wait_ge(route, NR * GROUPS)

            def load_rows(ep, s, n):
                S = ep * (2 * BS) + s
                if n >= BS:
                    sp.wait_ge(ys_done, 2 * (S - BS) + 2)
                sp.dma_start(Xr[s % BS],
                             xe[bass.ds(S * BW, BW), :].rearrange("(a p) r -> p a r", p=P)
                             ).then_inc(rows_in[s % BS], 16)

            def load_wd(ep, k, n):
                if n >= 1:
                    sp.wait_ge(y_full, (ep * 2 + k - 1) * BS)
                sp.dma_start(WD[k].rearrange("p f n -> p (f n)"),
                             wd[bass.ds((ep * 2 + k) * P, P), :]).then_inc(wd_in[k], 16)

            def expert_pair(ep, n):
                for s in range(2 * BS):
                    if s % BS == 0:
                        load_wd(ep, s // BS, n)
                    load_rows(ep, s, 10 * n + s)

            expert_pair(0, 0)
            with sp.Fori(1, E // 2) as ep:
                expert_pair(ep, 1)

            for k in range(2):
                sp.wait_ge(y_sent[k], 32 * (E * BS // 2))
            sp.wait_ge(ys_done, 2 * E * BS)

            def load_y(i, k, n):
                if n >= 1:
                    sp.wait_ge(comb, 3 * (i * 2 + k - 2) + 1)
                for kk in range(2):
                    sp.dma_start(YC[k][:, kk],
                                 ybuf[bass.ds((i * 2 + k) * GW + kk * TOK, GW), :].rearrange("(t p) d -> p t d", p=P)
                                 ).then_inc(yc_in[k], 16)
            for k in range(2):
                load_y(0, k, 0)
            with sp.Fori(1, GROUPS // 2) as i:
                for k in range(2):
                    load_y(i, k, 1)

        @block.gpsimd
        def _(pool):
            pool.memset(zrow[:], 0.0).then_inc(fills, 1)
            pool.memset(erow[:], 0.0).then_inc(fills, 1)
            pool.memset(ident[:], 1.0).then_inc(fills, 1)
            pool.memset(tri[:], 1.0).then_inc(fills, 1)
            pool.memset(headmask[:], 1.0).then_inc(fills, 1)
            pool.memset(pairmask[:], 1.0).then_inc(fills, 1)
            pool.memset(before[:], 1.0).then_inc(fills, 1)
            pool.memset(ones[:], 1.0).then_inc(consts, 1)
            pool.memset(Sbd[:], 0.0).then_inc(consts, 1)
            pool.memset(mhalf[:], -0.5).then_inc(consts, 1)
            pool.memset(macc[:], 0.0).then_inc(consts, 1)
            pool.memset(e12[:], 1.0).then_inc(consts, 1)
            pool.iota(rev[:], [[-1, E]], base=E, channel_multiplier=0,
                      allow_small_or_imprecise_dtypes=True).then_inc(consts, 1)
            pool.iota(base[:], [[CAP, E]], base=0, channel_multiplier=0,
                      allow_small_or_imprecise_dtypes=True).then_inc(consts, 1)
            pool.iota(eid[:], [[1, E]], base=0, channel_multiplier=0,
                      allow_small_or_imprecise_dtypes=True).then_inc(consts, 1)
            pool.iota(tokf[:], [[P, GT]], base=0, channel_multiplier=1,
                      allow_small_or_imprecise_dtypes=True).then_inc(consts, 1)
            pool.iota(carry[:], [[0, 4], [-1, 2]], base=1, channel_multiplier=0,
                      allow_small_or_imprecise_dtypes=True).then_inc(consts, 1)
            pool.wait_ge(fills, 7)
            pool.memset(erow[:, :, D + 2:D + 3], BIG).then_inc(consts, 1)
            pool.affine_select(out=ident[:], in_=ident[:], pattern=[[-1, P]], compare_op=ALU.is_equal, fill=0.0,
                               base=0, channel_multiplier=1).then_inc(consts, 1)
            pool.affine_select(out=tri[:], in_=tri[:], pattern=[[1, P]], compare_op=ALU.is_ge, fill=0.0,
                               base=0, channel_multiplier=-1).then_inc(consts, 1)
            pool.affine_select(out=before[:], in_=before[:], pattern=[[1, P]], compare_op=ALU.is_gt, fill=0.0,
                               base=0, channel_multiplier=-1).then_inc(consts, 1)
            hm = headmask[:].rearrange("p (c s) w -> p c s w", c=DC)
            pool.affine_select(out=hm, in_=hm, pattern=[[0, DC], [-DH, HC], [0, SW]], compare_op=ALU.is_ge,
                               fill=0.0, base=0, channel_multiplier=1).then_inc(wipe, 1)
            pool.affine_select(out=pairmask[:], in_=pairmask[:], pattern=[[-2 * DH, GT]], compare_op=ALU.is_ge,
                               fill=0.0, base=0, channel_multiplier=1).then_inc(wipe, 1)
            pool.wait_ge(wipe, 2)
            pool.affine_select(out=hm, in_=hm, pattern=[[0, DC], [DH, HC], [0, SW]], compare_op=ALU.is_ge,
                               fill=0.0, base=DH - 1, channel_multiplier=-1).then_inc(consts, 1)
            pool.affine_select(out=pairmask[:], in_=pairmask[:], pattern=[[2 * DH, GT]], compare_op=ALU.is_ge,
                               fill=0.0, base=DH - 1, channel_multiplier=-1).then_inc(consts, 1)

            def breather(k):
                pool.tensor_tensor(idle[:, k:k + 1], mhalf[:, 0:1], mhalf[:, 0:1], ALU.add).then_inc(breath, 1)

            def slot_(it, j, n):
                T = it * 8 + j
                G = it * 2 + j // 4
                gn, q, gp = n // 4, j % 4, (j // 4) % 2
                if q == 2 and group_ok(gn + 2):
                    pool.wait_ge(vpe1, G + 3)
                    pool.tensor_tensor(rs1[:], vp1[:], mhalf[:], ALU.pow).then_inc(rstd1, 1)
                if q == 1 and group_ok(gn - 1):
                    pool.wait_ge(vpe2, G)
                    pool.tensor_tensor(rs2[:], vp2[:], mhalf[:], ALU.pow).then_inc(rstd2, 1)
                leaving = q < 2 and group_ok(gn - 3)
                if leaving and q == 0:
                    pool.wait_ge(route, NR * (G - 3) + NR)
                    if gn == 3:
                        pool.wait_ge(init_out, 32)
                def modulate():
                    hp = 1 - gp
                    if q == 2:
                        if group_ok(gn - 3):
                            pool.wait_ge(sent[hp], 128 * ((it - 1) if gp == 0 else it))
                    b = halves(it, 0 if gp == 1 else 1)
                    pool.wait_ge(n2_ready, 4 * (G - 1) + 2 * (q - 1))
                    breather(2 * q - 4)
                    for t in (2 * q - 4, 2 * q - 3):
                        pool.tensor_tensor(N2[:, t, :], N2[:, t, :],
                                           MB[:, bass.ds(b, 1), 2, :].rearrange("p a d -> p (a d)"),
                                           ALU.mult).then_inc(h2_scaled, 1)
                    pool.wait_ge(h2_scaled, 4 * (G - 1) + 2 * (q - 1))
                    breather(2 * q - 3)
                    for t in (2 * q - 4, 2 * q - 3):
                        pool.tensor_tensor(Hrow[:, hp, t, 0:D], N2[:, t, :],
                                           MB[:, bass.ds(b, 1), 1, :].rearrange("p a d -> p (a d)"),
                                           ALU.add).then_inc(h2_done, 1)

                if q == 3 and group_ok(gn - 1):
                    modulate()
                if tile_ok(n - 1):
                    pool.wait_ge(og_done, T)
                    xt = X[:, bass.ds(T - 1, 1), :].rearrange("p a d -> p (a d)")
                    pool.tensor_tensor(xt, xt, og[:], ALU.add).then_inc(x1_done, 1)
                if q == 2 and group_ok(gn - 1):
                    modulate()
                if leaving:
                    for t in (2 * q, 2 * q + 1):
                        for k in range(2):
                            pool.indirect_dma_start(
                                xe, bass.IndirectOffsetOnAxis(sloti[:, k, t:t + 1], 0), Hrow[:, 1 - gp, t, :], None,
                                bounds_check=SLOTS - 1, oob_is_err=False).then_inc(sent[1 - gp], 16)

            pool.wait_ge(consts, N_CONST)
            pool.wait_ge(gate_fix, 10)
            run_slots(pool, slot_)

            def give_back(ep, s, n):
                S = ep * (2 * BS) + s
                pool.wait_ge(breath, 4 * GROUPS + S)
                pool.wait_ge(ys_done, 2 * S + 2)
                breather(4)
                for a in range(2):
                    pool.indirect_dma_start(
                        ybuf, bass.IndirectOffsetOnAxis(desti[s % 2][:, a:a + 1], 0), Ys[s % 2][:, a, :], None,
                        bounds_check=2 * TOK - 1, oob_is_err=False).then_inc(y_sent[s % 2], 16)

            with pool.Fori(0, E // 2) as ep:
                for s in range(2 * BS):
                    give_back(ep, s, 0)

        @block.scalar
        def _(act):
            act.dma_start(cT[:], c).then_inc(c_in, 16)
            act.dma_start(wmod_sb, wmod).then_inc(c_in, 16)
            for dst, src in ((w_qkv, wqkv), (w_o, wo), (w_r, wr), (w_g, wg)):
                act.dma_start(dst[:], src).then_inc(w_in, 16)
            act.wait_ge(consts, N_CONST)
            act.dma_start(xe.rearrange("(p n) r -> p n r", p=P),
                          erow[:].to_broadcast([P, SLOTS // P, ROW])).then_inc(init_out, 16)
            act.dma_start(ybuf.rearrange("(p n) r -> p n r", p=P),
                          zrow[:].to_broadcast([P, 2 * TOK // P, D])).then_inc(init_out, 16)
            act.wait_ge(c_in, 32)
            act.activation(cS[:], cT[:], ACT.Silu).then_inc(c_silu, 1)
            act.wait_ge(mod_mm, 1)
            act.activation(saca[:, 0:DC, :], MA[:, 0:DC * BATCH].rearrange("p (a b) -> p a b", a=DC),
                           ACT.Copy).then_inc(mod_ev, 1)
            act.activation(saca[:, DC:2 * DC, :],
                           MA[:, DC * BATCH:2 * DC * BATCH].rearrange("p (a b) -> p a b", a=DC),
                           ACT.Copy, bias=1.0).then_inc(mod_ev, 1)

            def stage1_transposed(it, G, cidx, bcol):
                N = G + 1
                act.wait_ge(pj_full, 8 * N + cidx + 1)
                act.activation(hT[:, cidx, :], PJ[cidx][:], ACT.Identity,
                               scale=saca[:, DC + cidx, bass.ds(bcol, 1)],
                               bias=saca[:, cidx, bass.ds(bcol, 1)]).then_inc(pj_read, 1)

            def stage1_qk(G, m, npar, n_next):
                N = G + 1
                act.wait_ge(pj_full, 8 * N + m + 3)
                if n_next >= 1:
                    act.wait_ge(phi_done, 4 * (N - 1) + m + 1)
                if n_next >= 2:
                    act.wait_ge(av_done, 4 * (N - 1))
                dst = QT if m < 2 else KT
                act.activation(EX[:, m, :], PJ[m % 2][:], ACT.Exp)
                act.activation(dst[:, npar, m % 2, :], PJ[m % 2][:], ACT.Relu).then_inc(pj_read, 1)

            def stage1_v(G, u, npar, n_next):
                N = G + 1
                act.wait_ge(pj_full, 8 * N + u + 7)
                if n_next >= 2:
                    act.wait_ge(av_done, 4 * (N - 1))
                act.activation(VA[:, npar, 2 * u:2 * u + 2, :, 0:DH],
                               PJ[u][:].rearrange("p (t h e) -> p t h e", t=2, h=H),
                               ACT.Copy).then_inc(pj_read, 1)

            def head_masks(G, cidx, npar, n_next):
                N = G + 1
                act.wait_ge(phi_done, 4 * N + cidx + 1)
                for odd in range(2):
                    act.activation(QM[:, npar, odd, cidx, :], QT[:, npar, cidx, :], ACT.Copy,
                                   scale=parity[:, odd:odd + 1]).then_inc(qm_done, 1)

            def slot_(it, j, n):
                T = it * 8 + j
                G = it * 2 + j // 4
                gn, q, gp = n // 4, j % 4, (j // 4) % 2
                npar, nx = 1 - gp, n // 4 + 1
                tp = j % 2
                stage1 = group_ok(nx)
                if q in (1, 3) and group_ok(gn - 2):
                    act.wait_ge(lg_full if q == 1 else pos_full, G - 1)
                    act.activation((lg if q == 1 else pos)[:], MD[:, 0:GT * E].rearrange("p (t e) -> p t e", t=GT),
                                   ACT.Copy).then_inc(taken, 1)
                if tile_ok(n - 1):
                    act.wait_ge(av_done, T)
                    at_least(act, on_full, T - 1)
                    act.activation(OTs[:].rearrange("p a i -> p (a i)"), OB[:], ACT.Copy).then_inc(ot_done, 1)
                if q == 0 and group_ok(gn - 2):
                    for cidx in range(DC):
                        act.wait_ge(h2t_full, 2 * (G - 2) + cidx + 1)
                        if gn >= 3:
                            act.wait_ge(lg_full, G - 2)
                        act.activation(h2T[:, cidx, :], PJ[cidx][:], ACT.Copy).then_inc(h2t_done, 1)
                if tile_ok(n):
                    act.wait_ge(knt_full, T + 1)
                    at_least(act, state_full, T - 1)
                    act.activation(Kn[:, tp, :], MA[:, 0:D], ACT.Copy).then_inc(kn_done, 1)
                if stage1:
                    if q == 0:
                        bcol = halves(it, 0) if gp == 0 else halves(it, -1)
                        if isinstance(bcol, int):
                            bcol = max(bcol, 0)
                        stage1_transposed(it, G, 0, bcol)
                        stage1_transposed(it, G, 1, bcol)
                    elif q == 1:
                        stage1_qk(G, 1, npar, nx)
                    elif q == 2:
                        stage1_qk(G, 3, npar, nx)
                    else:
                        stage1_v(G, 1, npar, nx)
                if tile_ok(n - 1):
                    act.wait_ge(at_full, T)
                    at_least(act, op_full, T - 1)
                    act.activation(ATs[:].rearrange("p c i -> p (c i)"), MA[:, 0:D], ACT.Copy).then_inc(at_done, 1)
                if stage1:
                    if q == 0:
                        stage1_qk(G, 0, npar, nx)
                    elif q == 1:
                        stage1_qk(G, 2, npar, nx)
                    elif q == 2:
                        head_masks(G, 0, npar, nx)
                        stage1_v(G, 0, npar, nx)
                    else:
                        head_masks(G, 1, npar, nx)
                if q == 2 and group_ok(gn - 2):
                    g = G - 2
                    act.wait_ge(route, NR * g + 8)
                    act.activation(ee[:], lp[:], ACT.Exp).then_inc(gexp, 1)
                    act.activation(e12[:, 1, :], m2[:], ACT.Exp).then_inc(gexp, 1)

            act.wait_ge(dve_setup, 2)
            act.wait_ge(mod_ev, 2)
            run_slots(act, slot_)

            def hidden(ep, s, n):
                S = ep * (2 * BS) + s
                for hh in range(2):
                    act.wait_ge(gate_full, 2 * S + hh + 1)
                    if n >= 2:
                        act.wait_ge(y_full, S - 1)
                    act.activation(hid[s % 2][:, 2 * hh:2 * hh + 2, :],
                                   SC[hh][:].rearrange("p (f n) -> p f n", f=2), ACT.Silu).then_inc(hid_done, 1)

            for s in range(2 * BS):
                hidden(0, s, s)
            with act.Fori(1, E // 2) as ep:
                for s in range(2 * BS):
                    hidden(ep, s, 10)

            with act.Fori(0, GROUPS) as g:
                act.wait_ge(comb, 3 * g + 3)
                act.dma_start(out[bass.ds(g * GW, GW), :].rearrange("(t p) d -> p t d", p=P),
                              X[:, bass.ds(g * GT, GT), :]).then_inc(stored, 16)
            act.wait_ge(stored, 16 * GROUPS)

        @block.vector
        def _(dve):
            dve.memset(VA[:], 1.0).then_inc(dve_setup, 1)
            dve.wait_ge(consts, N_CONST)
            dve.tensor_reduce(parity[:, 0:1], pairmask[:], AX_X, ALU.add).then_inc(gate_fix, 1)
            dve.wait_ge(gate_fix, 1)
            dve.tensor_scalar(parity[:, 1:2], parity[:, 0:1], -1.0, 1.0, ALU.mult, ALU.add).then_inc(dve_setup, 1)
            for b in range(BATCH):
                for hh in range(2):
                    dve.wait_ge(mod_mm, 2 + 2 * b + hh)
                    dve.tensor_copy(MB[:, b, 2 * hh:2 * hh + 2, :],
                                    SC[hh][:].rearrange("p (k d) -> p k d", k=2)).then_inc(mb_ev, 1)
            dve.wait_ge(mb_ev, 2 * BATCH)
            dve.tensor_scalar(MB[:, :, 2, :], MB[:, :, 2, :], 1.0, None, ALU.add).then_inc(gate_fix, 1)
            tmp = KTf[:, 0:BATCH * D].rearrange("p (b d) -> p b d", b=BATCH)
            sgn = QTf[:, 0:BATCH * D].rearrange("p (b d) -> p b d", b=BATCH)
            n = 2
            for kind in (0, 3):
                gate = MB[:, :, kind, :]
                dve.scalar_tensor_tensor(tmp, gate, -1.0, gate, ALU.mult, ALU.max).then_inc(gate_fix, 1)
                dve.tensor_scalar(sgn, gate, 0.0, 2.0, ALU.is_ge, ALU.mult).then_inc(gate_fix, 1)
                n += 2
                dve.wait_ge(gate_fix, n)
                dve.tensor_scalar(tmp, tmp, 0.25, None, ALU.max).then_inc(gate_fix, 1)
                n += 1
                dve.wait_ge(gate_fix, n)
                dve.scalar_tensor_tensor(gate, sgn, -1.0, tmp, ALU.add, ALU.mult).then_inc(gate_fix, 1)
                n += 1
                dve.wait_ge(gate_fix, n)

            def masked_scores(T, r, tp, n):
                dve.wait_ge(sc_full, 4 * T + r + 1)
                if r == 0 and n >= 2:
                    dve.wait_ge(av_done, T - 1)
                o = Sm[:, tp].rearrange("p (c s) i -> p c s i", c=DC)[:, :, 2 * r:2 * r + 2, :]
                dve.tensor_tensor(o, SC[r % 2][:].rearrange("p (c s i) -> p c s i", c=2, s=2),
                                  tri[:].unsqueeze(1).unsqueeze(1).to_broadcast([P, 2, 2, P]),
                                  ALU.mult).then_inc(sm_done, 1)

            def normalise_heads(T):
                on = MD[:].rearrange("p (h w) -> p h w", h=H)
                dve.wait_ge(on_full, T)
                dve.tensor_scalar(den[:].unsqueeze(2), on[:, :, DH:DH + 1], DEN_EPS, None, ALU.max).then_inc(den_done, 1)
                dve.wait_ge(den_done, T)
                dve.reciprocal(rden[:], den[:]).then_inc(rden_done, 1)
                dve.wait_ge(rden_done, T)
                at_least(dve, at_full, T - 1)
                dve.tensor_tensor(An[:], on[:, :, 0:DH], rden[:].unsqueeze(2).to_broadcast([P, H, DH]),
                                  ALU.mult).then_inc(an_done, 1)

            def state(it, T, j):
                keep_it = carry[:].rearrange("p a b -> p (a b)")[:, bass.ds(it, 1)] if j == 7 else 1.0
                dve.wait_ge(state_full, T + 1)
                dve.scalar_tensor_tensor(Sbd[:, :, 0:SW], SB[:, 0:H * SW].rearrange("p (h w) -> p h w", h=H),
                                         keep_it, headmask[:], ALU.mult, ALU.mult).then_inc(sbd_done, 1)

            def phi(G, m, npar):
                N = G + 1
                dst = (QT if m < 2 else KT)[:, npar, m % 2, :]
                dve.wait_ge(pj_read, 8 * N + m + 3)
                dve.scalar_tensor_tensor(dst, dst, 1.0, EX[:, m, :], ALU.add, ALU.min).then_inc(phi_done, 1)

            def ln_tail(st, mv, vp, s_ag, s_vp, count):
                for t in range(GT):
                    dve.bn_aggr(mv[:, t, :], st[:, t, :]).then_inc(s_ag, 1)
                dve.wait_ge(s_ag, 4 * count)
                dve.tensor_scalar(vp[:].unsqueeze(2), mv[:, :, 1:2], LN_EPS, None, ALU.add).then_inc(s_vp, 1)

            def ln1_stats(it, G, gp):
                L = G + 2
                xi = it + 2 if not isinstance(it, int) else it + 2
                dve.wait_ge(x_in[gp], 16 * xi)
                for t in range(GT):
                    dve.bn_stats(st1[:, t, :], X[:, bass.ds(L * GT + t, 1), :].rearrange("p a d -> p (a d)")
                                 ).then_inc(bn1, 1)
                dve.wait_ge(bn1, 4 * (L + 1))

            def ln1_norm(G, gl):
                L = G + 2
                dve.wait_ge(rstd1, L + 1)
                if gl >= 1:
                    dve.wait_ge(pj_full, 8 * (L - 1) + 2)
                for t in range(GT):
                    dve.tensor_scalar(N1[:, t, :], X[:, bass.ds(L * GT + t, 1), :].rearrange("p a d -> p (a d)"),
                                      mv1[:, t, 0:1], rs1[:, t:t + 1], ALU.subtract, ALU.mult).then_inc(n1_ready, 1)

            def ln2_norm(G, gn):
                g = G - 1
                dve.wait_ge(rstd2, G)
                if gn - 1 >= 1:
                    dve.wait_ge(h2_done, 4 * g)
                for t in range(GT):
                    dve.tensor_scalar(N2[:, t, :], X[:, bass.ds(g * GT + t, 1), :].rearrange("p a d -> p (a d)"),
                                      mv2[:, t, 0:1], rs2[:, t:t + 1], ALU.subtract, ALU.mult).then_inc(n2_ready, 1)

            revb = rev[:].unsqueeze(1).to_broadcast([P, GT, E])
            steps = [0]

            def step(ins):
                steps[0] += 1
                ins.then_inc(route, 1)

            def after(g):
                dve.wait_ge(route, NR * g + steps[0])

            def wide(a):
                return a.unsqueeze(2).to_broadcast([P, GT, E])

            def choose(g):
                steps[0] = 0
                dve.wait_ge(taken, 2 * g + 1)
                step(dve.tensor_reduce(lmax[:], lg[:], AX_X, ALU.max))
                after(g)
                step(dve.tensor_tensor(lp[:], lg[:], wide(lmax[:]), ALU.subtract))
                after(g)
                step(dve.tensor_scalar(lp[:], lp[:], -104.0, None, ALU.max))
                after(g)
                step(dve.scalar_tensor_tensor(cand[:], lp[:], 0.0, revb, ALU.is_equal, ALU.mult))
                after(g)
                step(dve.tensor_reduce(rk[:, 0, :], cand[:], AX_X, ALU.max))
                after(g)
                step(dve.tensor_tensor(oh[:, 0], revb, wide(rk[:, 0, :]), ALU.is_equal))
                after(g)
                step(dve.scalar_tensor_tensor(lp2[:], oh[:, 0], -1.0e30, lp[:], ALU.mult, ALU.add))
                after(g)
                step(dve.tensor_reduce(m2[:], lp2[:], AX_X, ALU.max))
                after(g)
                step(dve.tensor_tensor(cand[:], lp2[:], wide(m2[:]), ALU.is_equal))
                after(g)
                step(dve.tensor_tensor(cand[:], cand[:], revb, ALU.mult))
                after(g)
                step(dve.tensor_reduce(rk[:, 1, :], cand[:], AX_X, ALU.max))
                after(g)
                step(dve.tensor_tensor(oh[:, 1], revb, wide(rk[:, 1, :]), ALU.is_equal))
                after(g)
                step(dve.tensor_tensor(mask[:], oh[:, 0], oh[:, 1], ALU.add))

            def place(it, g, pg, gn):
                dve.wait_ge(taken, 2 * g + 2)
                step(dve.tensor_scalar(drop[:], pos[:], float(CAP), BIG, ALU.is_ge, ALU.mult))
                step(dve.tensor_tensor(pbase[:], pos[:], base[:].unsqueeze(1).to_broadcast([P, GT, E]), ALU.add))
                step(dve.tensor_reduce(msum[:], mask[:].rearrange("p t e -> p e t"), AX_X, ALU.add))
                step(dve.tensor_reduce(esum[:], ee[:], AX_X, ALU.add))
                after(g)
                step(dve.tensor_tensor(pbase[:], pbase[:], drop[:], ALU.add))
                step(dve.reciprocal(esum[:], esum[:]))
                step(dve.tensor_tensor(macc[:], macc[:], msum[:], ALU.add))
                after(g)
                step(dve.tensor_tensor(pick[:], oh[:], pbase[:].unsqueeze(1).to_broadcast([P, 2, GT, E]), ALU.mult))
                step(dve.tensor_tensor(gk[:], e12[:], esum[:].unsqueeze(1).to_broadcast([P, 2, GT]), ALU.mult))
                after(g)
                step(dve.tensor_reduce(slot[:], pick[:], AX_X, ALU.add))
                after(g)
                if gn >= 3:
                    dve.wait_ge(sent[1 - pg], 128 * ((it - 1) if pg == 0 else it))
                step(dve.tensor_copy(sloti[:], slot[:]))
                step(dve.scalar_tensor_tensor(gk[:], slot[:], BIG / 2, gk[:], ALU.is_lt, ALU.mult))
                after(g)
                step(dve.tensor_reduce(esum[:], gk[:].rearrange("p k t -> p t k"), AX_X, ALU.add))
                after(g)
                step(dve.tensor_scalar(esum[:], esum[:], 1e-6, None, ALU.add))
                after(g)
                step(dve.reciprocal(esum[:], esum[:]))
                after(g)
                row = Hrow[:, pg].rearrange("p t r -> p r t")
                step(dve.tensor_tensor(row[:, D:D + 2, :], gk[:],
                                       esum[:].unsqueeze(1).to_broadcast([P, 2, GT]), ALU.mult))

            def place_ids(g, pg):
                row = Hrow[:, pg].rearrange("p t r -> p r t")
                dve.tensor_scalar(row[:, D + 3:D + 4, :], rk[:, 0:1, :], -1.0, float(E), ALU.mult, ALU.add)
                dve.tensor_copy(row[:, D + 2:D + 3, :], tokf[:].unsqueeze(1))

            def slot_(it, j, n):
                T = it * 8 + j
                G = it * 2 + j // 4
                gn, q, gp = n // 4, j % 4, (j // 4) % 2
                npar = 1 - gp
                tp = j % 2
                stage1 = group_ok(gn + 1)
                if tile_ok(n):
                    masked_scores(T, 0, tp, n)
                    masked_scores(T, 1, tp, n)
                if tile_ok(n - 1):
                    normalise_heads(T)
                if tile_ok(n):
                    masked_scores(T, 2, tp, n)
                    masked_scores(T, 3, tp, n)
                    state(it, T, j)
                if tile_ok(n - 1):
                    b = halves(it, 0 if j >= 1 else 1)
                    dve.wait_ge(op_full, T)
                    at_least(dve, x1_done, T - 1)
                    dve.tensor_tensor(og[:], MD[:, 0:D], MB[:, bass.ds(b, 1), 0, :].rearrange("p a d -> p (a d)"),
                                      ALU.mult).then_inc(og_done, 1)
                if tile_ok(n - 2):
                    dve.wait_ge(x1_done, T - 1)
                    dve.bn_stats(st2[:, (j - 2) % 4, :], X[:, bass.ds(T - 2, 1), :].rearrange("p a d -> p (a d)")
                                 ).then_inc(bn2, 1)
                if q == 1:
                    if group_ok(gn - 1):
                        dve.wait_ge(bn2, 4 * G)
                    if stage1:
                        phi(G, 0, npar)
                        phi(G, 1, npar)
                    if group_ok(gn - 1):
                        ln_tail(st2, mv2, vp2, ag2, vpe2, G)
                    if group_ok(gn - 2):
                        choose(G - 2)
                if q == 2:
                    if stage1:
                        phi(G, 2, npar)
                        phi(G, 3, npar)
                    if group_ok(gn + 2):
                        ln1_stats(it, G, gp)
                    if group_ok(gn - 1):
                        ln2_norm(G, gn)
                    if group_ok(gn + 2):
                        ln_tail(st1, mv1, vp1, ag1, vpe1, G + 3)
                if q == 3:
                    if group_ok(gn + 2):
                        ln1_norm(G, gn + 2)
                    if group_ok(gn - 2):
                        steps[0] = 13
                        dve.wait_ge(gexp, 2 * (G - 2) + 2)
                        place_ids(G - 2, gp)
                        place(it, G - 2, gp, gn)
                        assert steps[0] == NR, steps[0]
                if q == 0 and group_ok(gn - 3):
                    dve.tensor_scalar(tokf[:], tokf[:], float(GW), None, ALU.add).then_inc(dve_setup, 1)

            run_slots(dve, slot_)

            def transposed_rows(S, par):
                dve.wait_ge(xt_full, S + 1)
                dve.tensor_copy(XT[par].rearrange("p c n -> p (c n)"), PJ[par][:]).then_inc(xt_done, 1)

            def slot_meta(ep, s, n):
                S, par, m = ep * (2 * BS) + s, s % 2, 4 * 0
                t = bs[par]
                first, other, wa, wb, w, dst = (t[:, 2 * i:2 * i + 2].unsqueeze(2) for i in range(6))
                row = Xr[s % BS]
                eno = eid[:, bass.ds(ep * 2 + s // BS, 1)]
                dve.wait_ge(rows_in[s % BS], 16 * (ep * 2 + s // BS + 1))
                dve.tensor_scalar(first, row[:, :, D + 3:D + 4], eno, None, ALU.is_equal).then_inc(meta, 1)
                dve.wait_ge(meta, 6 * S + 1)
                dve.tensor_scalar(other, first, -1.0, 1.0, ALU.mult, ALU.add).then_inc(meta, 1)
                dve.tensor_tensor(wa, row[:, :, D:D + 1], first, ALU.mult).then_inc(meta, 1)
                dve.wait_ge(meta, 6 * S + 3)
                dve.tensor_tensor(wb, row[:, :, D + 1:D + 2], other, ALU.mult).then_inc(meta, 1)
                dve.scalar_tensor_tensor(dst, other, float(TOK), row[:, :, D + 2:D + 3], ALU.mult,
                                         ALU.add).then_inc(meta, 1)
                dve.wait_ge(meta, 6 * S + 5)
                dve.tensor_tensor(w, wa, wb, ALU.add).then_inc(meta, 1)
                if n >= 2:
                    dve.wait_ge(y_sent[par], 32 * (ep * BS + s // 2))
                dve.wait_ge(meta, 6 * S + 6)
                dve.tensor_copy(desti[par][:].unsqueeze(2), dst)

            def weighted_rows(ep, s):
                S, par = ep * (2 * BS) + s, s % 2
                dve.wait_ge(y_full, S + 1)
                for a in range(2):
                    dve.tensor_scalar(Ys[par][:, a, :], (MA, MD)[par][:, a * D:(a + 1) * D],
                                      bs[par][:, 8 + a:9 + a], None, ALU.mult).then_inc(ys_done, 1)

            def step_b(ep, s, n, last):
                if not (last and s + 2 >= 2 * BS):
                    transposed_rows(ep * (2 * BS) + s + 2, s % 2)
                slot_meta(ep, s, n)
                weighted_rows(ep, s)

            transposed_rows(0, 0)
            transposed_rows(1, 1)
            for s in range(2 * BS):
                step_b(0, s, s, False)
            with dve.Fori(1, E // 2 - 1) as ep:
                for s in range(2 * BS):
                    step_b(ep, s, 10, False)
            for s in range(2 * BS):
                step_b(E // 2 - 1, s, 10, True)

            with dve.Fori(0, GROUPS // 2) as i:
                for k in range(2):
                    g = i * 2 + k
                    dve.wait_ge(yc_in[k], 32 * i + 32)
                    y = YC[k]
                    xs = X[:, bass.ds(g * GT, GT), :]
                    gb = MB[:, bass.ds(i // 2, 1), 3, :].to_broadcast([P, GT, D])
                    dve.tensor_tensor(N1[:], y[:, 0], y[:, 1], ALU.add).then_inc(comb, 1)
                    dve.wait_ge(comb, 3 * g + 1)
                    dve.tensor_tensor(N1[:], N1[:], gb, ALU.mult).then_inc(comb, 1)
                    dve.wait_ge(comb, 3 * g + 2)
                    dve.tensor_tensor(xs, xs, N1[:], ALU.add).then_inc(comb, 1)
                    dve.wait_ge(comb, 3 * g + 3)

        @block.tensor
        def _(pe):
            mm = pe.matmul
            pe.wait_ge(c_silu, 1)
            for m in range(2 * DC):
                for k in range(DC):
                    last = mm(MA[:, m * BATCH:(m + 1) * BATCH], wmod_sb[:, k, m * P:(m + 1) * P], cS[:, k, :],
                              start=(k == 0), stop=(k == DC - 1))
            last.then_inc(mod_mm, 1)
            for b in range(BATCH):
                for hh in range(2):
                    if b >= 1:
                        pe.wait_ge(mb_ev, 2 * (b - 1) + hh + 1)
                    for k in range(DC):
                        last = mm(SC[hh][:], cS[:, k, b:b + 1].to_broadcast([P, P]),
                                  wmod_sb[:, k, (2 + 2 * hh) * D:(4 + 2 * hh) * D],
                                  start=(k == 0), stop=(k == DC - 1))
                    last.then_inc(mod_mm, 1)
            pe.wait_ge(w_in, 64)
            pe.wait_ge(dve_setup, 2)
            pe.wait_ge(consts, N_CONST)
            pe.wait_ge(gate_fix, 10)

            def scores(T, G, q, r, gp):
                if r == 0 and q == 0:
                    pe.wait_ge(qm_done, 4 * G + 4)
                    pe.wait_ge(phi_done, 4 * G + 4)
                at_least(pe, sm_done, 4 * T + r - 1)
                for cc in range(DC):
                    for odd in range(2):
                        i = 2 * cc + odd
                        last = mm(SC[r % 2][:, i * P:(i + 1) * P],
                                  KT[32 * r:32 * r + 32, gp, cc, q * P:(q + 1) * P],
                                  QM[32 * r:32 * r + 32, gp, odd, cc, q * P:(q + 1) * P], start=True, stop=True)
                last.then_inc(sc_full, 1)

            def head_rows(T, q):
                pe.wait_ge(ot_done, T)
                at_least(pe, og_done, T - 1)
                for i in range(4):
                    last = pe.transpose(MD[:, i * P:(i + 1) * P], OTs[:, i, :], ident[:])
                last.then_inc(on_full, 1)

            def key_rows(T, q, gp):
                at_least(pe, at_done, T - 1)
                for cc in range(DC):
                    last = pe.transpose(MA[:, cc * P:(cc + 1) * P], KT[:, gp, cc, q * P:(q + 1) * P], ident[:])
                last.then_inc(knt_full, 1)

            def from_state(T, q, gp):
                at_least(pe, ot_done, T)
                at_least(pe, sbd_done, T)
                for i in range(4):
                    mm(OB[:, i * P:(i + 1) * P], Sbd[:, 4 * i:4 * i + 4, :].rearrange("p h w -> p (h w)"),
                       QT[:, gp, i // 2, q * P:(q + 1) * P], start=(i == 0), stop=False, skip_group_check=True)

            def from_tile(T, q, gp, tp, part):
                pe.wait_ge(sm_done, 4 * T + 2 + 2 * part)
                for i in (part, part + 2):
                    for a in range(4):
                        h = 4 * i + a
                        last = mm(OB[32 * a:32 * a + VW, i * P:(i + 1) * P], VA[:, gp, q, h, :], Sm[:, tp, h, :],
                                  start=False, stop=(part == 1), skip_group_check=True)
                if part == 1:
                    last.then_inc(av_done, 1)

            def add_to_state(T, q, gp, tp, j):
                pe.wait_ge(kn_done, T + 1)
                both = SB[:, 0:H * SW]
                if j == 0:
                    mm(both.rearrange("p (h w) -> p h w", h=H), ident[:], Sbd[:, :, 0:SW], start=True, stop=False,
                       skip_group_check=True)
                for cc in range(DC):
                    last = mm(SB[:, cc * HC * SW:(cc + 1) * HC * SW].rearrange("p (h w) -> p h w", h=HC),
                              Kn[:, tp, cc * P:(cc + 1) * P], VA[:, gp, q, cc * HC:(cc + 1) * HC, 0:SW],
                              start=False, stop=True, skip_group_check=True)
                last.then_inc(state_full, 1)

            def attention_columns(T, n):
                pe.wait_ge(an_done, T)
                if tile_ok(n):
                    pe.wait_ge(kn_done, T + 1)
                else:
                    pe.wait_ge(at_done, T - 1)
                a = An[:].rearrange("p h e -> p (h e)")
                for cc in range(DC):
                    last = pe.transpose(MA[:, cc * P:(cc + 1) * P], a[:, cc * P:(cc + 1) * P], ident[:])
                last.then_inc(at_full, 1)

            def out_product(T):
                pe.wait_ge(at_done, T)
                for cc in range(DC):
                    last = mm(MD[:, 0:D], ATs[:, cc, :], w_o[:, cc, :], start=(cc == 0), stop=(cc == DC - 1))
                last.then_inc(op_full, 1)

            def stage1_transposes(G, gn):
                N = G + 1
                pe.wait_ge(n1_ready, 4 * N + 4)
                at_least(pe, pj_read, 8 * N)
                if group_ok(gn - 2):
                    pe.wait_ge(h2t_done, 2 * (G - 2) + 2)
                for cc in range(DC):
                    for t in range(GT):
                        last = pe.transpose(PJ[cc][:, t * P:(t + 1) * P], N1[:, t, cc * P:(cc + 1) * P], ident[:])
                    last.then_inc(pj_full, 1)

            def stage1_qk(G, m):
                N = G + 1
                pe.wait_ge(pj_read, 8 * N + max(m + 1, 2))
                for cc in range(DC):
                    last = mm(PJ[m % 2][:], w_qkv[:, cc, m * P:(m + 1) * P], hT[:, cc, :],
                              start=(cc == 0), stop=(cc == DC - 1))
                last.then_inc(pj_full, 1)

            def stage1_v(G, u):
                N = G + 1
                pe.wait_ge(pj_read, 8 * N + 5 + u)
                for t in range(2):
                    for cc in range(DC):
                        last = mm(PJ[u][:, t * D:(t + 1) * D], hT[:, cc, (2 * u + t) * P:(2 * u + t + 1) * P],
                                  w_qkv[:, cc, 2 * D:3 * D], start=(cc == 0), stop=(cc == DC - 1))
                last.then_inc(pj_full, 1)

            def h2_transposes(G, gn, hp):
                pe.wait_ge(h2_done, 4 * (G - 1))
                if group_ok(gn):
                    pe.wait_ge(pj_read, 8 * G + 8)
                else:
                    pe.wait_ge(h2t_done, 2 * (G - 2))
                for cc in range(DC):
                    for t in range(GT):
                        last = pe.transpose(PJ[cc][:, t * P:(t + 1) * P], Hrow[:, hp, t, cc * P:(cc + 1) * P],
                                            ident[:])
                    last.then_inc(h2t_full, 1)

            def logits(G, T, n):
                g = G - 2
                pe.wait_ge(h2t_done, 2 * g + 2)
                at_least(pe, og_done, T if tile_ok(n - 1) else TILES)
                if n // 4 - 2 >= 1:
                    pe.wait_ge(route, NR * g)
                for t in range(GT):
                    for cc in range(DC):
                        last = mm(MD[:, t * E:(t + 1) * E], h2T[:, cc, t * P:(t + 1) * P], w_r[:, cc, :],
                                  start=(cc == 0), stop=(cc == DC - 1))
                last.then_inc(lg_full, 1)

            def positions(G, T, n):
                g = G - 2
                pe.wait_ge(route, NR * g + 13)
                at_least(pe, og_done, T if tile_ok(n - 1) else TILES)
                all_ = MD[:, 0:GT * E].rearrange("p (t e) -> p t e", t=GT)
                mm(all_, before[:], mask[:], start=True, stop=True, skip_group_check=True)
                for t in range(GT - 1):
                    mm(all_[:, t + 1:GT, :], ones[:], mask[:, t:t + 1, :].to_broadcast([P, GT - 1 - t, E]),
                       start=False, stop=True, skip_group_check=True)
                mm(all_, ones[:], macc[:].unsqueeze(1).to_broadcast([P, GT, E]), start=False, stop=True,
                   skip_group_check=True).then_inc(pos_full, 1)

            def slot_(it, j, n):
                T = it * 8 + j
                G = it * 2 + j // 4
                gn, q, gp = n // 4, j % 4, (j // 4) % 2
                tp = j % 2
                stage1 = group_ok(gn + 1)
                if tile_ok(n):
                    scores(T, G, q, 0, gp)
                    scores(T, G, q, 1, gp)
                if q == 0 and group_ok(gn - 2):
                    h2_transposes(G, gn, gp)
                if tile_ok(n - 1):
                    if q == 1 and group_ok(gn - 2):
                        pe.wait_ge(taken, 2 * (G - 2) + 1)
                    if q == 3 and group_ok(gn - 2):
                        pe.wait_ge(taken, 2 * (G - 2) + 2)
                    head_rows(T, q)
                if tile_ok(n):
                    key_rows(T, q, gp)
                    from_state(T, q, gp)
                if stage1:
                    if q == 0:
                        stage1_transposes(G, gn)
                    elif q == 1:
                        stage1_qk(G, 1)
                    elif q == 2:
                        stage1_qk(G, 3)
                    else:
                        stage1_v(G, 1)
                if tile_ok(n):
                    scores(T, G, q, 2, gp)
                    scores(T, G, q, 3, gp)
                if tile_ok(n - 1):
                    attention_columns(T, n)
                if tile_ok(n):
                    from_tile(T, q, gp, tp, 0)
                    add_to_state(T, q, gp, tp, j)
                if tile_ok(n - 1):
                    out_product(T)
                if stage1:
                    if q == 0:
                        stage1_qk(G, 0)
                    elif q == 1:
                        stage1_qk(G, 2)
                    elif q == 2:
                        stage1_v(G, 0)
                if tile_ok(n):
                    from_tile(T, q, gp, tp, 1)
                if q == 0 and group_ok(gn - 2):
                    logits(G, T, n)
                if q == 2 and group_ok(gn - 2):
                    positions(G, T, n)

            run_slots(pe, slot_)

            pe.wait_ge(route, NR * GROUPS)

            def slot_columns(ep, s, n):
                S, par = ep * (2 * BS) + s, s % 2
                pe.wait_ge(rows_in[s % BS], 16 * (ep * 2 + s // BS + 1))
                if n >= 2:
                    pe.wait_ge(xt_done, S - 1)
                for cc in range(DC):
                    for a in range(2):
                        last = pe.transpose(PJ[par][:, cc * BW + a * P:cc * BW + (a + 1) * P],
                                            Xr[s % BS][:, a, cc * P:(cc + 1) * P], ident[:])
                last.then_inc(xt_full, 1)

            def gate(ep, s, n):
                S, par = ep * (2 * BS) + s, s % 2
                pe.wait_ge(xt_done, S + 1)
                for hh in range(2):
                    if n >= 1:
                        pe.wait_ge(hid_done, 2 * (S - 1) + hh + 1)
                    for f in (2 * hh, 2 * hh + 1):
                        for cc in range(DC):
                            last = mm(SC[hh][:, (f % 2) * BW:(f % 2 + 1) * BW], w_g[:, cc, f * P:(f + 1) * P],
                                      XT[par][:, cc, :], start=(cc == 0), stop=(cc == DC - 1))
                    last.then_inc(gate_full, 1)

            def down(ep, s, n):
                S, par, k = ep * (2 * BS) + s, s % 2, s // BS
                pe.wait_ge(hid_done, 2 * S + 2)
                if s % BS == 0:
                    pe.wait_ge(wd_in[k], 16 * (ep + 1))
                if n >= 2:
                    pe.wait_ge(ys_done, 2 * (S - 1))
                for a in range(2):
                    for f in range(FC):
                        last = mm((MA, MD)[par][:, a * D:(a + 1) * D], hid[par][:, f, a * P:(a + 1) * P],
                                  WD[k][:, f, :], start=(f == 0), stop=(f == FC - 1))
                last.then_inc(y_full, 1)

            def step_b(ep, s, n, last):
                for ahead, part in ((2, slot_columns), (1, gate)):
                    if not (last and s + ahead >= 2 * BS):
                        part(*((ep, s + ahead) if s + ahead < 2 * BS else (ep + 1, s + ahead - 2 * BS)), n + ahead)
                down(ep, s, n)

            slot_columns(0, 0, 0)
            slot_columns(0, 1, 1)
            gate(0, 0, 0)
            for s in range(2 * BS):
                step_b(0, s, s, False)
            with pe.Fori(1, E // 2 - 1) as ep:
                for s in range(2 * BS):
                    step_b(ep, s, 10, False)
            for s in range(2 * BS):
                step_b(E // 2 - 1, s, 10, True)


def kernel(L0_attn_x, L0_attn_w_qkv, L0_attn_w_out, L0_ffn_w_router, L0_ffn_w_gate, L0_ffn_w_down, L0_c, L0_wmod):
    import numpy as np
    import concourse.bacc as bacc
    from concourse.bass_utils import run_bass_kernel_spmd

    def chunked(a):
        a = np.asarray(a)
        return np.ascontiguousarray(a.reshape(DC, P, -1).transpose(1, 0, 2))

    wdn = np.asarray(L0_ffn_w_down).transpose(0, 2, 1).reshape(E, FC, P, D).transpose(0, 2, 1, 3)
    arrays = {
        "x": np.ascontiguousarray(np.asarray(L0_attn_x).reshape(TOK, D)),
        "wqkv": chunked(np.asarray(L0_attn_w_qkv).T),
        "wo": chunked(np.asarray(L0_attn_w_out).T),
        "wr": chunked(np.asarray(L0_ffn_w_router).T),
        "wg": chunked(np.asarray(L0_ffn_w_gate).T),
        "wd": np.ascontiguousarray(wdn.reshape(E * P, FC * D)),
        "c": chunked(np.asarray(L0_c).T),
        "wmod": chunked(L0_wmod),
    }
    nc = bacc.Bacc("TRN2", target_bir_lowering=False, num_devices=1)
    ins = [nc.dram_tensor(k, a.shape, F32, kind="ExternalInput").ap() for k, a in arrays.items()]
    out = nc.dram_tensor("out", (TOK, D), F32, kind="ExternalOutput").ap()
    xe = nc.dram_tensor("slot_rows", (SLOTS, ROW), F32, kind="Internal").ap()
    ybuf = nc.dram_tensor("token_rows", (2 * TOK, D), F32, kind="Internal").ap()
    adaln_block(nc, *ins, out, xe, ybuf)
    r = run_bass_kernel_spmd(nc, [arrays], core_ids=[0])
    return np.asarray(r.results[0]["out"]).reshape(BATCH, SEQ, D)
```

```python
from contextlib import ExitStack

import concourse.bass as bass
from concourse import mybir

F32 = mybir.dt.float32
BF16 = mybir.dt.bfloat16
F32R = mybir.dt.float32r
I32 = mybir.dt.int32
ALU = mybir.AluOpType
ACT = mybir.ActivationFunctionType
AX_X = mybir.AxisListType.X

P = 128
D = 256
DC = D // P
H = 16
DH = D // H
HC = H // DC
VW = 32
SW = DH + 1
SPLIT = ((0, 0), (0, 1), (1, 0))
BATCH = 4
SEQ = 2048
TOK = BATCH * SEQ
TILES = TOK // P
GT = 4
GROUPS = TILES // GT
GW = GT * P
E = 8
F = 512
FC = F // P
CAP = 1280
SLOTS = E * CAP
ROW = D + 4 + 3 * BATCH
PARTS = 3
BW = 256
BS = CAP // BW
BIG = 1.0e5
LN_EPS = 1e-5
DEN_EPS = 1e-6
NR = 29


def adaln_block(nc, x, wqkv, wo, wr, wg, wd, c, wmod, out, xe):
    with ExitStack() as ctx:
        def sb(name, shape, dt=F32):
            return ctx.enter_context(nc.sbuf_tensor(name, shape, dt))

        def ps(name):
            return ctx.enter_context(nc.psum_tensor(name, [P, 512], F32))

        def sem(name):
            return ctx.enter_context(nc.semaphore(name))

        X = sb("X", [P, TILES, D])
        Sm = sb("Sm", [P, 2, H, P])
        QT = sb("QT", [P, 2, DC, GW])
        QS = sb("QS", [P, 2, 2, 2, DC, P], F32R)
        KS = sb("KS", [P, 2, 2, DC, P], F32R)
        KT = sb("KT", [P, 2, DC, GW])
        VA = sb("VA", [P, 2, GT, H, SW])
        hT = sb("hT", [P, 2, DC, GW], F32R)
        N1 = sb("N1", [P, GT, D])
        w_d_lo = sb("w_d_lo", [P, FC, D], F32R)
        Hrow = sb("Hrow", [P, 2, GT, ROW])
        h2T = sb("h2T", [P, DC, GW])
        EX = sb("EX", [P, 2, GW])
        Kn = sb("Kn", [P, 2, D])
        Sbd = sb("Sbd", [P, H, VW])
        OTs = sb("OTs", [P, GT, P])
        An = sb("An", [P, H, DH])
        ATs = sb("ATs", [P, 2, DC, P], F32R)
        og = sb("og", [P, D])
        w_qkv = sb("w_qkv", [P, 2, DC, 3 * D], F32R)
        w_o = sb("w_o", [P, 2, DC, D], F32R)
        w_r = sb("w_r", [P, DC, E])
        w_g = sb("w_g", [P, 2, DC, F], F32R)
        cT = sb("cT", [P, DC, BATCH])
        cS = sb("cS", [P, DC, PARTS * BATCH])
        saca = sb("saca", [P, 2 * DC, BATCH])
        MB = sb("MB", [P, BATCH, 3, D])
        gbf = sb("gbf", [PARTS * BATCH, D])
        gbr = sb("gbr", [PARTS * BATCH, D])
        gbs = sb("gbs", [PARTS * BATCH, D])
        gb16 = sb("gb16", [PARTS * BATCH, PARTS, D], BF16)
        gbp = sb("gbp", [PARTS * BATCH, D], BF16)
        partmask = sb("partmask", [P, PARTS])
        bhot = sb("bhot", [P, BATCH, PARTS * BATCH])
        ohT = [sb(f"ohT{i}", [PARTS * BATCH, BW], BF16) for i in range(2)]
        ident = sb("ident", [P, P])
        tri = sb("tri", [P, P])
        before = sb("before", [P, P], BF16)
        ones = sb("ones", [P, P], BF16)
        headmask = sb("headmask", [P, H, SW])
        pairmask = sb("pairmask", [P, GT])
        parity = sb("parity", [P, 2])
        rev = sb("rev", [P, E])
        base = sb("base", [P, E])
        eid = sb("eid", [P, E])
        tokf = sb("tokf", [P, GT])
        carry = sb("carry", [P, 4, 2])
        mhalf = sb("mhalf", [P, GT])
        idle = sb("idle", [P, 5])
        erow = sb("erow", [P, 1, ROW])
        st1 = sb("st1", [P, GT, 6])
        mv1 = sb("mv1", [P, GT, 2])
        vp1 = sb("vp1", [P, GT])
        rs1 = sb("rs1", [P, GT])
        st2 = sb("st2", [P, GT, 6])
        mv2 = sb("mv2", [P, GT, 2])
        vp2 = sb("vp2", [P, GT])
        rs2 = sb("rs2", [P, GT])
        den = sb("den", [P, H])
        rden = sb("rden", [P, H])
        lg = sb("lg", [P, GT, E])
        pos = sb("pos", [P, GT, E])
        lmax = sb("lmax", [P, GT])
        lp = sb("lp", [P, GT, E])
        lp2 = sb("lp2", [P, GT, E])
        cand = sb("cand", [P, GT, E])
        rk = sb("rk", [P, 2, GT])
        oh = sb("oh", [P, 2, GT, E])
        m2 = sb("m2", [P, GT])
        mask = sb("mask", [P, GT, E], BF16)
        msum = sb("msum", [P, E])
        macc = sb("macc", [P, E], BF16)
        drop = sb("drop", [P, GT, E])
        pbase = sb("pbase", [P, GT, E])
        pick = sb("pick", [P, 2, GT, E])
        slot = sb("slot", [P, 2, GT])
        sloti = sb("sloti", [P, 2, GT], I32)
        keep = sb("keep", [P, 2, GT])
        ee = sb("ee", [P, GT, E])
        e12 = sb("e12", [P, 2, GT])
        esum = sb("esum", [P, GT])
        gk = sb("gk", [P, 2, GT])
        Smf = Sm[:].rearrange("p a h i -> p (a h i)")
        wmod_sb = Smf[:, 0:DC * 6 * D].rearrange("p (a n) -> p a n", a=DC)
        KTf = KT[:].rearrange("p a c n -> p (a c n)")
        QTf = QT[:].rearrange("p a c n -> p (a c n)")
        EXf = EX[:].rearrange("p a n -> p (a n)")
        Hf = Hrow[:].rearrange("p a t r -> p (a t r)")
        w_qkv_raw = Hf[:, 0:DC * 3 * D].rearrange("p (c n) -> p c n", c=DC)
        w_o_raw = Hf[:, DC * 3 * D:DC * 4 * D].rearrange("p (c n) -> p c n", c=DC)
        w_g_raw = h2T[:]
        hT_raw = N1[:].rearrange("p t d -> p (t d)").rearrange("p (c n) -> p c n", c=DC)
        VAf = VA[:].rearrange("p a t h w -> p (a t h w)")
        hid_raw = [VAf[:, i * 1024:(i + 1) * 1024].rearrange("p (f n) -> p f n", f=FC) for i in range(2)]
        qs_flat = QS[:].rearrange("p a b c d n -> p (a b c d n)")
        wq_flat = w_qkv[:].rearrange("p k c n -> p (k c n)")
        hid = [[a[:, k * 1024:(k + 1) * 1024].rearrange("p (f n) -> p f n", f=FC) for k in range(2)]
               for a in (qs_flat, hT[:].rearrange("p a c n -> p (a c n)"))]
        WD_raw = [N1[:], h2T[:].rearrange("p c n -> p (c n)").rearrange("p (f n) -> p f n", f=FC)]
        WD = [[wq_flat[:, k * 1024:(k + 1) * 1024].rearrange("p (f n) -> p f n", f=FC) for k in range(2)],
              [wq_flat[:, 2048:3072].rearrange("p (f n) -> p f n", f=FC), w_d_lo[:]]]
        Xr = [Hrow[:, i // 2, (i % 2) * 2:(i % 2) * 2 + 2, :] for i in range(4)]
        Xr.append(QTf[:, 0:2 * ROW].rearrange("p (a r) -> p a r", a=2))
        XT = [a.rearrange("p (k c n) -> p k c n", k=2, c=DC)
              for a in (KS[:].rearrange("p a k c n -> p (a k c n)"), w_o[:].rearrange("p k c n -> p (k c n)"))]
        Ys = [QTf[:, 1024 + i * 512:1536 + i * 512].rearrange("p (a n) -> p a n", a=2) for i in range(2)]
        bs = [VAf[:, 2048 + i * 16:2064 + i * 16] for i in range(2)]
        GB = [EXf[:, i * 512:(i + 1) * 512] for i in range(2)]
        desti = [sb(f"desti{i}", [P, 2], I32) for i in range(2)]
        PJ = [ps("PJ0"), ps("PJ1")]
        SC = [ps("SC0"), ps("SC1")]
        OB = ps("OB")
        SB = ps("SB")
        MA = ps("MA")
        MD = ps("MD")

        x_in = [sem("x_in0"), sem("x_in1")]
        w_in = sem("w_in")
        c_in = sem("c_in")
        init_out = sem("init_out")
        fills = sem("fills")
        consts = sem("consts")
        wipe = sem("wipe")
        c_silu = sem("c_silu")
        mod_mm = sem("mod_mm")
        mod_ev = sem("mod_ev")
        mb_ev = sem("mb_ev")
        gate_fix = sem("gate_fix")
        gb_split = sem("gb_split")
        dve_setup = sem("dve_setup")
        bn1 = sem("bn1")
        ag1 = sem("ag1")
        vpe1 = sem("vpe1")
        rstd1 = sem("rstd1")
        n1_ready = sem("n1_ready")
        pj_full = sem("pj_full")
        pj_read = sem("pj_read")
        phi_done = sem("phi_done")
        w_hi = sem("w_hi")
        w_lo = sem("w_lo")
        h_raw = sem("h_raw")
        h_hi = sem("h_hi")
        h_lo = sem("h_lo")
        q_hi = sem("q_hi")
        q_lo = sem("q_lo")
        k_hi = sem("k_hi")
        k_lo = sem("k_lo")
        sc_full = sem("sc_full")
        sm_done = sem("sm_done")
        knt_full = sem("knt_full")
        kn_done = sem("kn_done")
        state_full = sem("state_full")
        sbd_done = sem("sbd_done")
        av_done = sem("av_done")
        ot_done = sem("ot_done")
        on_full = sem("on_full")
        den_done = sem("den_done")
        rden_done = sem("rden_done")
        an_done = sem("an_done")
        at_full = sem("at_full")
        at_hi = sem("at_hi")
        at_lo = sem("at_lo")
        op_full = sem("op_full")
        og_done = sem("og_done")
        x1_done = sem("x1_done")
        bn2 = sem("bn2")
        ag2 = sem("ag2")
        vpe2 = sem("vpe2")
        rstd2 = sem("rstd2")
        n2_ready = sem("n2_ready")
        h2_scaled = sem("h2_scaled")
        h2_done = sem("h2_done")
        h2t_full = sem("h2t_full")
        h2t_done = sem("h2t_done")
        lg_full = sem("lg_full")
        taken = sem("taken")
        route = sem("route")
        gexp = sem("gexp")
        pos_full = sem("pos_full")
        breath = sem("breath")
        sent = [sem("sent0"), sem("sent1")]
        rows_in = [sem(f"rows_in{i}") for i in range(BS)]
        wd_in = [sem("wd_in0"), sem("wd_in1")]
        xt_full = sem("xt_full")
        xt_hi = sem("xt_hi")
        xt_lo = sem("xt_lo")
        wd_hi = sem("wd_hi")
        wd_lo = sem("wd_lo")
        gate_full = sem("gate_full")
        silu_done = sem("silu_done")
        hid_hi = sem("hid_hi")
        hid_lo = sem("hid_lo")
        y_full = sem("y_full")
        meta = sem("meta")
        ys_done = sem("ys_done")
        y_sent = [sem("y_sent0"), sem("y_sent1")]
        oh_done = sem("oh_done")
        gb_full = sem("gb_full")
        gb_done = sem("gb_done")
        stored = sem("stored")

        N_CONST = 16 + BATCH + 1
        block = ctx.enter_context(nc.Block())

        def at_least(eng, s, n):
            if not (isinstance(n, int) and n <= 0):
                eng.wait_ge(s, n)

        def run_slots(eng, slot):
            for it in (-1, 0, 1):
                for j in range(8):
                    slot(it, j, it * 8 + j)
            with eng.Fori(2, TILES // 8 - 1) as it:
                for j in range(8):
                    slot(it, j, 24 + j)
            for it in (TILES // 8 - 1, TILES // 8):
                for j in range(8):
                    slot(it, j, it * 8 + j)
            for j in range(2):
                slot(TILES // 8 + 1, j, TILES + 8 + j)

        def tile_ok(n):
            return 0 <= n < TILES

        def group_ok(n):
            return 0 <= n < GROUPS

        def halves(it, back):
            return (it - back) // 2 if isinstance(it, int) else (it - back) // 2

        def headslot(r):
            return [2 * r, 2 * r + 1]

        @block.sync
        def _(sp):
            xg = x.rearrange("(g t p) d -> g p t d", t=GT, p=P)
            sp.dma_start(X[:, 0:GT, :], xg[0]).then_inc(x_in[0], 16)
            sp.dma_start(X[:, GT:2 * GT, :], xg[1]).then_inc(x_in[1], 16)
            with sp.Fori(1, GROUPS // 2) as i:
                for k in range(2):
                    sp.wait_ge(x_in[k], i * 16)
                    sp.dma_start(X[:, bass.ds(i * (2 * GT) + k * GT, GT), :],
                                 x[bass.ds((i * 2 + k) * GW, GW), :].rearrange("(t p) d -> p t d", p=P)
                                 ).then_inc(x_in[k], 16)
            with sp.Fori(0, GROUPS) as g:
                sp.wait_ge(x1_done, g * GT + GT)
                sp.dma_start(out[bass.ds(g * GW, GW), :].rearrange("(t p) d -> p t d", p=P),
                             X[:, bass.ds(g * GT, GT), :]).then_inc(stored, 16)
            for k in range(2):
                sp.wait_ge(sent[k], 128 * (GROUPS // 2))
            sp.wait_ge(av_done, TILES)
            sp.wait_ge(route, NR * GROUPS)

            def load_rows(ep, s, n):
                S = ep * (2 * BS) + s
                if n >= BS:
                    sp.wait_ge(ys_done, 2 * (S - BS) + 2)
                sp.dma_start(Xr[s % BS],
                             xe[bass.ds(S * BW, BW), :].rearrange("(a p) r -> p a r", p=P)
                             ).then_inc(rows_in[s % BS], 16)

            def load_wd(ep, k, n):
                if n >= 1:
                    sp.wait_ge(wd_hi, ep * 2 + k - 1)
                    sp.wait_ge(wd_lo, ep * 2 + k - 1)
                sp.dma_start(WD_raw[k].rearrange("p f n -> p (f n)"),
                             wd[bass.ds((ep * 2 + k) * P, P), :]).then_inc(wd_in[k], 16)

            def expert_pair(ep, n):
                for s in range(2 * BS):
                    if s % BS == 0:
                        load_wd(ep, s // BS, n)
                    load_rows(ep, s, 10 * n + s)

            expert_pair(0, 0)
            with sp.Fori(1, E // 2) as ep:
                expert_pair(ep, 1)

        @block.gpsimd
        def _(pool):
            pool.memset(bhot[:], 0.0).then_inc(fills, 1)
            pool.memset(partmask[:], 1.0).then_inc(fills, 1)
            pool.memset(erow[:], 0.0).then_inc(fills, 1)
            pool.memset(ident[:], 1.0).then_inc(fills, 1)
            pool.memset(tri[:], 1.0).then_inc(fills, 1)
            pool.memset(headmask[:], 1.0).then_inc(fills, 1)
            pool.memset(pairmask[:], 1.0).then_inc(fills, 1)
            pool.memset(before[:], 1.0).then_inc(fills, 1)
            pool.memset(ones[:], 1.0).then_inc(consts, 1)
            pool.memset(Sbd[:], 0.0).then_inc(consts, 1)
            pool.memset(mhalf[:], -0.5).then_inc(consts, 1)
            pool.memset(macc[:], 0.0).then_inc(consts, 1)
            pool.memset(e12[:], 1.0).then_inc(consts, 1)
            pool.iota(rev[:], [[-1, E]], base=E, channel_multiplier=0,
                      allow_small_or_imprecise_dtypes=True).then_inc(consts, 1)
            pool.iota(base[:], [[CAP, E]], base=0, channel_multiplier=0,
                      allow_small_or_imprecise_dtypes=True).then_inc(consts, 1)
            pool.iota(eid[:], [[1, E]], base=0, channel_multiplier=0,
                      allow_small_or_imprecise_dtypes=True).then_inc(consts, 1)
            pool.iota(tokf[:], [[P, GT]], base=0, channel_multiplier=1,
                      allow_small_or_imprecise_dtypes=True).then_inc(consts, 1)
            pool.iota(carry[:], [[0, 4], [-1, 2]], base=1, channel_multiplier=0,
                      allow_small_or_imprecise_dtypes=True).then_inc(consts, 1)
            pool.wait_ge(fills, 8)
            for b in range(BATCH):
                pool.memset(bhot[:, b, :].rearrange("p (k b) -> p k b", k=PARTS)[:, :, b:b + 1],
                            1.0).then_inc(consts, 1)
            pool.memset(erow[:, :, D + 2:D + 3], BIG).then_inc(consts, 1)
            pool.affine_select(out=ident[:], in_=ident[:], pattern=[[-1, P]], compare_op=ALU.is_equal, fill=0.0,
                               base=0, channel_multiplier=1).then_inc(consts, 1)
            pool.affine_select(out=tri[:], in_=tri[:], pattern=[[1, P]], compare_op=ALU.is_ge, fill=0.0,
                               base=0, channel_multiplier=-1).then_inc(consts, 1)
            pool.affine_select(out=before[:], in_=before[:], pattern=[[1, P]], compare_op=ALU.is_gt, fill=0.0,
                               base=0, channel_multiplier=-1).then_inc(consts, 1)
            hm = headmask[:].rearrange("p (c s) w -> p c s w", c=DC)
            pool.affine_select(out=hm, in_=hm, pattern=[[0, DC], [-DH, HC], [0, SW]], compare_op=ALU.is_ge,
                               fill=0.0, base=0, channel_multiplier=1).then_inc(wipe, 1)
            pool.affine_select(out=pairmask[:], in_=pairmask[:], pattern=[[-2 * DH, GT]], compare_op=ALU.is_ge,
                               fill=0.0, base=0, channel_multiplier=1).then_inc(wipe, 1)
            pool.affine_select(out=partmask[:], in_=partmask[:], pattern=[[-BATCH, PARTS]], compare_op=ALU.is_ge,
                               fill=0.0, base=0, channel_multiplier=1).then_inc(wipe, 1)
            pool.wait_ge(wipe, 3)
            pool.affine_select(out=partmask[:], in_=partmask[:], pattern=[[BATCH, PARTS]], compare_op=ALU.is_ge,
                               fill=0.0, base=BATCH - 1, channel_multiplier=-1).then_inc(consts, 1)
            pool.affine_select(out=hm, in_=hm, pattern=[[0, DC], [DH, HC], [0, SW]], compare_op=ALU.is_ge,
                               fill=0.0, base=DH - 1, channel_multiplier=-1).then_inc(consts, 1)
            pool.affine_select(out=pairmask[:], in_=pairmask[:], pattern=[[2 * DH, GT]], compare_op=ALU.is_ge,
                               fill=0.0, base=DH - 1, channel_multiplier=-1).then_inc(consts, 1)

            def breather(k):
                pool.tensor_tensor(idle[:, k:k + 1], mhalf[:, 0:1], mhalf[:, 0:1], ALU.add).then_inc(breath, 1)

            def slot_(it, j, n):
                T = it * 8 + j
                G = it * 2 + j // 4
                gn, q, gp, tp = n // 4, j % 4, (j // 4) % 2, j % 2
                if tile_ok(n + 1):
                    q1, g1 = (q + 1) % 4, (gp if q < 3 else 1 - gp)
                    pool.wait_ge(k_hi, T + 2)
                    pool.tensor_tensor(KS[:, 1 - tp, 1], KT[:, g1, :, q1 * P:(q1 + 1) * P],
                                       KS[:, 1 - tp, 0].bitcast(F32), ALU.subtract).then_inc(k_lo, 1)
                leaving = q < 2 and group_ok(gn - 3)
                if leaving and q == 0:
                    pool.wait_ge(route, NR * (G - 3) + NR)
                    if gn == 3:
                        pool.wait_ge(init_out, 16)
                def modulate():
                    hp = 1 - gp
                    b = halves(it, 0 if gp == 1 else 1)
                    pool.wait_ge(n2_ready, 4 * (G - 1) + 2 * (q - 1))
                    breather(2 * q - 4)
                    for t in (2 * q - 4, 2 * q - 3):
                        pool.tensor_tensor(Hrow[:, hp, t, 0:D], Hrow[:, hp, t, 0:D],
                                           MB[:, bass.ds(b, 1), 2, :].rearrange("p a d -> p (a d)"),
                                           ALU.mult).then_inc(h2_scaled, 1)
                    pool.wait_ge(h2_scaled, 4 * (G - 1) + 2 * (q - 1))
                    breather(2 * q - 3)
                    for t in (2 * q - 4, 2 * q - 3):
                        pool.tensor_tensor(Hrow[:, hp, t, 0:D], Hrow[:, hp, t, 0:D],
                                           MB[:, bass.ds(b, 1), 1, :].rearrange("p a d -> p (a d)"),
                                           ALU.add).then_inc(h2_done, 1)

                if q == 3 and group_ok(gn - 1):
                    modulate()
                if tile_ok(n - 1):
                    pool.wait_ge(og_done, T)
                    xt = X[:, bass.ds(T - 1, 1), :].rearrange("p a d -> p (a d)")
                    pool.tensor_tensor(xt, xt, og[:], ALU.add).then_inc(x1_done, 1)
                if q == 2 and group_ok(gn - 1):
                    modulate()
                if q == 2 and group_ok(gn + 2):
                    pool.wait_ge(vpe1, G + 3)
                    pool.tensor_tensor(rs1[:], vp1[:], mhalf[:], ALU.pow).then_inc(rstd1, 1)
                if q == 1 and group_ok(gn - 1):
                    pool.wait_ge(vpe2, G)
                    pool.tensor_tensor(rs2[:], vp2[:], mhalf[:], ALU.pow).then_inc(rstd2, 1)
                if leaving:
                    for t in (2 * q, 2 * q + 1):
                        for k in range(2):
                            pool.indirect_dma_start(
                                xe, bass.IndirectOffsetOnAxis(sloti[:, k, t:t + 1], 0), Hrow[:, 1 - gp, t, :], None,
                                bounds_check=SLOTS - 1, oob_is_err=False).then_inc(sent[1 - gp], 16)

            pool.wait_ge(consts, N_CONST)
            pool.wait_ge(gate_fix, 10)
            run_slots(pool, slot_)

            def down_lo(ep, k):
                pool.wait_ge(wd_hi, ep * 2 + k + 1)
                pool.tensor_tensor(WD[k][1], WD_raw[k], WD[k][0].bitcast(F32), ALU.subtract).then_inc(wd_lo, 1)

            def give_back(ep, s, n):
                S = ep * (2 * BS) + s
                if s % BS == 2 and not (n >= 100 and s >= BS):
                    down_lo(*((ep, 1) if s < BS else (ep + 1, 0)))
                if s % BS == 0 and n >= 1:
                    pool.wait_ge(y_sent[0], 32 * (ep * BS + (s + 1) // 2))
                    pool.wait_ge(y_sent[1], 32 * (ep * BS + s // 2))
                pool.wait_ge(breath, 4 * GROUPS + S)
                pool.wait_ge(ys_done, 2 * S + 2)
                breather(4)
                for a in range(2):
                    pool.indirect_dma_start(
                        out, bass.IndirectOffsetOnAxis(desti[s % 2][:, a:a + 1], 0), Ys[s % 2][:, a, :], None,
                        bounds_check=TOK - 1, oob_is_err=False, compute_op=ALU.add).then_inc(y_sent[s % 2], 16)

            down_lo(0, 0)
            pool.wait_ge(stored, 16 * GROUPS)
            for s in range(2 * BS):
                give_back(0, s, s)
            with pool.Fori(1, E // 2 - 1) as ep:
                for s in range(2 * BS):
                    give_back(ep, s, 10)
            for s in range(2 * BS):
                give_back(E // 2 - 1, s, 100)
            for k in range(2):
                pool.wait_ge(y_sent[k], 32 * (E * BS // 2))

        @block.scalar
        def _(act):
            act.dma_start(cT[:], c).then_inc(c_in, 16)
            act.dma_start(wmod_sb, wmod).then_inc(c_in, 16)
            for dst, src in ((w_qkv_raw, wqkv), (w_o_raw, wo), (w_r[:], wr), (w_g_raw, wg)):
                act.dma_start(dst, src).then_inc(w_in, 16)
            act.wait_ge(consts, N_CONST)
            act.dma_start(xe.rearrange("(p n) r -> p n r", p=P),
                          erow[:].to_broadcast([P, SLOTS // P, ROW])).then_inc(init_out, 16)
            act.wait_ge(c_in, 32)
            act.activation(cS[:].rearrange("p c (k b) -> p c k b", k=PARTS),
                           cT[:].unsqueeze(2).to_broadcast([P, DC, PARTS, BATCH]), ACT.Silu).then_inc(c_silu, 1)
            act.wait_ge(mod_mm, 1)
            act.activation(saca[:, 0:DC, :], MA[:, 0:DC * BATCH].rearrange("p (a b) -> p a b", a=DC),
                           ACT.Copy).then_inc(mod_ev, 1)
            act.activation(saca[:, DC:2 * DC, :],
                           MA[:, DC * BATCH:2 * DC * BATCH].rearrange("p (a b) -> p a b", a=DC),
                           ACT.Copy, bias=1.0).then_inc(mod_ev, 1)

            act.wait_ge(w_in, 64)
            for dst, src in ((w_qkv, w_qkv_raw), (w_o, w_o_raw), (w_g, w_g_raw)):
                act.activation(dst[:, 0], src, ACT.Copy).then_inc(w_hi, 1)

            def stage1_transposed(it, G, cidx, bcol):
                N = G + 1
                act.wait_ge(pj_full, 8 * N + 2)
                act.activation(hT_raw[:, cidx, :], PJ[cidx][:], ACT.Identity,
                               scale=saca[:, DC + cidx, bass.ds(bcol, 1)],
                               bias=saca[:, cidx, bass.ds(bcol, 1)]).then_inc(h_raw, 1)

            def stage1_hi(G):
                N = G + 1
                for cidx in range(DC):
                    act.wait_ge(h_raw, 2 * N + cidx + 1)
                    act.activation(hT[:, 0, cidx, :], hT_raw[:, cidx, :], ACT.Copy).then_inc(h_hi, 1)

            def stage1_qk(G, m, npar, n_next):
                N = G + 1
                act.wait_ge(pj_full, 8 * N + m + 3)
                if n_next >= 1 or m >= 2:
                    act.wait_ge(phi_done, 4 * N + m - 1)
                if n_next >= 2:
                    act.wait_ge(av_done, 4 * (N - 1))
                dst = QT if m < 2 else KT
                act.activation(EX[:, m % 2, :], PJ[m % 2][:], ACT.Exp)
                act.activation(dst[:, npar, m % 2, :], PJ[m % 2][:], ACT.Relu).then_inc(pj_read, 1)

            def next_tile_hi(T, q, gp, tp, n):
                q1, g1 = (q + 1) % 4, (gp if q < 3 else 1 - gp)
                act.wait_ge(phi_done, (T + 1 - q1) + 4)
                if n >= 1:
                    act.wait_ge(sc_full, 4 * T)
                for odd in range(2):
                    act.activation(QS[:, 1 - tp, 0, odd], QT[:, g1, :, q1 * P:(q1 + 1) * P], ACT.Copy,
                                   scale=parity[:, odd:odd + 1]).then_inc(q_hi, 1)
                act.activation(KS[:, 1 - tp, 0], KT[:, g1, :, q1 * P:(q1 + 1) * P], ACT.Copy).then_inc(k_hi, 1)

            def stage1_v(G, u, npar, n_next):
                N = G + 1
                act.wait_ge(pj_full, 8 * N + u + 7)
                if n_next >= 2:
                    act.wait_ge(av_done, 4 * (N - 1))
                act.activation(VA[:, npar, 2 * u:2 * u + 2, :, 0:DH],
                               PJ[u][:].rearrange("p (t h e) -> p t h e", t=2, h=H),
                               ACT.Copy).then_inc(pj_read, 1)

            def slot_(it, j, n):
                T = it * 8 + j
                G = it * 2 + j // 4
                gn, q, gp = n // 4, j % 4, (j // 4) % 2
                npar, nx = 1 - gp, n // 4 + 1
                tp = j % 2
                stage1 = group_ok(nx)
                if q in (1, 3) and group_ok(gn - 2):
                    act.wait_ge(lg_full if q == 1 else pos_full, G - 1)
                    act.activation((lg if q == 1 else pos)[:], MD[:, 0:GT * E].rearrange("p (t e) -> p t e", t=GT),
                                   ACT.Copy).then_inc(taken, 1)
                if tile_ok(n - 1):
                    act.wait_ge(av_done, T)
                    at_least(act, on_full, T - 1)
                    act.activation(OTs[:].rearrange("p a i -> p (a i)"), OB[:], ACT.Copy).then_inc(ot_done, 1)
                if tile_ok(n + 1):
                    next_tile_hi(T, q, gp, tp, n)
                if q == 0 and group_ok(gn - 2):
                    for cidx in range(DC):
                        act.wait_ge(h2t_full, 2 * (G - 2) + cidx + 1)
                        if gn >= 3:
                            act.wait_ge(lg_full, G - 2)
                        act.activation(h2T[:, cidx, :], PJ[cidx][:], ACT.Copy).then_inc(h2t_done, 1)
                if tile_ok(n):
                    act.wait_ge(knt_full, T + 1)
                    at_least(act, state_full, T - 1)
                    act.activation(Kn[:, tp, :], MA[:, 0:D], ACT.Copy).then_inc(kn_done, 1)
                if stage1:
                    if q == 0:
                        bcol = halves(it, 0) if gp == 0 else halves(it, -1)
                        if isinstance(bcol, int):
                            bcol = max(bcol, 0)
                        stage1_transposed(it, G, 0, bcol)
                        stage1_transposed(it, G, 1, bcol)
                        stage1_hi(G)
                    elif q == 1:
                        stage1_qk(G, 1, npar, nx)
                    elif q == 2:
                        stage1_qk(G, 3, npar, nx)
                    else:
                        stage1_v(G, 1, npar, nx)
                if tile_ok(n - 1):
                    act.wait_ge(at_full, T)
                    at_least(act, op_full, T - 1)
                    act.activation(ATs[:, 0].rearrange("p c i -> p (c i)"), MA[:, 0:D], ACT.Copy).then_inc(at_hi, 1)
                if stage1:
                    if q == 0:
                        stage1_qk(G, 0, npar, nx)
                    elif q == 1:
                        stage1_qk(G, 2, npar, nx)
                    elif q == 2:
                        stage1_v(G, 0, npar, nx)
                if q == 2 and group_ok(gn - 2):
                    g = G - 2
                    act.wait_ge(route, NR * g + 8)
                    act.activation(ee[:], lp[:], ACT.Exp).then_inc(gexp, 1)
                    act.activation(e12[:, 1, :], m2[:], ACT.Exp).then_inc(gexp, 1)

            act.wait_ge(dve_setup, 2)
            act.wait_ge(mod_ev, 2)
            run_slots(act, slot_)

            def hidden(ep, s, n):
                S = ep * (2 * BS) + s
                for hh in range(2):
                    act.wait_ge(gate_full, 2 * S + hh + 1)
                    if n >= 2:
                        act.wait_ge(hid_lo, 2 * (S - 2) + hh + 1)
                        act.wait_ge(y_full, S - 1)
                    f = slice(2 * hh, 2 * hh + 2)
                    act.activation(hid_raw[s % 2][:, f, :], SC[hh][:].rearrange("p (f n) -> p f n", f=2),
                                   ACT.Silu).then_inc(silu_done, 1)
                    act.wait_ge(silu_done, 2 * S + hh + 1)
                    act.activation(hid[s % 2][0][:, f, :], hid_raw[s % 2][:, f, :], ACT.Copy).then_inc(hid_hi, 1)

            def slots_hi(ep, s, n):
                S = ep * (2 * BS) + s
                act.wait_ge(xt_full, S + 1)
                if n >= 2:
                    act.wait_ge(gate_full, 2 * (S - 1))
                act.activation(XT[s % 2][:, 0].rearrange("p c n -> p (c n)"), PJ[s % 2][:],
                               ACT.Copy).then_inc(xt_hi, 1)

            def down_hi(ep, k, n):
                act.wait_ge(wd_in[k], 16 * (ep + 1))
                if n >= 1:
                    act.wait_ge(y_full, (ep * 2 + k - 1) * BS)
                act.activation(WD[k][0], WD_raw[k], ACT.Copy).then_inc(wd_hi, 1)

            def batches(ep, s, n):
                S = ep * (2 * BS) + s
                act.wait_ge(xt_full, S + 1)
                if n >= 2:
                    act.wait_ge(gb_full, S - 1)
                act.activation(ohT[s % 2][:], OB[0:PARTS * BATCH, 0:BW], ACT.Copy).then_inc(oh_done, 1)

            def gates(ep, s, n):
                S = ep * (2 * BS) + s
                act.wait_ge(gb_full, S + 1)
                if n >= 2:
                    act.wait_ge(ys_done, 2 * (S - 1))
                act.activation(GB[s % 2], SB[:], ACT.Copy).then_inc(gb_done, 1)

            def step_b(ep, s, n, last):
                if not (last and s >= 2 * BS - 2):
                    slots_hi(*((ep, s + 2) if s + 2 < 2 * BS else (ep + 1, s + 2 - 2 * BS)), n + 2)
                    batches(*((ep, s + 2) if s + 2 < 2 * BS else (ep + 1, s + 2 - 2 * BS)), n + 2)
                if not (last and s == 2 * BS - 1):
                    e1, s1 = (ep, s + 1) if s + 1 < 2 * BS else (ep + 1, 0)
                    gates(e1, s1, n + 1)
                    hidden(e1, s1, n + 1)
                if s % BS == 1 and not (last and s >= BS):
                    down_hi(*((ep, 1, n // 10) if s < BS else (ep + 1, 0, 1)))

            down_hi(0, 0, 0)
            for s in range(2):
                slots_hi(0, s, s)
                batches(0, s, s)
            gates(0, 0, 0)
            hidden(0, 0, 0)
            for s in range(2 * BS):
                step_b(0, s, s, False)
            with act.Fori(1, E // 2 - 1) as ep:
                for s in range(2 * BS):
                    step_b(ep, s, 10, False)
            for s in range(2 * BS):
                step_b(E // 2 - 1, s, 10, True)

        @block.vector
        def _(dve):
            dve.memset(VA[:], 1.0).then_inc(dve_setup, 1)
            dve.wait_ge(consts, N_CONST)
            dve.tensor_reduce(parity[:, 0:1], pairmask[:], AX_X, ALU.add).then_inc(gate_fix, 1)
            dve.wait_ge(gate_fix, 1)
            dve.tensor_scalar(parity[:, 1:2], parity[:, 0:1], -1.0, 1.0, ALU.mult, ALU.add).then_inc(dve_setup, 1)
            for b in range(BATCH):
                for hh, kinds in ((0, 2), (1, 1)):
                    dve.wait_ge(mod_mm, 2 + 2 * b + hh)
                    dve.tensor_copy(MB[:, b, 2 * hh:2 * hh + kinds, :],
                                    SC[hh][:, 0:kinds * D].rearrange("p (k d) -> p k d", k=kinds)).then_inc(mb_ev, 1)
            dve.wait_ge(mod_mm, 2 + 2 * BATCH)
            dve.tensor_copy(gbf[:], MD[0:PARTS * BATCH, 0:D]).then_inc(mb_ev, 1)
            dve.wait_ge(mb_ev, 2 * BATCH + 1)
            dve.tensor_scalar(MB[:, :, 2, :], MB[:, :, 2, :], 1.0, None, ALU.add).then_inc(gate_fix, 1)
            tmp = KTf[:, 0:BATCH * D].rearrange("p (b d) -> p b d", b=BATCH)
            sgn = QTf[:, 0:BATCH * D].rearrange("p (b d) -> p b d", b=BATCH)
            n = 2
            for gate, tmp, sgn in ((MB[:, :, 0, :], tmp, sgn), (gbf[:], gbr[:], gbs[:])):
                dve.scalar_tensor_tensor(tmp, gate, -1.0, gate, ALU.mult, ALU.max).then_inc(gate_fix, 1)
                dve.tensor_scalar(sgn, gate, 0.0, 2.0, ALU.is_ge, ALU.mult).then_inc(gate_fix, 1)
                n += 2
                dve.wait_ge(gate_fix, n)
                dve.tensor_scalar(tmp, tmp, 0.25, None, ALU.max).then_inc(gate_fix, 1)
                n += 1
                dve.wait_ge(gate_fix, n)
                dve.scalar_tensor_tensor(gate, sgn, -1.0, tmp, ALU.add, ALU.mult).then_inc(gate_fix, 1)
                n += 1
                dve.wait_ge(gate_fix, n)

            def split_gb():
                m = 0

                def part(ins):
                    nonlocal m
                    m += 1
                    ins.then_inc(gb_split, 1)
                    dve.wait_ge(gb_split, m)
                for k, src in enumerate((gbf, gbr, gbs)):
                    part(dve.tensor_copy(gb16[:, k, :], src[:]))
                    if k < PARTS - 1:
                        part(dve.tensor_tensor((gbr, gbs)[k][:], src[:], gb16[:, k, :], ALU.subtract))
                part(dve.tensor_scalar(gbp[:], gb16[:, 0, :], partmask[0:PARTS * BATCH, 0:1], None, ALU.mult))
                for k in (1, 2):
                    part(dve.scalar_tensor_tensor(gbp[:], gb16[:, k, :], partmask[0:PARTS * BATCH, k:k + 1], gbp[:],
                                                  ALU.mult, ALU.add))

            split_gb()
            for k, (dst, src) in enumerate(((w_qkv, w_qkv_raw), (w_o, w_o_raw), (w_g, w_g_raw))):
                dve.wait_ge(w_hi, k + 1)
                dve.tensor_tensor(dst[:, 1], src, dst[:, 0].bitcast(F32), ALU.subtract).then_inc(w_lo, 1)

            def masked_scores(T, r, tp, n):
                dve.wait_ge(sc_full, 4 * T + r + 1)
                if r == 0 and n >= 2:
                    dve.wait_ge(av_done, T - 1)
                o = Sm[:, tp].rearrange("p (c s) i -> p c s i", c=DC)[:, :, 2 * r:2 * r + 2, :]
                dve.tensor_tensor(o, SC[r % 2][:].rearrange("p (c s i) -> p c s i", c=2, s=2),
                                  tri[:].unsqueeze(1).unsqueeze(1).to_broadcast([P, 2, 2, P]),
                                  ALU.mult).then_inc(sm_done, 1)

            def normalise_heads(T):
                on = MD[:].rearrange("p (h w) -> p h w", h=H)
                dve.wait_ge(on_full, T)
                dve.tensor_scalar(den[:].unsqueeze(2), on[:, :, DH:DH + 1], DEN_EPS, None, ALU.max).then_inc(den_done, 1)
                dve.wait_ge(den_done, T)
                dve.reciprocal(rden[:], den[:]).then_inc(rden_done, 1)
                dve.wait_ge(rden_done, T)
                at_least(dve, at_full, T - 1)
                dve.tensor_tensor(An[:], on[:, :, 0:DH], rden[:].unsqueeze(2).to_broadcast([P, H, DH]),
                                  ALU.mult).then_inc(an_done, 1)

            def attention_lo(T):
                dve.wait_ge(at_hi, T)
                dve.tensor_tensor(ATs[:, 1].rearrange("p c i -> p (c i)"), MA[:, 0:D],
                                  ATs[:, 0].rearrange("p c i -> p (c i)").bitcast(F32),
                                  ALU.subtract).then_inc(at_lo, 1)

            def next_tile_lo(T, q, gp, tp):
                q1, g1 = (q + 1) % 4, (gp if q < 3 else 1 - gp)
                for odd in range(2):
                    dve.wait_ge(q_hi, 2 * (T + 1) + odd + 1)
                    dve.scalar_tensor_tensor(QS[:, 1 - tp, 1, odd], QT[:, g1, :, q1 * P:(q1 + 1) * P],
                                             parity[:, odd:odd + 1], QS[:, 1 - tp, 0, odd].bitcast(F32),
                                             ALU.mult, ALU.subtract).then_inc(q_lo, 1)

            def stage1_lo(G):
                for cidx in range(DC):
                    dve.wait_ge(h_hi, 2 * (G + 1) + cidx + 1)
                    dve.tensor_tensor(hT[:, 1, cidx, :], hT_raw[:, cidx, :], hT[:, 0, cidx, :].bitcast(F32),
                                      ALU.subtract).then_inc(h_lo, 1)

            def state(it, T, j):
                keep_it = carry[:].rearrange("p a b -> p (a b)")[:, bass.ds(it, 1)] if j == 7 else 1.0
                dve.wait_ge(state_full, T + 1)
                dve.scalar_tensor_tensor(Sbd[:, :, 0:SW], SB[:, 0:H * SW].rearrange("p (h w) -> p h w", h=H),
                                         keep_it, headmask[:], ALU.mult, ALU.mult).then_inc(sbd_done, 1)

            def phi(G, m, npar):
                N = G + 1
                dst = (QT if m < 2 else KT)[:, npar, m % 2, :]
                dve.wait_ge(pj_read, 6 * N + m + 1)
                dve.scalar_tensor_tensor(dst, dst, 1.0, EX[:, m % 2, :], ALU.add, ALU.min).then_inc(phi_done, 1)

            def ln_tail(st, mv, vp, s_ag, s_vp, count):
                for t in range(GT):
                    dve.bn_aggr(mv[:, t, :], st[:, t, :]).then_inc(s_ag, 1)
                dve.wait_ge(s_ag, 4 * count)
                dve.tensor_scalar(vp[:].unsqueeze(2), mv[:, :, 1:2], LN_EPS, None, ALU.add).then_inc(s_vp, 1)

            def ln1_stats(it, G, gp):
                L = G + 2
                xi = it + 2 if not isinstance(it, int) else it + 2
                dve.wait_ge(x_in[gp], 16 * xi)
                for t in range(GT):
                    dve.bn_stats(st1[:, t, :], X[:, bass.ds(L * GT + t, 1), :].rearrange("p a d -> p (a d)")
                                 ).then_inc(bn1, 1)
                dve.wait_ge(bn1, 4 * (L + 1))

            def ln1_norm(G, gl):
                L = G + 2
                dve.wait_ge(rstd1, L + 1)
                if gl >= 1:
                    dve.wait_ge(h_lo, 2 * L)
                for t in range(GT):
                    dve.tensor_scalar(N1[:, t, :], X[:, bass.ds(L * GT + t, 1), :].rearrange("p a d -> p (a d)"),
                                      mv1[:, t, 0:1], rs1[:, t:t + 1], ALU.subtract, ALU.mult).then_inc(n1_ready, 1)

            def ln2_norm(it, G, gn, gp):
                g = G - 1
                dve.wait_ge(rstd2, G)
                if gn >= 3:
                    dve.wait_ge(sent[1 - gp], 128 * ((it - 1) if gp == 0 else it))
                for t in range(GT):
                    dve.tensor_scalar(Hrow[:, 1 - gp, t, 0:D], X[:, bass.ds(g * GT + t, 1), :].rearrange("p a d -> p (a d)"),
                                      mv2[:, t, 0:1], rs2[:, t:t + 1], ALU.subtract, ALU.mult).then_inc(n2_ready, 1)

            revb = rev[:].unsqueeze(1).to_broadcast([P, GT, E])
            steps = [0]

            def step(ins):
                steps[0] += 1
                ins.then_inc(route, 1)

            def after(g):
                dve.wait_ge(route, NR * g + steps[0])

            def wide(a):
                return a.unsqueeze(2).to_broadcast([P, GT, E])

            def choose(g):
                steps[0] = 0
                dve.wait_ge(taken, 2 * g + 1)
                step(dve.tensor_reduce(lmax[:], lg[:], AX_X, ALU.max))
                after(g)
                step(dve.tensor_tensor(lp[:], lg[:], wide(lmax[:]), ALU.subtract))
                after(g)
                step(dve.tensor_scalar(lp[:], lp[:], -104.0, None, ALU.max))
                after(g)
                step(dve.scalar_tensor_tensor(cand[:], lp[:], 0.0, revb, ALU.is_equal, ALU.mult))
                after(g)
                step(dve.tensor_reduce(rk[:, 0, :], cand[:], AX_X, ALU.max))
                after(g)
                step(dve.tensor_tensor(oh[:, 0], revb, wide(rk[:, 0, :]), ALU.is_equal))
                after(g)
                step(dve.scalar_tensor_tensor(lp2[:], oh[:, 0], -1.0e30, lp[:], ALU.mult, ALU.add))
                after(g)
                step(dve.tensor_reduce(m2[:], lp2[:], AX_X, ALU.max))
                after(g)
                step(dve.tensor_tensor(cand[:], lp2[:], wide(m2[:]), ALU.is_equal))
                after(g)
                step(dve.tensor_tensor(cand[:], cand[:], revb, ALU.mult))
                after(g)
                step(dve.tensor_reduce(rk[:, 1, :], cand[:], AX_X, ALU.max))
                after(g)
                step(dve.tensor_tensor(oh[:, 1], revb, wide(rk[:, 1, :]), ALU.is_equal))
                after(g)
                step(dve.tensor_tensor(mask[:], oh[:, 0], oh[:, 1], ALU.add))

            def place(it, g, pg, gn):
                dve.wait_ge(taken, 2 * g + 2)
                step(dve.tensor_scalar(drop[:], pos[:], float(CAP), BIG, ALU.is_ge, ALU.mult))
                step(dve.tensor_tensor(pbase[:], pos[:], base[:].unsqueeze(1).to_broadcast([P, GT, E]), ALU.add))
                step(dve.tensor_reduce(msum[:], mask[:].rearrange("p t e -> p e t"), AX_X, ALU.add))
                step(dve.tensor_reduce(esum[:], ee[:], AX_X, ALU.add))
                after(g)
                step(dve.tensor_tensor(pbase[:], pbase[:], drop[:], ALU.add))
                step(dve.reciprocal(esum[:], esum[:]))
                step(dve.tensor_tensor(macc[:], macc[:], msum[:], ALU.add))
                after(g)
                step(dve.tensor_tensor(pick[:], oh[:], pbase[:].unsqueeze(1).to_broadcast([P, 2, GT, E]), ALU.mult))
                step(dve.tensor_tensor(gk[:], e12[:], esum[:].unsqueeze(1).to_broadcast([P, 2, GT]), ALU.mult))
                after(g)
                step(dve.tensor_reduce(slot[:], pick[:], AX_X, ALU.add))
                after(g)
                if gn >= 3:
                    dve.wait_ge(sent[1 - pg], 128 * ((it - 1) if pg == 0 else it))
                step(dve.tensor_copy(sloti[:], slot[:]))
                step(dve.scalar_tensor_tensor(gk[:], slot[:], BIG / 2, gk[:], ALU.is_lt, ALU.mult))
                after(g)
                step(dve.tensor_reduce(esum[:], gk[:].rearrange("p k t -> p t k"), AX_X, ALU.add))
                after(g)
                step(dve.tensor_scalar(esum[:], esum[:], 1e-6, None, ALU.add))
                after(g)
                step(dve.reciprocal(esum[:], esum[:]))
                after(g)
                row = Hrow[:, pg].rearrange("p t r -> p r t")
                step(dve.tensor_tensor(row[:, D:D + 2, :], gk[:],
                                       esum[:].unsqueeze(1).to_broadcast([P, 2, GT]), ALU.mult))

            def place_ids(it, pg):
                row = Hrow[:, pg].rearrange("p t r -> p r t")
                dve.tensor_scalar(row[:, D + 3:D + 4, :], rk[:, 0:1, :], -1.0, float(E), ALU.mult, ALU.add)
                dve.tensor_copy(row[:, D + 2:D + 3, :], tokf[:].unsqueeze(1))
                dve.tensor_copy(row[:, D + 4:ROW, :],
                                bhot[:, bass.ds(halves(it, 1), 1), :].rearrange("p a k -> p k a")
                                .to_broadcast([P, PARTS * BATCH, GT]))

            def slot_(it, j, n):
                T = it * 8 + j
                G = it * 2 + j // 4
                gn, q, gp = n // 4, j % 4, (j // 4) % 2
                npar = 1 - gp
                tp = j % 2
                stage1 = group_ok(gn + 1)
                if tile_ok(n):
                    masked_scores(T, 0, tp, n)
                    masked_scores(T, 1, tp, n)
                if tile_ok(n - 1):
                    normalise_heads(T)
                if tile_ok(n + 1):
                    next_tile_lo(T, q, gp, tp)
                if q == 0 and stage1:
                    stage1_lo(G)
                if tile_ok(n):
                    masked_scores(T, 2, tp, n)
                    masked_scores(T, 3, tp, n)
                if tile_ok(n - 1):
                    attention_lo(T)
                if tile_ok(n):
                    state(it, T, j)
                if tile_ok(n - 1):
                    b = halves(it, 0 if j >= 1 else 1)
                    dve.wait_ge(op_full, T)
                    at_least(dve, x1_done, T - 1)
                    dve.tensor_tensor(og[:], MD[:, 0:D], MB[:, bass.ds(b, 1), 0, :].rearrange("p a d -> p (a d)"),
                                      ALU.mult).then_inc(og_done, 1)
                if tile_ok(n - 2):
                    dve.wait_ge(x1_done, T - 1)
                    dve.bn_stats(st2[:, (j - 2) % 4, :], X[:, bass.ds(T - 2, 1), :].rearrange("p a d -> p (a d)")
                                 ).then_inc(bn2, 1)
                if q == 0 and stage1:
                    phi(G, 0, npar)
                if q == 1:
                    if group_ok(gn - 1):
                        dve.wait_ge(bn2, 4 * G)
                    if stage1:
                        phi(G, 1, npar)
                    if group_ok(gn - 1):
                        ln_tail(st2, mv2, vp2, ag2, vpe2, G)
                    if group_ok(gn - 2):
                        choose(G - 2)
                if q == 2:
                    if stage1:
                        phi(G, 2, npar)
                        phi(G, 3, npar)
                    if group_ok(gn + 2):
                        ln1_stats(it, G, gp)
                    if group_ok(gn - 1):
                        ln2_norm(it, G, gn, gp)
                    if group_ok(gn + 2):
                        ln_tail(st1, mv1, vp1, ag1, vpe1, G + 3)
                if q == 3:
                    if group_ok(gn + 2):
                        ln1_norm(G, gn + 2)
                    if group_ok(gn - 2):
                        steps[0] = 13
                        dve.wait_ge(gexp, 2 * (G - 2) + 2)
                        place_ids(it, gp)
                        place(it, G - 2, gp, gn)
                        assert steps[0] == NR, steps[0]
                if q == 0 and group_ok(gn - 3):
                    dve.tensor_scalar(tokf[:], tokf[:], float(GW), None, ALU.add).then_inc(dve_setup, 1)

            run_slots(dve, slot_)

            def slots_lo(S, par):
                dve.wait_ge(xt_hi, S + 1)
                dve.tensor_tensor(XT[par][:, 1].rearrange("p c n -> p (c n)"), PJ[par][:],
                                  XT[par][:, 0].rearrange("p c n -> p (c n)").bitcast(F32),
                                  ALU.subtract).then_inc(xt_lo, 1)

            def hidden_lo(S, par):
                for hh in range(2):
                    f = slice(2 * hh, 2 * hh + 2)
                    dve.wait_ge(hid_hi, 2 * S + hh + 1)
                    dve.tensor_tensor(hid[par][1][:, f, :], hid_raw[par][:, f, :],
                                      hid[par][0][:, f, :].bitcast(F32), ALU.subtract).then_inc(hid_lo, 1)

            def slot_meta(ep, s, n):
                S, par = ep * (2 * BS) + s, s % 2
                t = bs[par]
                first, other, wa, wb, w = (t[:, 2 * i:2 * i + 2].unsqueeze(2) for i in range(5))
                row = Xr[s % BS]
                eno = eid[:, bass.ds(ep * 2 + s // BS, 1)]
                dve.wait_ge(rows_in[s % BS], 16 * (ep * 2 + s // BS + 1))
                dve.tensor_scalar(first, row[:, :, D + 3:D + 4], eno, None, ALU.is_equal).then_inc(meta, 1)
                if n >= 2:
                    dve.wait_ge(y_sent[par], 32 * (ep * BS + s // 2))
                dve.tensor_copy(desti[par][:].unsqueeze(2), row[:, :, D + 2:D + 3]).then_inc(meta, 1)
                dve.wait_ge(meta, 5 * S + 1)
                dve.tensor_scalar(other, first, -1.0, 1.0, ALU.mult, ALU.add).then_inc(meta, 1)
                dve.tensor_tensor(wa, row[:, :, D:D + 1], first, ALU.mult)
                dve.wait_ge(meta, 5 * S + 3)
                dve.tensor_tensor(wb, row[:, :, D + 1:D + 2], other, ALU.mult).then_inc(meta, 1)
                dve.wait_ge(meta, 5 * S + 4)
                dve.tensor_tensor(w, wa, wb, ALU.add).then_inc(meta, 1)

            def weighted_rows(ep, s):
                S, par = ep * (2 * BS) + s, s % 2
                dve.wait_ge(gb_done, S + 1)
                dve.wait_ge(y_full, S + 1)
                dve.wait_ge(meta, 5 * S + 5)
                for a in range(2):
                    dve.scalar_tensor_tensor(Ys[par][:, a, :], (MA, MD)[par][:, a * D:(a + 1) * D],
                                             bs[par][:, 8 + a:9 + a], GB[par][:, a * D:(a + 1) * D],
                                             ALU.mult, ALU.mult).then_inc(ys_done, 1)

            def step_b(ep, s, n, last):
                if not (last and s + 2 >= 2 * BS):
                    slots_lo(ep * (2 * BS) + s + 2, s % 2)
                slot_meta(ep, s, n)
                if not (last and s + 1 >= 2 * BS):
                    hidden_lo(ep * (2 * BS) + s + 1, (s + 1) % 2)
                weighted_rows(ep, s)

            slots_lo(0, 0)
            slots_lo(1, 1)
            hidden_lo(0, 0)
            for s in range(2 * BS):
                step_b(0, s, s, False)
            with dve.Fori(1, E // 2 - 1) as ep:
                for s in range(2 * BS):
                    step_b(ep, s, 10, False)
            for s in range(2 * BS):
                step_b(E // 2 - 1, s, 10, True)

        @block.tensor
        def _(pe):
            mm = pe.matmul
            pe.wait_ge(c_silu, 1)
            for m in range(2 * DC):
                for k in range(DC):
                    last = mm(MA[:, m * BATCH:(m + 1) * BATCH], wmod_sb[:, k, m * P:(m + 1) * P], cS[:, k, 0:BATCH],
                              start=(k == 0), stop=(k == DC - 1))
            last.then_inc(mod_mm, 1)
            for b in range(BATCH):
                for hh, kinds in ((0, 2), (1, 1)):
                    if b >= 1:
                        pe.wait_ge(mb_ev, 2 * (b - 1) + hh + 1)
                    for k in range(DC):
                        last = mm(SC[hh][:, 0:kinds * D], cS[:, k, b:b + 1].to_broadcast([P, P]),
                                  wmod_sb[:, k, (2 + 2 * hh) * D:(2 + 2 * hh + kinds) * D],
                                  start=(k == 0), stop=(k == DC - 1))
                    last.then_inc(mod_mm, 1)
            for k in range(DC):
                last = mm(MD[0:PARTS * BATCH, 0:D], cS[:, k, :],
                          wmod_sb[:, k, 5 * D:6 * D], start=(k == 0), stop=(k == DC - 1))
            last.then_inc(mod_mm, 1)
            pe.wait_ge(w_in, 64)
            pe.wait_ge(w_lo, 3)
            pe.wait_ge(dve_setup, 2)
            pe.wait_ge(consts, N_CONST)
            pe.wait_ge(gate_fix, 10)
            pe.wait_ge(gb_split, 8)
            pe.wait_ge(mb_ev, 2 * BATCH + 1)

            def scores(T, tp, r):
                if r == 0:
                    pe.wait_ge(q_lo, 2 * T + 2)
                    pe.wait_ge(k_lo, T + 1)
                at_least(pe, sm_done, 4 * T + r - 1)
                rows = slice(32 * r, 32 * r + 32)
                for cc in range(DC):
                    for i, (kp, qp) in enumerate(SPLIT):
                        last = mm(SC[r % 2][:, cc * 2 * P:(cc + 1) * 2 * P], KS[rows, tp, kp, cc, :],
                                  QS[rows, tp, qp, :, cc, :], start=(i == 0), stop=(i == len(SPLIT) - 1))
                last.then_inc(sc_full, 1)

            def head_rows(T, q):
                pe.wait_ge(ot_done, T)
                at_least(pe, og_done, T - 1)
                for i in range(4):
                    last = pe.transpose(MD[:, i * P:(i + 1) * P], OTs[:, i, :], ident[:])
                last.then_inc(on_full, 1)

            def key_rows(T, q, gp):
                at_least(pe, at_lo, T - 1)
                for cc in range(DC):
                    last = pe.transpose(MA[:, cc * P:(cc + 1) * P], KT[:, gp, cc, q * P:(q + 1) * P], ident[:])
                last.then_inc(knt_full, 1)

            def from_state(T, q, gp):
                at_least(pe, ot_done, T)
                at_least(pe, sbd_done, T)
                for i in range(4):
                    mm(OB[:, i * P:(i + 1) * P], Sbd[:, 4 * i:4 * i + 4, :].rearrange("p h w -> p (h w)"),
                       QT[:, gp, i // 2, q * P:(q + 1) * P], start=(i == 0), stop=False, skip_group_check=True)

            def from_tile(T, q, gp, tp, part):
                pe.wait_ge(sm_done, 4 * T + 2 + 2 * part)
                for i in (part, part + 2):
                    for a in range(4):
                        h = 4 * i + a
                        last = mm(OB[32 * a:32 * a + SW, i * P:(i + 1) * P], VA[:, gp, q, h, :], Sm[:, tp, h, :],
                                  start=False, stop=(part == 1), skip_group_check=True)
                if part == 1:
                    last.then_inc(av_done, 1)

            def add_to_state(T, q, gp, tp, j):
                pe.wait_ge(kn_done, T + 1)
                both = SB[:, 0:H * SW]
                if j == 0:
                    mm(both.rearrange("p (h w) -> p h w", h=H), ident[:], Sbd[:, :, 0:SW], start=True, stop=False,
                       skip_group_check=True)
                for cc in range(DC):
                    last = mm(SB[:, cc * HC * SW:(cc + 1) * HC * SW].rearrange("p (h w) -> p h w", h=HC),
                              Kn[:, tp, cc * P:(cc + 1) * P], VA[:, gp, q, cc * HC:(cc + 1) * HC, 0:SW],
                              start=False, stop=True, skip_group_check=True)
                last.then_inc(state_full, 1)

            def attention_columns(T, n):
                pe.wait_ge(an_done, T)
                if tile_ok(n):
                    pe.wait_ge(kn_done, T + 1)
                else:
                    pe.wait_ge(at_lo, T - 1)
                a = An[:].rearrange("p h e -> p (h e)")
                for cc in range(DC):
                    last = pe.transpose(MA[:, cc * P:(cc + 1) * P], a[:, cc * P:(cc + 1) * P], ident[:])
                last.then_inc(at_full, 1)

            def out_product(T):
                pe.wait_ge(at_lo, T)
                for cc in range(DC):
                    for i, (ap, wp) in enumerate(SPLIT):
                        last = mm(MD[:, 0:D], ATs[:, ap, cc, :], w_o[:, wp, cc, :], start=(cc + i == 0),
                                  stop=(cc == DC - 1 and i == len(SPLIT) - 1))
                last.then_inc(op_full, 1)

            def stage1_transposes(G, gn):
                N = G + 1
                pe.wait_ge(n1_ready, 4 * N + 4)
                at_least(pe, pj_read, 6 * N)
                if group_ok(gn - 2):
                    pe.wait_ge(h2t_done, 2 * (G - 2) + 2)
                for cc in range(DC):
                    for t in range(GT):
                        last = pe.transpose(PJ[cc][:, t * P:(t + 1) * P], N1[:, t, cc * P:(cc + 1) * P], ident[:])
                    last.then_inc(pj_full, 1)

            def stage1_qk(G, m, beside=None):
                N = G + 1
                if m == 0:
                    pe.wait_ge(h_raw, 2 * N + 2)
                    pe.wait_ge(h_lo, 2 * N + 2)
                elif m >= 2:
                    pe.wait_ge(pj_read, 6 * N + m - 1)
                for cc in range(DC):
                    for i, (hp, wp) in enumerate(SPLIT):
                        last = mm(PJ[m % 2][:], w_qkv[:, wp, cc, m * P:(m + 1) * P], hT[:, hp, cc, :],
                                  start=(cc + i == 0), stop=(cc == DC - 1 and i == len(SPLIT) - 1))
                        if beside and cc == 1:
                            beside(i)
                last.then_inc(pj_full, 1)

            def stage1_v(G, u):
                N = G + 1
                pe.wait_ge(pj_read, 6 * N + 3 + u)
                for t in range(2):
                    for cc in range(DC):
                        for i, (hp, wp) in enumerate(SPLIT):
                            last = mm(PJ[u][:, t * D:(t + 1) * D],
                                      hT[:, hp, cc, (2 * u + t) * P:(2 * u + t + 1) * P],
                                      w_qkv[:, wp, cc, 2 * D:3 * D], start=(cc + i == 0),
                                      stop=(cc == DC - 1 and i == len(SPLIT) - 1))
                last.then_inc(pj_full, 1)

            def h2_transposes(G, gn, hp):
                pe.wait_ge(h2_done, 4 * (G - 1))
                if group_ok(gn):
                    pe.wait_ge(pj_read, 6 * G + 6)
                else:
                    pe.wait_ge(h2t_done, 2 * (G - 2))
                for cc in range(DC):
                    for t in range(GT):
                        last = pe.transpose(PJ[cc][:, t * P:(t + 1) * P], Hrow[:, hp, t, cc * P:(cc + 1) * P],
                                            ident[:])
                    last.then_inc(h2t_full, 1)

            def logits_free(G, T, n):
                g = G - 2
                pe.wait_ge(h2t_done, 2 * g + 2)
                at_least(pe, og_done, T if tile_ok(n - 1) else TILES)
                if n // 4 - 2 >= 1:
                    pe.wait_ge(route, NR * g)

            def logits_of(t):
                for cc in range(DC):
                    last = mm(MD[:, t * E:(t + 1) * E], h2T[:, cc, t * P:(t + 1) * P], w_r[:, cc, :],
                              start=(cc == 0), stop=(cc == DC - 1))
                if t == GT - 1:
                    last.then_inc(lg_full, 1)

            def positions(G, T, n):
                g = G - 2
                pe.wait_ge(route, NR * g + 13)
                at_least(pe, og_done, T if tile_ok(n - 1) else TILES)
                all_ = MD[:, 0:GT * E].rearrange("p (t e) -> p t e", t=GT)
                mm(all_, before[:], mask[:], start=True, stop=True, skip_group_check=True)
                for t in range(GT - 1):
                    mm(all_[:, t + 1:GT, :], ones[:], mask[:, t:t + 1, :].to_broadcast([P, GT - 1 - t, E]),
                       start=False, stop=True, skip_group_check=True)
                mm(all_, ones[:], macc[:].unsqueeze(1).to_broadcast([P, GT, E]), start=False, stop=True,
                   skip_group_check=True).then_inc(pos_full, 1)

            def slot_(it, j, n):
                T = it * 8 + j
                G = it * 2 + j // 4
                gn, q, gp = n // 4, j % 4, (j // 4) % 2
                tp = j % 2
                stage1 = group_ok(gn + 1)
                if tile_ok(n):
                    scores(T, tp, 0)
                    scores(T, tp, 1)
                if q == 0 and group_ok(gn - 2):
                    h2_transposes(G, gn, gp)
                if tile_ok(n - 1):
                    if q == 1 and group_ok(gn - 2):
                        pe.wait_ge(taken, 2 * (G - 2) + 1)
                    if q == 3 and group_ok(gn - 2):
                        pe.wait_ge(taken, 2 * (G - 2) + 2)
                    head_rows(T, q)
                if tile_ok(n):
                    key_rows(T, q, gp)
                    from_state(T, q, gp)
                if stage1:
                    if q == 0:
                        stage1_transposes(G, gn)
                    elif q == 1:
                        stage1_qk(G, 1)
                    elif q == 2:
                        stage1_qk(G, 3)
                    else:
                        stage1_v(G, 1)
                if tile_ok(n):
                    scores(T, tp, 2)
                    scores(T, tp, 3)
                if tile_ok(n - 1):
                    attention_columns(T, n)
                if tile_ok(n):
                    from_tile(T, q, gp, tp, 0)
                    add_to_state(T, q, gp, tp, j)
                if tile_ok(n - 1):
                    out_product(T)
                if stage1:
                    if q == 0:
                        def beside(i):
                            if i == 0:
                                logits_free(G, T, n)
                            logits_of(i)
                        stage1_qk(G, 0, beside if group_ok(gn - 2) else None)
                    elif q == 1:
                        stage1_qk(G, 2)
                    elif q == 2:
                        stage1_v(G, 0)
                if tile_ok(n):
                    from_tile(T, q, gp, tp, 1)
                if q == 0 and group_ok(gn - 2):
                    if not stage1:
                        logits_free(G, T, n)
                    for t in range(len(SPLIT) if stage1 else 0, GT):
                        logits_of(t)
                if q == 2 and group_ok(gn - 2):
                    positions(G, T, n)

            run_slots(pe, slot_)

            pe.wait_ge(route, NR * GROUPS)

            def slot_columns(ep, s, n):
                S, par = ep * (2 * BS) + s, s % 2
                pe.wait_ge(rows_in[s % BS], 16 * (ep * 2 + s // BS + 1))
                if n >= 2:
                    pe.wait_ge(xt_lo, S - 1)
                for cc in range(DC):
                    for a in range(2):
                        last = pe.transpose(PJ[par][:, cc * BW + a * P:cc * BW + (a + 1) * P],
                                            Xr[s % BS][:, a, cc * P:(cc + 1) * P], ident[:])
                if n >= 1:
                    pe.wait_ge(oh_done, S)
                for a in range(2):
                    last = pe.transpose(OB[0:PARTS * BATCH, a * P:(a + 1) * P],
                                        Xr[s % BS][:, a, D + 4:ROW], ident[:])
                last.then_inc(xt_full, 1)

            def gate(ep, s, n):
                S, par = ep * (2 * BS) + s, s % 2
                if n >= 1:
                    pe.wait_ge(gb_done, S)
                pe.wait_ge(oh_done, S + 1)
                for a in range(2):
                    last = mm(SB[:, a * D:(a + 1) * D], ohT[par][:, a * P:(a + 1) * P], gbp[:], start=True, stop=True)
                last.then_inc(gb_full, 1)
                pe.wait_ge(xt_lo, S + 1)
                for hh in range(2):
                    if n >= 1:
                        pe.wait_ge(silu_done, 2 * (S - 1) + hh + 1)
                    for f in (2 * hh, 2 * hh + 1):
                        for cc in range(DC):
                            for i, (wp, xp) in enumerate(SPLIT):
                                last = mm(SC[hh][:, (f % 2) * BW:(f % 2 + 1) * BW],
                                          w_g[:, wp, cc, f * P:(f + 1) * P], XT[par][:, xp, cc, :],
                                          start=(cc + i == 0), stop=(cc == DC - 1 and i == len(SPLIT) - 1))
                    last.then_inc(gate_full, 1)

            def down(ep, s, n):
                S, par, k = ep * (2 * BS) + s, s % 2, s // BS
                if n >= 2:
                    pe.wait_ge(ys_done, 2 * (S - 1))
                pe.wait_ge(hid_lo, 2 * S + 2)
                if s % BS == 0:
                    pe.wait_ge(wd_lo, ep * 2 + k + 1)
                for a in range(2):
                    for f in range(FC):
                        for i, (hp, wp) in enumerate(SPLIT):
                            last = mm((MA, MD)[par][:, a * D:(a + 1) * D], hid[par][hp][:, f, a * P:(a + 1) * P],
                                      WD[k][wp][:, f, :], start=(f + i == 0),
                                      stop=(f == FC - 1 and i == len(SPLIT) - 1))
                last.then_inc(y_full, 1)

            def step_b(ep, s, n, last):
                for ahead, part in ((2, slot_columns), (1, gate)):
                    if not (last and s + ahead >= 2 * BS):
                        part(*((ep, s + ahead) if s + ahead < 2 * BS else (ep + 1, s + ahead - 2 * BS)), n + ahead)
                down(ep, s, n)

            slot_columns(0, 0, 0)
            slot_columns(0, 1, 1)
            gate(0, 0, 0)
            for s in range(2 * BS):
                step_b(0, s, s, False)
            with pe.Fori(1, E // 2 - 1) as ep:
                for s in range(2 * BS):
                    step_b(ep, s, 10, False)
            for s in range(2 * BS):
                step_b(E // 2 - 1, s, 10, True)


def kernel(L0_attn_x, L0_attn_w_qkv, L0_attn_w_out, L0_ffn_w_router, L0_ffn_w_gate, L0_ffn_w_down, L0_c, L0_wmod):
    import numpy as np
    import concourse.bacc as bacc
    from concourse.bass_utils import run_bass_kernel_spmd

    def chunked(a):
        a = np.asarray(a)
        return np.ascontiguousarray(a.reshape(DC, P, -1).transpose(1, 0, 2))

    wdn = np.asarray(L0_ffn_w_down).transpose(0, 2, 1).reshape(E, FC, P, D).transpose(0, 2, 1, 3)
    arrays = {
        "x": np.ascontiguousarray(np.asarray(L0_attn_x).reshape(TOK, D)),
        "wqkv": chunked(np.asarray(L0_attn_w_qkv).T),
        "wo": chunked(np.asarray(L0_attn_w_out).T),
        "wr": chunked(np.asarray(L0_ffn_w_router).T),
        "wg": chunked(np.asarray(L0_ffn_w_gate).T),
        "wd": np.ascontiguousarray(wdn.reshape(E * P, FC * D)),
        "c": chunked(np.asarray(L0_c).T),
        "wmod": chunked(L0_wmod),
    }
    nc = bacc.Bacc("TRN2", target_bir_lowering=False, num_devices=1)
    ins = [nc.dram_tensor(k, a.shape, F32, kind="ExternalInput").ap() for k, a in arrays.items()]
    out = nc.dram_tensor("out", (TOK, D), F32, kind="ExternalOutput").ap()
    xe = nc.dram_tensor("slot_rows", (SLOTS, ROW), F32, kind="Internal").ap()
    adaln_block(nc, *ins, out, xe)
    r = run_bass_kernel_spmd(nc, [arrays], core_ids=[0])
    return np.asarray(r.results[0]["out"]).reshape(BATCH, SEQ, D)
```

```python
from contextlib import ExitStack

import concourse.bass as bass
from concourse import mybir

F32 = mybir.dt.float32
BF16 = mybir.dt.bfloat16
F32R = mybir.dt.float32r
I32 = mybir.dt.int32
ALU = mybir.AluOpType
ACT = mybir.ActivationFunctionType
AX_X = mybir.AxisListType.X

P = 128
D = 256
DC = D // P
H = 16
DH = D // H
HC = H // DC
VW = 32
SW = DH + 1
SPLIT = ((0, 0), (0, 1), (1, 0))
BATCH = 4
SEQ = 2048
TOK = BATCH * SEQ
TILES = TOK // P
GT = 4
GROUPS = TILES // GT
GW = GT * P
E = 8
F = 512
FC = F // P
CAP = 1280
SLOTS = E * CAP
ROW = D + 4 + 3 * BATCH
PARTS = 3
BW = 256
BS = CAP // BW
BIG = 1.0e5
LN_EPS = 1e-5
DEN_EPS = 1e-6
NR = 29


def adaln_block(nc, x, wqkv, wo, wr, wg, wd, c, wmod, out, xe, mod_rows):
    with ExitStack() as ctx:
        def sb(name, shape, dt=F32):
            return ctx.enter_context(nc.sbuf_tensor(name, shape, dt))

        def ps(name):
            return ctx.enter_context(nc.psum_tensor(name, [P, 512], F32))

        def sem(name):
            return ctx.enter_context(nc.semaphore(name))

        X = sb("X", [P, TILES, D])
        Sm = sb("Sm", [P, 2, H, P])
        QT = sb("QT", [P, 2, DC, GW])
        QS = sb("QS", [P, 2, 2, 2, DC, P], F32R)
        KS = sb("KS", [P, 2, 2, DC, P], F32R)
        KT = sb("KT", [P, 2, DC, GW])
        VA = sb("VA", [P, 2, GT, H, SW])
        hT = sb("hT", [P, 2, DC, GW], F32R)
        N1 = sb("N1", [P, GT, D])
        w_d_lo = sb("w_d_lo", [P, FC, D], F32R)
        Hrow = sb("Hrow", [P, 2, GT, ROW])
        h2T = sb("h2T", [P, DC, GW])
        EX = sb("EX", [P, 2, GW])
        Kn = sb("Kn", [P, 2, D])
        Sbd = sb("Sbd", [P, H, VW])
        OTs = sb("OTs", [P, GT, P])
        An = sb("An", [P, H, DH])
        ATs = sb("ATs", [P, 2, DC, P], F32R)
        og = sb("og", [P, D])
        w_qkv = sb("w_qkv", [P, 2, DC, 3 * D], F32R)
        w_o = sb("w_o", [P, 2, DC, D], F32R)
        w_r = sb("w_r", [P, DC, 32])
        lgT = sb("lgT", [P, P])
        w_g = sb("w_g", [P, 2, DC, F], F32R)
        cT = sb("cT", [P, DC, BATCH])
        cS = sb("cS", [P, DC, PARTS * BATCH])
        saca = sb("saca", [P, 2 * DC, BATCH])
        MB = sb("MB", [P, BATCH, 3, D])
        gb16 = sb("gb16", [PARTS * BATCH, PARTS, D], BF16)
        gbp = sb("gbp", [PARTS * BATCH, D], BF16)
        partmask = sb("partmask", [P, PARTS])
        bhot = sb("bhot", [P, BATCH, PARTS * BATCH])
        ohT = [sb(f"ohT{i}", [PARTS * BATCH, BW], BF16) for i in range(2)]
        ident = sb("ident", [P, P])
        tri = sb("tri", [P, P])
        before = sb("before", [P, P], BF16)
        ones = sb("ones", [P, P], BF16)
        headmask = sb("headmask", [P, H, SW])
        pairmask = sb("pairmask", [P, GT])
        parity = sb("parity", [P, 2])
        rev = sb("rev", [P, E])
        base = sb("base", [P, E])
        eid = sb("eid", [P, E])
        tokf = sb("tokf", [P, GT])
        carry = sb("carry", [P, 4, 2])
        mhalf = sb("mhalf", [P, GT])
        idle = sb("idle", [P, 5])
        erow = sb("erow", [P, 1, ROW])
        st1 = sb("st1", [P, GT, 6])
        mv1 = sb("mv1", [P, GT, 2])
        vp1 = sb("vp1", [P, GT])
        rs1 = sb("rs1", [P, GT])
        nm1 = sb("nm1", [P, GT])
        nb1 = sb("nb1", [P, GT])
        st2 = sb("st2", [P, GT, 6])
        mv2 = sb("mv2", [P, GT, 2])
        vp2 = sb("vp2", [P, GT])
        rs2 = sb("rs2", [P, GT])
        nm2 = sb("nm2", [P, GT])
        nb2 = sb("nb2", [P, GT])
        den = sb("den", [P, H])
        rden = sb("rden", [P, H])
        lg = sb("lg", [P, GT, E])
        pos = sb("pos", [P, GT, E])
        lmax = sb("lmax", [P, GT])
        lp = sb("lp", [P, GT, E])
        lp2 = sb("lp2", [P, GT, E])
        cand = sb("cand", [P, GT, E])
        rk = sb("rk", [P, 2, GT])
        oh = sb("oh", [P, 2, GT, E])
        m2 = sb("m2", [P, GT])
        mask = sb("mask", [P, GT, E], BF16)
        msum = sb("msum", [P, E])
        macc = sb("macc", [P, E], BF16)
        drop = sb("drop", [P, GT, E])
        pbase = sb("pbase", [P, GT, E])
        pick = sb("pick", [P, 2, GT, E])
        slot = sb("slot", [P, 2, GT])
        sloti = sb("sloti", [P, 2, GT], I32)
        keep = sb("keep", [P, 2, GT])
        ee = sb("ee", [P, GT, E])
        e12 = sb("e12", [P, 2, GT])
        esum = sb("esum", [P, GT])
        gk = sb("gk", [P, 2, GT])
        Smf = Sm[:].rearrange("p a h i -> p (a h i)")
        mod12 = Smf[0:PARTS * BATCH, DC * 6 * D:(DC * 6 + 4) * D].rearrange("p (k d) -> p k d", k=4)
        tmp, sgn = (EX[0:PARTS * BATCH, i, :].rearrange("p (k d) -> p k d", k=2) for i in range(2))
        wmod_sb = Smf[:, 0:DC * 6 * D].rearrange("p (a n) -> p a n", a=DC)
        KTf = KT[:].rearrange("p a c n -> p (a c n)")
        QTf = QT[:].rearrange("p a c n -> p (a c n)")
        EXf = EX[:].rearrange("p a n -> p (a n)")
        Hf = Hrow[:].rearrange("p a t r -> p (a t r)")
        w_qkv_raw = Hf[:, 0:DC * 3 * D].rearrange("p (c n) -> p c n", c=DC)
        w_o_raw = Hf[:, DC * 3 * D:DC * 4 * D].rearrange("p (c n) -> p c n", c=DC)
        w_g_raw = h2T[:]
        hT_raw = N1[:].rearrange("p t d -> p (t d)").rearrange("p (c n) -> p c n", c=DC)
        VAf = VA[:].rearrange("p a t h w -> p (a t h w)")
        hid_raw = [VAf[:, i * 1024:(i + 1) * 1024].rearrange("p (f n) -> p f n", f=FC) for i in range(2)]
        qs_flat = QS[:].rearrange("p a b c d n -> p (a b c d n)")
        wq_flat = w_qkv[:].rearrange("p k c n -> p (k c n)")
        hid = [[a[:, k * 1024:(k + 1) * 1024].rearrange("p (f n) -> p f n", f=FC) for k in range(2)]
               for a in (qs_flat, hT[:].rearrange("p a c n -> p (a c n)"))]
        WD_raw = [N1[:], h2T[:].rearrange("p c n -> p (c n)").rearrange("p (f n) -> p f n", f=FC)]
        WD = [[wq_flat[:, k * 1024:(k + 1) * 1024].rearrange("p (f n) -> p f n", f=FC) for k in range(2)],
              [wq_flat[:, 2048:3072].rearrange("p (f n) -> p f n", f=FC), w_d_lo[:]]]
        Xr = [Hrow[:, i // 2, (i % 2) * 2:(i % 2) * 2 + 2, :] for i in range(4)]
        Xr.append(QTf[:, 0:2 * ROW].rearrange("p (a r) -> p a r", a=2))
        XT = [a.rearrange("p (k c n) -> p k c n", k=2, c=DC)
              for a in (KS[:].rearrange("p a k c n -> p (a k c n)"), w_o[:].rearrange("p k c n -> p (k c n)"))]
        Ys = [QTf[:, 1024 + i * 512:1536 + i * 512].rearrange("p (a n) -> p a n", a=2) for i in range(2)]
        bs = [VAf[:, 2048 + i * 16:2064 + i * 16] for i in range(2)]
        GB = [EXf[:, i * 512:(i + 1) * 512] for i in range(2)]
        desti = [sb(f"desti{i}", [P, 2], I32) for i in range(2)]
        PJ = [ps("PJ0"), ps("PJ1")]
        SC = [ps("SC0"), ps("SC1")]
        OB = ps("OB")
        SB = ps("SB")
        MA = ps("MA")
        MD = ps("MD")

        lg_ps = PJ[1][:, P:2 * P].rearrange("p (t w) -> p t w", t=GT)
        pos_ps = MD[:, 0:GT * E].rearrange("p (t e) -> p t e", t=GT)

        x_in = [sem("x_in0"), sem("x_in1")]
        w_in = sem("w_in")
        c_in = sem("c_in")
        init_out = sem("init_out")
        fills = sem("fills")
        consts = sem("consts")
        wipe = sem("wipe")
        c_silu = sem("c_silu")
        mod_mm = sem("mod_mm")
        mod_ev = sem("mod_ev")
        mb_ev = sem("mb_ev")
        gate_fix = sem("gate_fix")
        gb_split = sem("gb_split")
        mb_in = sem("mb_in")
        dve_setup = sem("dve_setup")
        bn1 = sem("bn1")
        ag1 = sem("ag1")
        vpe1 = sem("vpe1")
        pow1 = sem("pow1")
        rstd1 = sem("rstd1")
        n1_ready = sem("n1_ready")
        pj_full = sem("pj_full")
        pj_read = sem("pj_read")
        phi_done = sem("phi_done")
        w_hi = sem("w_hi")
        w_lo = sem("w_lo")
        h_raw = sem("h_raw")
        h_hi = sem("h_hi")
        h_lo = sem("h_lo")
        q_hi = sem("q_hi")
        q_lo = sem("q_lo")
        k_hi = sem("k_hi")
        k_lo = sem("k_lo")
        sc_full = sem("sc_full")
        sm_done = sem("sm_done")
        knt_full = sem("knt_full")
        kn_done = sem("kn_done")
        state_full = sem("state_full")
        sbd_done = sem("sbd_done")
        av_done = sem("av_done")
        ot_done = sem("ot_done")
        on_full = sem("on_full")
        den_done = sem("den_done")
        rden_done = sem("rden_done")
        an_done = sem("an_done")
        at_full = sem("at_full")
        at_hi = sem("at_hi")
        at_lo = sem("at_lo")
        op_full = sem("op_full")
        og_done = sem("og_done")
        x1_done = sem("x1_done")
        bn2 = sem("bn2")
        ag2 = sem("ag2")
        vpe2 = sem("vpe2")
        pow2 = sem("pow2")
        rstd2 = sem("rstd2")
        n2_ready = sem("n2_ready")
        last_rows = sem("last_rows")
        h2_scaled = sem("h2_scaled")
        h2_done = sem("h2_done")
        h2t_full = sem("h2t_full")
        h2t_done = sem("h2t_done")
        wr_zero = sem("wr_zero")
        lgt_full = sem("lgt_full")
        lgt_done = sem("lgt_done")
        lg_full = sem("lg_full")
        taken = sem("taken")
        route = sem("route")
        gexp = sem("gexp")
        pos_full = sem("pos_full")
        breath = sem("breath")
        sent = [sem("sent0"), sem("sent1")]
        rows_in = [sem(f"rows_in{i}") for i in range(BS)]
        wd_in = [sem("wd_in0"), sem("wd_in1")]
        xt_full = sem("xt_full")
        xt_hi = sem("xt_hi")
        xt_lo = sem("xt_lo")
        wd_hi = sem("wd_hi")
        wd_lo = sem("wd_lo")
        gate_full = sem("gate_full")
        silu_done = sem("silu_done")
        hid_hi = sem("hid_hi")
        hid_lo = sem("hid_lo")
        y_full = sem("y_full")
        meta = sem("meta")
        ys_done = sem("ys_done")
        y_sent = [sem("y_sent0"), sem("y_sent1")]
        oh_done = sem("oh_done")
        gb_full = sem("gb_full")
        gb_done = sem("gb_done")
        stored = sem("stored")

        N_CONST = 16 + BATCH + 1
        block = ctx.enter_context(nc.Block())

        def at_least(eng, s, n):
            if not (isinstance(n, int) and n <= 0):
                eng.wait_ge(s, n)

        def run_slots(eng, slot, early=None, early_at=1):
            for it in (-1, 0, 1):
                for j in range(8):
                    slot(it, j, it * 8 + j)
                    if early and it == -1 and j == early_at:
                        early()
            with eng.Fori(2, TILES // 8 - 1) as it:
                for j in range(8):
                    slot(it, j, 24 + j)
            for it in (TILES // 8 - 1, TILES // 8):
                for j in range(8):
                    slot(it, j, it * 8 + j)
            for j in range(2):
                slot(TILES // 8 + 1, j, TILES + 8 + j)

        def tile_ok(n):
            return 0 <= n < TILES

        def group_ok(n):
            return 0 <= n < GROUPS

        def halves(it, back):
            return (it - back) // 2 if isinstance(it, int) else (it - back) // 2

        def headslot(r):
            return [2 * r, 2 * r + 1]

        @block.sync
        def _(sp):
            xg = x.rearrange("(g t p) d -> g p t d", t=GT, p=P)
            sp.dma_start(X[:, 0:GT, :], xg[0]).then_inc(x_in[0], 16)
            sp.dma_start(X[:, GT:2 * GT, :], xg[1]).then_inc(x_in[1], 16)
            sp.wait_ge(gate_fix, 5)
            sp.dma_start(mod_rows, mod12[0:BATCH, 0:3, :].rearrange("p k d -> p (k d)")).then_inc(mb_in, 16)
            sp.wait_ge(mb_in, 16)
            sp.dma_start(MB[:].rearrange("p b k d -> p (b k d)"),
                         mod_rows.rearrange("b n -> (b n)").unsqueeze(0).to_broadcast([P, BATCH * 3 * D])
                         ).then_inc(mb_in, 16)
            with sp.Fori(1, GROUPS // 2) as i:
                for k in range(2):
                    sp.wait_ge(x_in[k], i * 16)
                    sp.dma_start(X[:, bass.ds(i * (2 * GT) + k * GT, GT), :],
                                 x[bass.ds((i * 2 + k) * GW, GW), :].rearrange("(t p) d -> p t d", p=P)
                                 ).then_inc(x_in[k], 16)
            with sp.Fori(0, GROUPS) as g:
                sp.wait_ge(x1_done, g * GT + GT)
                sp.dma_start(out[bass.ds(g * GW, GW), :].rearrange("(t p) d -> p t d", p=P),
                             X[:, bass.ds(g * GT, GT), :]).then_inc(stored, 16)
            def load_wd(ep, k, n):
                if n >= 1:
                    sp.wait_ge(wd_hi, ep * 2 + k - 1)
                    sp.wait_ge(wd_lo, ep * 2 + k - 1)
                sp.dma_start(WD_raw[k].rearrange("p f n -> p (f n)"),
                             wd[bass.ds((ep * 2 + k) * P, P), :]).then_inc(wd_in[k], 16)

            sp.wait_ge(last_rows, 1)
            sp.wait_ge(h2t_done, 2 * GROUPS)
            load_wd(0, 0, 0)
            for k in range(2):
                sp.wait_ge(sent[k], 128 * (GROUPS // 2))
            sp.wait_ge(av_done, TILES)
            sp.wait_ge(route, NR * GROUPS)

            def load_rows(ep, s, n):
                S = ep * (2 * BS) + s
                if n >= BS:
                    sp.wait_ge(ys_done, 2 * (S - BS) + 2)
                sp.dma_start(Xr[s % BS],
                             xe[bass.ds(S * BW, BW), :].rearrange("(a p) r -> p a r", p=P)
                             ).then_inc(rows_in[s % BS], 16)

            def expert_pair(ep, n):
                for s in range(2 * BS):
                    if s % BS == 0 and not (n == 0 and s == 0):
                        load_wd(ep, s // BS, n)
                    load_rows(ep, s, 10 * n + s)

            expert_pair(0, 0)
            with sp.Fori(1, E // 2) as ep:
                expert_pair(ep, 1)

        @block.gpsimd
        def _(pool):
            pool.memset(w_r[:], 0.0).then_inc(wr_zero, 1)
            pool.memset(bhot[:], 0.0).then_inc(fills, 1)
            pool.memset(partmask[:], 1.0).then_inc(fills, 1)
            pool.memset(erow[:], 0.0).then_inc(fills, 1)
            pool.memset(ident[:], 1.0).then_inc(fills, 1)
            pool.memset(tri[:], 1.0).then_inc(fills, 1)
            pool.memset(headmask[:], 1.0).then_inc(fills, 1)
            pool.memset(pairmask[:], 1.0).then_inc(fills, 1)
            pool.memset(before[:], 1.0).then_inc(fills, 1)
            pool.memset(ones[:], 1.0).then_inc(consts, 1)
            pool.memset(Sbd[:], 0.0).then_inc(consts, 1)
            pool.memset(mhalf[:], -0.5).then_inc(consts, 1)
            pool.memset(macc[:], 0.0).then_inc(consts, 1)
            pool.memset(e12[:], 1.0).then_inc(consts, 1)
            pool.iota(rev[:], [[-1, E]], base=E, channel_multiplier=0,
                      allow_small_or_imprecise_dtypes=True).then_inc(consts, 1)
            pool.iota(base[:], [[CAP, E]], base=0, channel_multiplier=0,
                      allow_small_or_imprecise_dtypes=True).then_inc(consts, 1)
            pool.iota(eid[:], [[1, E]], base=0, channel_multiplier=0,
                      allow_small_or_imprecise_dtypes=True).then_inc(consts, 1)
            pool.iota(tokf[:], [[P, GT]], base=0, channel_multiplier=1,
                      allow_small_or_imprecise_dtypes=True).then_inc(consts, 1)
            pool.iota(carry[:], [[0, 4], [-1, 2]], base=1, channel_multiplier=0,
                      allow_small_or_imprecise_dtypes=True).then_inc(consts, 1)
            pool.wait_ge(fills, 8)
            for b in range(BATCH):
                pool.memset(bhot[:, b, :].rearrange("p (k b) -> p k b", k=PARTS)[:, :, b:b + 1],
                            1.0).then_inc(consts, 1)
            pool.memset(erow[:, :, D + 2:D + 3], BIG).then_inc(consts, 1)
            pool.affine_select(out=ident[:], in_=ident[:], pattern=[[-1, P]], compare_op=ALU.is_equal, fill=0.0,
                               base=0, channel_multiplier=1).then_inc(consts, 1)
            pool.affine_select(out=tri[:], in_=tri[:], pattern=[[1, P]], compare_op=ALU.is_ge, fill=0.0,
                               base=0, channel_multiplier=-1).then_inc(consts, 1)
            pool.affine_select(out=before[:], in_=before[:], pattern=[[1, P]], compare_op=ALU.is_gt, fill=0.0,
                               base=0, channel_multiplier=-1).then_inc(consts, 1)
            hm = headmask[:].rearrange("p (c s) w -> p c s w", c=DC)
            pool.affine_select(out=hm, in_=hm, pattern=[[0, DC], [-DH, HC], [0, SW]], compare_op=ALU.is_ge,
                               fill=0.0, base=0, channel_multiplier=1).then_inc(wipe, 1)
            pool.affine_select(out=pairmask[:], in_=pairmask[:], pattern=[[-2 * DH, GT]], compare_op=ALU.is_ge,
                               fill=0.0, base=0, channel_multiplier=1).then_inc(wipe, 1)
            pool.affine_select(out=partmask[:], in_=partmask[:], pattern=[[-BATCH, PARTS]], compare_op=ALU.is_ge,
                               fill=0.0, base=0, channel_multiplier=1).then_inc(wipe, 1)
            pool.wait_ge(wipe, 3)
            pool.affine_select(out=partmask[:], in_=partmask[:], pattern=[[BATCH, PARTS]], compare_op=ALU.is_ge,
                               fill=0.0, base=BATCH - 1, channel_multiplier=-1).then_inc(consts, 1)
            pool.affine_select(out=hm, in_=hm, pattern=[[0, DC], [DH, HC], [0, SW]], compare_op=ALU.is_ge,
                               fill=0.0, base=DH - 1, channel_multiplier=-1).then_inc(consts, 1)
            pool.affine_select(out=pairmask[:], in_=pairmask[:], pattern=[[2 * DH, GT]], compare_op=ALU.is_ge,
                               fill=0.0, base=DH - 1, channel_multiplier=-1).then_inc(consts, 1)

            def breather(k):
                pool.tensor_tensor(idle[:, k:k + 1], mhalf[:, 0:1], mhalf[:, 0:1], ALU.add).then_inc(breath, 1)

            def slot_(it, j, n):
                T = it * 8 + j
                G = it * 2 + j // 4
                gn, q, gp, tp = n // 4, j % 4, (j // 4) % 2, j % 2
                if tile_ok(n + 1):
                    q1, g1 = (q + 1) % 4, (gp if q < 3 else 1 - gp)
                    pool.wait_ge(k_hi, T + 2)
                    pool.tensor_tensor(KS[:, 1 - tp, 1], KT[:, g1, :, q1 * P:(q1 + 1) * P],
                                       KS[:, 1 - tp, 0].bitcast(F32), ALU.subtract).then_inc(k_lo, 1)
                leaving = q < 2 and group_ok(gn - 3)
                if leaving and q == 0:
                    pool.wait_ge(route, NR * (G - 3) + NR)
                    if gn - 3 == GROUPS - 1:
                        pool.wait_ge(last_rows, 1)
                    if gn == 3:
                        pool.wait_ge(init_out, 16)
                def modulate():
                    hp = 1 - gp
                    if gn == 1 and q == 2:
                        pool.wait_ge(mb_in, 32)
                    b = halves(it, 0 if gp == 1 else 1)
                    pool.wait_ge(n2_ready, 4 * (G - 1) + 2 * (q - 1))
                    breather(2 * q - 4)
                    for t in (2 * q - 4, 2 * q - 3):
                        pool.tensor_tensor(Hrow[:, hp, t, 0:D], Hrow[:, hp, t, 0:D],
                                           MB[:, bass.ds(b, 1), 2, :].rearrange("p a d -> p (a d)"),
                                           ALU.mult).then_inc(h2_scaled, 1)
                    pool.wait_ge(h2_scaled, 4 * (G - 1) + 2 * (q - 1))
                    breather(2 * q - 3)
                    for t in (2 * q - 4, 2 * q - 3):
                        pool.tensor_tensor(Hrow[:, hp, t, 0:D], Hrow[:, hp, t, 0:D],
                                           MB[:, bass.ds(b, 1), 1, :].rearrange("p a d -> p (a d)"),
                                           ALU.add).then_inc(h2_done, 1)

                if q == 3 and group_ok(gn - 1) and gn != GROUPS:
                    modulate()
                def send(half):
                    for t in (2 * half, 2 * half + 1):
                        for k in range(2):
                            pool.indirect_dma_start(
                                xe, bass.IndirectOffsetOnAxis(sloti[:, k, t:t + 1], 0), Hrow[:, 1 - gp, t, :], None,
                                bounds_check=SLOTS - 1, oob_is_err=False).then_inc(sent[1 - gp], 16)

                if leaving and q == 1 and gn != GROUPS:
                    send(1)
                if q == 0 and group_ok(gn + 1):
                    for cidx in range(DC):
                        pool.wait_ge(h_hi, 2 * (G + 1) + cidx + 1)
                        pool.tensor_tensor(hT[:, 1, cidx, :], hT_raw[:, cidx, :], hT[:, 0, cidx, :].bitcast(F32),
                                           ALU.subtract).then_inc(h_lo, 1)
                if tile_ok(n - 1):
                    pool.wait_ge(og_done, T)
                    xt = X[:, bass.ds(T - 1, 1), :].rearrange("p a d -> p (a d)")
                    pool.tensor_tensor(xt, xt, og[:], ALU.add).then_inc(x1_done, 1)
                if q == 2 and group_ok(gn - 1) and gn != GROUPS:
                    modulate()
                def deviations(rs, vp, nm, nb, s_vp, s_pow, s_rstd, count):
                    pool.wait_ge(s_vp, count)
                    pool.tensor_tensor(rs[:], vp[:], mhalf[:], ALU.pow).then_inc(s_pow, 1)
                    pool.wait_ge(s_pow, count)
                    pool.tensor_tensor(nb[:], nm[:], rs[:], ALU.mult).then_inc(s_rstd, 1)

                if q == 1 and group_ok(gn + 2):
                    deviations(rs1, vp1, nm1, nb1, vpe1, pow1, rstd1, G + 3)
                if q == 1 and group_ok(gn - 1):
                    deviations(rs2, vp2, nm2, nb2, vpe2, pow2, rstd2, G)
                if leaving and q == 0 and gn != GROUPS:
                    send(0)
                if leaving and q == 1 and gn == GROUPS:
                    send(0)
                    send(1)

            pool.wait_ge(consts, N_CONST)
            run_slots(pool, slot_)

            def down_lo(ep, k):
                pool.wait_ge(wd_hi, ep * 2 + k + 1)
                pool.tensor_tensor(WD[k][1], WD_raw[k], WD[k][0].bitcast(F32), ALU.subtract).then_inc(wd_lo, 1)

            def give_back(ep, s, n):
                S = ep * (2 * BS) + s
                if s % BS == 2 and not (n >= 100 and s >= BS):
                    down_lo(*((ep, 1) if s < BS else (ep + 1, 0)))
                if s % BS == 0 and n >= 1:
                    pool.wait_ge(y_sent[0], 32 * (ep * BS + (s + 1) // 2))
                    pool.wait_ge(y_sent[1], 32 * (ep * BS + s // 2))
                pool.wait_ge(breath, 4 * (GROUPS - 1) + S)
                pool.wait_ge(ys_done, 2 * S + 2)
                breather(4)
                for a in range(2):
                    pool.indirect_dma_start(
                        out, bass.IndirectOffsetOnAxis(desti[s % 2][:, a:a + 1], 0), Ys[s % 2][:, a, :], None,
                        bounds_check=TOK - 1, oob_is_err=False, compute_op=ALU.add).then_inc(y_sent[s % 2], 16)

            down_lo(0, 0)
            pool.wait_ge(stored, 16 * GROUPS)
            for s in range(2 * BS):
                give_back(0, s, s)
            with pool.Fori(1, E // 2 - 1) as ep:
                for s in range(2 * BS):
                    give_back(ep, s, 10)
            for s in range(2 * BS):
                give_back(E // 2 - 1, s, 100)
            for k in range(2):
                pool.wait_ge(y_sent[k], 32 * (E * BS // 2))

        @block.scalar
        def _(act):
            act.dma_start(cT[:], c).then_inc(c_in, 16)
            act.dma_start(wmod_sb, wmod).then_inc(c_in, 16)
            act.wait_ge(wr_zero, 1)
            for dst, src in ((w_qkv_raw, wqkv), (w_o_raw, wo), (w_r[:, :, 0:E], wr), (w_g_raw, wg)):
                act.dma_start(dst, src).then_inc(w_in, 16)
            act.wait_ge(consts, N_CONST)
            act.dma_start(xe.rearrange("(p n) r -> p n r", p=P),
                          erow[:].to_broadcast([P, SLOTS // P, ROW])).then_inc(init_out, 16)
            act.wait_ge(c_in, 32)
            act.activation(cS[:].rearrange("p c (k b) -> p c k b", k=PARTS),
                           cT[:].unsqueeze(2).to_broadcast([P, DC, PARTS, BATCH]), ACT.Silu).then_inc(c_silu, 1)
            act.wait_ge(mod_mm, 1)
            act.activation(saca[:, 0:DC, :], MA[:, 0:DC * BATCH].rearrange("p (a b) -> p a b", a=DC),
                           ACT.Copy).then_inc(mod_ev, 1)
            act.activation(saca[:, DC:2 * DC, :],
                           MA[:, DC * BATCH:2 * DC * BATCH].rearrange("p (a b) -> p a b", a=DC),
                           ACT.Copy, bias=1.0).then_inc(mod_ev, 1)

            act.wait_ge(w_in, 64)
            for dst, src in ((w_qkv, w_qkv_raw), (w_o, w_o_raw)):
                act.activation(dst[:, 0], src, ACT.Copy).then_inc(w_hi, 1)

            def early():
                act.activation(w_g[:, 0], w_g_raw, ACT.Copy).then_inc(w_hi, 1)

            def stage1_transposed(it, G, cidx, bcol):
                N = G + 1
                act.wait_ge(pj_full, 8 * N + 2)
                act.activation(hT_raw[:, cidx, :], PJ[cidx][:], ACT.Identity,
                               scale=saca[:, DC + cidx, bass.ds(bcol, 1)],
                               bias=saca[:, cidx, bass.ds(bcol, 1)]).then_inc(h_raw, 1)

            def stage1_hi(G):
                N = G + 1
                for cidx in range(DC):
                    act.wait_ge(h_raw, 2 * N + cidx + 1)
                    act.activation(hT[:, 0, cidx, :], hT_raw[:, cidx, :], ACT.Copy).then_inc(h_hi, 1)

            def stage1_qk(G, m, npar, n_next):
                N = G + 1
                act.wait_ge(pj_full, 8 * N + m + 3)
                if n_next == 0 and m == 0:
                    act.wait_ge(gb_split, 8)
                if n_next >= 1 or m >= 2:
                    act.wait_ge(phi_done, 4 * N + m - 1)
                if n_next >= 2:
                    act.wait_ge(av_done, 4 * (N - 1))
                dst = QT if m < 2 else KT
                act.activation(EX[:, m % 2, :], PJ[m % 2][:], ACT.Exp)
                act.activation(dst[:, npar, m % 2, :], PJ[m % 2][:], ACT.Relu).then_inc(pj_read, 1)

            def normalise(dst, t, xt, rs, nb, s_ready):
                act.activation(dst, X[:, bass.ds(xt, 1), :].rearrange("p a d -> p (a d)"), ACT.Identity,
                               scale=rs[:, t:t + 1], bias=nb[:, t:t + 1]).then_inc(s_ready, 1)

            def ln2_norm(it, G, gn, gp):
                act.wait_ge(rstd2, G)
                if gn == GROUPS:
                    act.wait_ge(h_lo, 2 * GROUPS)
                elif gn >= 3:
                    act.wait_ge(sent[1 - gp], 128 * ((it - 1) if gp == 0 else it))
                for t in range(GT):
                    normalise(N1[:, t, :] if gn == GROUPS else Hrow[:, 1 - gp, t, 0:D], t, (G - 1) * GT + t, rs2, nb2, n2_ready)

            def ln1_norm(G, gl):
                L = G + 2
                act.wait_ge(rstd1, L + 1)
                if gl >= 1:
                    act.wait_ge(h_lo, 2 * L)
                for t in range(GT):
                    normalise(N1[:, t, :], t, L * GT + t, rs1, nb1, n1_ready)

            def take(dst, src, s_full, G):
                act.wait_ge(s_full, G - 1)
                act.activation(dst[:], src, ACT.Copy).then_inc(taken, 1)

            def next_tile_hi(T, q, gp, tp, n):
                q1, g1 = (q + 1) % 4, (gp if q < 3 else 1 - gp)
                act.wait_ge(phi_done, (T + 1 - q1) + 4)
                if n >= 1:
                    act.wait_ge(sc_full, 4 * T)
                for odd in range(2):
                    act.activation(QS[:, 1 - tp, 0, odd], QT[:, g1, :, q1 * P:(q1 + 1) * P], ACT.Copy,
                                   scale=parity[:, odd:odd + 1]).then_inc(q_hi, 1)
                act.activation(KS[:, 1 - tp, 0], KT[:, g1, :, q1 * P:(q1 + 1) * P], ACT.Copy).then_inc(k_hi, 1)

            def stage1_v(G, u, npar, n_next):
                N = G + 1
                act.wait_ge(pj_full, 8 * N + u + 7)
                if n_next >= 2:
                    act.wait_ge(av_done, 4 * (N - 1))
                act.activation(VA[:, npar, 2 * u:2 * u + 2, :, 0:DH],
                               PJ[u][:].rearrange("p (t h e) -> p t h e", t=2, h=H),
                               ACT.Copy).then_inc(pj_read, 1)

            def slot_(it, j, n):
                T = it * 8 + j
                G = it * 2 + j // 4
                gn, q, gp = n // 4, j % 4, (j // 4) % 2
                npar, nx = 1 - gp, n // 4 + 1
                tp = j % 2
                stage1 = group_ok(nx)
                if q == 1 and group_ok(gn - 2):
                    act.wait_ge(lgt_full, G - 1)
                    act.activation(lgT[:], PJ[1][:, 0:P], ACT.Copy).then_inc(lgt_done, 1)
                if tile_ok(n - 1):
                    act.wait_ge(av_done, T)
                    at_least(act, on_full, T - 1)
                    act.activation(OTs[:].rearrange("p a i -> p (a i)"), OB[:], ACT.Copy).then_inc(ot_done, 1)
                if q == 1 and group_ok(gn - 2):
                    take(lg, lg_ps[:, :, 0:E], lg_full, G)
                if q == 3 and group_ok(gn - 2):
                    take(pos, pos_ps, pos_full, G)
                if tile_ok(n + 1):
                    next_tile_hi(T, q, gp, tp, n)
                if q == 0 and group_ok(gn - 2):
                    for cidx in range(DC):
                        act.wait_ge(h2t_full, 2 * (G - 2) + cidx + 1)
                        if gn >= 3:
                            act.wait_ge(lg_full, G - 2)
                        act.activation(h2T[:, cidx, :], PJ[cidx][:], ACT.Copy).then_inc(h2t_done, 1)
                if q == 0 and gn == GROUPS + 1:
                    act.wait_ge(sent[gp], 128 * (GROUPS // 2 - 1))
                    act.activation(Hrow[:, gp, :, 0:D], N1[:], ACT.Copy).then_inc(last_rows, 1)
                if tile_ok(n):
                    act.wait_ge(knt_full, T + 1)
                    at_least(act, state_full, T - 1)
                    act.activation(Kn[:, tp, :], MA[:, 0:D], ACT.Copy).then_inc(kn_done, 1)
                if stage1:
                    if q == 0:
                        bcol = halves(it, 0) if gp == 0 else halves(it, -1)
                        if isinstance(bcol, int):
                            bcol = max(bcol, 0)
                        stage1_transposed(it, G, 0, bcol)
                        stage1_transposed(it, G, 1, bcol)
                    elif q == 1:
                        stage1_qk(G, 0, npar, nx)
                    elif q == 2:
                        stage1_qk(G, 2, npar, nx)
                    else:
                        stage1_v(G, 0, npar, nx)
                if tile_ok(n - 1):
                    act.wait_ge(at_full, T)
                    at_least(act, op_full, T - 1)
                    act.activation(ATs[:, 0].rearrange("p c i -> p (c i)"), MA[:, 0:D], ACT.Copy).then_inc(at_hi, 1)
                if q == 2 and group_ok(gn - 1):
                    ln2_norm(it, G, gn, gp)
                if q == 3 and group_ok(gn + 2):
                    ln1_norm(G, gn + 2)
                if stage1:
                    if q == 0:
                        stage1_hi(G)
                    elif q == 1:
                        stage1_qk(G, 1, npar, nx)
                    elif q == 2:
                        stage1_qk(G, 3, npar, nx)
                    elif q == 3:
                        stage1_v(G, 1, npar, nx)
                if q == 2 and group_ok(gn - 2):
                    g = G - 2
                    act.wait_ge(route, NR * g + 8)
                    act.activation(ee[:], lp[:], ACT.Exp).then_inc(gexp, 1)
                    act.activation(e12[:, 1, :], m2[:], ACT.Exp).then_inc(gexp, 1)

            act.wait_ge(dve_setup, 2)
            act.wait_ge(mod_ev, 2)
            run_slots(act, slot_, early, 4)

            def hidden(ep, s, n):
                S = ep * (2 * BS) + s
                for hh in range(2):
                    act.wait_ge(gate_full, 2 * S + hh + 1)
                    if n >= 2:
                        act.wait_ge(hid_lo, 2 * (S - 2) + hh + 1)
                        act.wait_ge(y_full, S - 1)
                    f = slice(2 * hh, 2 * hh + 2)
                    act.activation(hid_raw[s % 2][:, f, :], SC[hh][:].rearrange("p (f n) -> p f n", f=2),
                                   ACT.Silu).then_inc(silu_done, 1)
                    act.wait_ge(silu_done, 2 * S + hh + 1)
                    act.activation(hid[s % 2][0][:, f, :], hid_raw[s % 2][:, f, :], ACT.Copy).then_inc(hid_hi, 1)

            def slots_hi(ep, s, n):
                S = ep * (2 * BS) + s
                act.wait_ge(xt_full, S + 1)
                if n >= 2:
                    act.wait_ge(gate_full, 2 * (S - 1))
                act.activation(XT[s % 2][:, 0].rearrange("p c n -> p (c n)"), PJ[s % 2][:],
                               ACT.Copy).then_inc(xt_hi, 1)

            def down_hi(ep, k, n):
                act.wait_ge(wd_in[k], 16 * (ep + 1))
                if n >= 1:
                    act.wait_ge(y_full, (ep * 2 + k - 1) * BS)
                act.activation(WD[k][0], WD_raw[k], ACT.Copy).then_inc(wd_hi, 1)

            def batches(ep, s, n):
                S = ep * (2 * BS) + s
                act.wait_ge(xt_full, S + 1)
                if n >= 2:
                    act.wait_ge(gb_full, S - 1)
                act.activation(ohT[s % 2][:], OB[0:PARTS * BATCH, 0:BW], ACT.Copy).then_inc(oh_done, 1)

            def gates(ep, s, n):
                S = ep * (2 * BS) + s
                act.wait_ge(gb_full, S + 1)
                if n >= 2:
                    act.wait_ge(ys_done, 2 * (S - 1))
                act.activation(GB[s % 2], SB[:], ACT.Copy).then_inc(gb_done, 1)

            def step_b(ep, s, n, last):
                if not (last and s >= 2 * BS - 2):
                    slots_hi(*((ep, s + 2) if s + 2 < 2 * BS else (ep + 1, s + 2 - 2 * BS)), n + 2)
                    batches(*((ep, s + 2) if s + 2 < 2 * BS else (ep + 1, s + 2 - 2 * BS)), n + 2)
                if not (last and s == 2 * BS - 1):
                    e1, s1 = (ep, s + 1) if s + 1 < 2 * BS else (ep + 1, 0)
                    gates(e1, s1, n + 1)
                    hidden(e1, s1, n + 1)
                if s % BS == 1 and not (last and s >= BS):
                    down_hi(*((ep, 1, n // 10) if s < BS else (ep + 1, 0, 1)))

            down_hi(0, 0, 0)
            for s in range(2):
                slots_hi(0, s, s)
                batches(0, s, s)
            gates(0, 0, 0)
            hidden(0, 0, 0)
            for s in range(2 * BS):
                step_b(0, s, s, False)
            with act.Fori(1, E // 2 - 1) as ep:
                for s in range(2 * BS):
                    step_b(ep, s, 10, False)
            for s in range(2 * BS):
                step_b(E // 2 - 1, s, 10, True)

        @block.vector
        def _(dve):
            dve.memset(VA[:], 1.0).then_inc(dve_setup, 1)
            dve.wait_ge(consts, N_CONST)
            dve.tensor_reduce(parity[:, 0:1], pairmask[:], AX_X, ALU.add).then_inc(gate_fix, 1)
            dve.wait_ge(gate_fix, 1)
            dve.tensor_scalar(parity[:, 1:2], parity[:, 0:1], -1.0, 1.0, ALU.mult, ALU.add).then_inc(dve_setup, 1)
            def early():
                for k, (dst, src) in enumerate(((w_qkv, w_qkv_raw), (w_o, w_o_raw))):
                    dve.wait_ge(w_hi, k + 1)
                    dve.tensor_tensor(dst[:, 1], src, dst[:, 0].bitcast(F32), ALU.subtract).then_inc(w_lo, 1)
                dve.wait_ge(mod_mm, 3)
                dve.tensor_copy(mod12[:, 0:2, :], SC0m[:]).then_inc(gate_fix, 1)
                dve.tensor_scalar(mod12[:, 2, :], SC1m[:, 0, :], 1.0, None, ALU.add)
                dve.tensor_copy(mod12[:, 3, :], SC1m[:, 1, :]).then_inc(gate_fix, 1)
                dve.wait_ge(gate_fix, 3)
                gate = mod12[:, 0:4:3, :]
                dve.scalar_tensor_tensor(tmp, gate, -1.0, gate, ALU.mult, ALU.max)
                dve.tensor_scalar(sgn, gate, 0.0, 2.0, ALU.is_ge, ALU.mult).then_inc(gate_fix, 1)
                dve.wait_ge(gate_fix, 4)
                dve.tensor_scalar(tmp, tmp, 0.25, None, ALU.max).then_inc(mb_ev, 1)
                dve.wait_ge(mb_ev, 1)
                dve.scalar_tensor_tensor(gate, sgn, -1.0, tmp, ALU.add, ALU.mult).then_inc(gate_fix, 1)
                dve.wait_ge(gate_fix, 5)
                m = 0

                def part(ins):
                    nonlocal m
                    m += 1
                    ins.then_inc(gb_split, 1)
                    dve.wait_ge(gb_split, m)
                srcs = (mod12[:, 3, :], tmp[:, 0, :], tmp[:, 1, :])
                for k, src in enumerate(srcs):
                    part(dve.tensor_copy(gb16[:, k, :], src))
                    if k < PARTS - 1:
                        part(dve.tensor_tensor(srcs[k + 1], src, gb16[:, k, :], ALU.subtract))
                part(dve.tensor_scalar(gbp[:], gb16[:, 0, :], partmask[0:PARTS * BATCH, 0:1], None, ALU.mult))
                for k in (1, 2):
                    part(dve.scalar_tensor_tensor(gbp[:], gb16[:, k, :], partmask[0:PARTS * BATCH, k:k + 1], gbp[:],
                                                  ALU.mult, ALU.add))
                dve.wait_ge(w_hi, 3)
                dve.tensor_tensor(w_g[:, 1], w_g_raw, w_g[:, 0].bitcast(F32), ALU.subtract).then_inc(w_lo, 1)

            SC0m, SC1m = (SC[k][0:PARTS * BATCH, :].rearrange("p (k d) -> p k d", k=2) for k in range(2))

            def masked_scores(T, r, tp, n):
                dve.wait_ge(sc_full, 4 * T + r + 1)
                if r == 0 and n >= 2:
                    dve.wait_ge(av_done, T - 1)
                o = Sm[:, tp].rearrange("p (c s) i -> p c s i", c=DC)[:, :, 2 * r:2 * r + 2, :]
                dve.tensor_tensor(o, SC[r % 2][:].rearrange("p (c s i) -> p c s i", c=2, s=2),
                                  tri[:].unsqueeze(1).unsqueeze(1).to_broadcast([P, 2, 2, P]),
                                  ALU.mult).then_inc(sm_done, 1)

            def normalise_heads(T, between):
                on = MD[:].rearrange("p (h w) -> p h w", h=H)
                dve.wait_ge(on_full, T)
                dve.tensor_scalar(den[:].unsqueeze(2), on[:, :, DH:DH + 1], DEN_EPS, None, ALU.max).then_inc(den_done, 1)
                between(False)
                dve.wait_ge(den_done, T)
                dve.reciprocal(rden[:], den[:]).then_inc(rden_done, 1)
                between()
                dve.wait_ge(rden_done, T)
                at_least(dve, at_full, T - 1)
                dve.tensor_tensor(An[:], on[:, :, 0:DH], rden[:].unsqueeze(2).to_broadcast([P, H, DH]),
                                  ALU.mult).then_inc(an_done, 1)

            def attention_lo(T):
                dve.wait_ge(at_hi, T)
                dve.tensor_tensor(ATs[:, 1].rearrange("p c i -> p (c i)"), MA[:, 0:D],
                                  ATs[:, 0].rearrange("p c i -> p (c i)").bitcast(F32),
                                  ALU.subtract).then_inc(at_lo, 1)

            def next_tile_lo(T, q, gp, tp, between):
                q1, g1 = (q + 1) % 4, (gp if q < 3 else 1 - gp)
                for odd in range(2):
                    dve.wait_ge(q_hi, 2 * (T + 1) + odd + 1)
                    dve.scalar_tensor_tensor(QS[:, 1 - tp, 1, odd], QT[:, g1, :, q1 * P:(q1 + 1) * P],
                                             parity[:, odd:odd + 1], QS[:, 1 - tp, 0, odd].bitcast(F32),
                                             ALU.mult, ALU.subtract).then_inc(q_lo, 1)
                    between()

            def state(it, T, j):
                keep_it = carry[:].rearrange("p a b -> p (a b)")[:, bass.ds(it, 1)] if j == 7 else 1.0
                dve.wait_ge(state_full, T + 1)
                dve.scalar_tensor_tensor(Sbd[:, :, 0:SW], SB[:, 0:H * SW].rearrange("p (h w) -> p h w", h=H),
                                         keep_it, headmask[:], ALU.mult, ALU.mult).then_inc(sbd_done, 1)

            def phi(G, m, npar):
                N = G + 1
                dst = (QT if m < 2 else KT)[:, npar, m % 2, :]
                dve.wait_ge(pj_read, 6 * N + m + 1)
                dve.scalar_tensor_tensor(dst, dst, 1.0, EX[:, m % 2, :], ALU.add, ALU.min).then_inc(phi_done, 1)

            def ln_tail(st, mv, vp, nm, s_ag, s_vp, count):
                for t in range(GT):
                    dve.bn_aggr(mv[:, t, :], st[:, t, :]).then_inc(s_ag, 1)
                dve.wait_ge(s_ag, 4 * count)
                dve.tensor_scalar(nm[:].unsqueeze(2), mv[:, :, 0:1], -1.0, None, ALU.mult)
                dve.tensor_scalar(vp[:].unsqueeze(2), mv[:, :, 1:2], LN_EPS, None, ALU.add).then_inc(s_vp, 1)

            def ln1_stats(it, G, gp):
                L = G + 2
                xi = it + 2 if not isinstance(it, int) else it + 2
                dve.wait_ge(x_in[gp], 16 * xi)
                for t in range(GT):
                    dve.bn_stats(st1[:, t, :], X[:, bass.ds(L * GT + t, 1), :].rearrange("p a d -> p (a d)")
                                 ).then_inc(bn1, 1)

            revb = rev[:].unsqueeze(1).to_broadcast([P, GT, E])

            def wide(a):
                return a.unsqueeze(2).to_broadcast([P, GT, E])

            def done(ins):
                ins.then_inc(route, 1)

            def choose(g, k):
                if k == 0:
                    dve.wait_ge(taken, 2 * g + 1)
                else:
                    dve.wait_ge(route, NR * g + k)
                if k == 0:
                    done(dve.tensor_reduce(lmax[:], lg[:], AX_X, ALU.max))
                elif k == 1:
                    done(dve.tensor_tensor(lp[:], lg[:], wide(lmax[:]), ALU.subtract))
                elif k == 2:
                    done(dve.tensor_scalar(lp[:], lp[:], -104.0, None, ALU.max))
                elif k == 3:
                    done(dve.scalar_tensor_tensor(cand[:], lp[:], 0.0, revb, ALU.is_equal, ALU.mult))
                elif k == 4:
                    done(dve.tensor_reduce(rk[:, 0, :], cand[:], AX_X, ALU.max))
                elif k == 5:
                    done(dve.tensor_tensor(oh[:, 0], revb, wide(rk[:, 0, :]), ALU.is_equal))
                elif k == 6:
                    done(dve.scalar_tensor_tensor(lp2[:], oh[:, 0], -1.0e30, lp[:], ALU.mult, ALU.add))
                elif k == 7:
                    done(dve.tensor_reduce(m2[:], lp2[:], AX_X, ALU.max))
                elif k == 8:
                    done(dve.tensor_tensor(cand[:], lp2[:], wide(m2[:]), ALU.is_equal))
                elif k == 9:
                    done(dve.tensor_tensor(cand[:], cand[:], revb, ALU.mult))
                elif k == 10:
                    done(dve.tensor_reduce(rk[:, 1, :], cand[:], AX_X, ALU.max))
                elif k == 11:
                    done(dve.tensor_tensor(oh[:, 1], revb, wide(rk[:, 1, :]), ALU.is_equal))
                elif k == 12:
                    done(dve.tensor_tensor(mask[:], oh[:, 0], oh[:, 1], ALU.add))

            def place(it, g, pg, gn, k):
                before_step = (13, 17, 20, 22, 23, 25, 26, 27, 28, 29)
                if k == 0:
                    dve.wait_ge(taken, 2 * g + 2)
                    dve.wait_ge(gexp, 2 * g + 2)
                elif k <= 8:
                    dve.wait_ge(route, NR * g + before_step[k])
                if k == 0:
                    done(dve.tensor_scalar(drop[:], pos[:], float(CAP), BIG, ALU.is_ge, ALU.mult))
                    done(dve.tensor_tensor(pbase[:], pos[:], base[:].unsqueeze(1).to_broadcast([P, GT, E]), ALU.add))
                    done(dve.tensor_reduce(msum[:], mask[:].rearrange("p t e -> p e t"), AX_X, ALU.add))
                    done(dve.tensor_reduce(esum[:], ee[:], AX_X, ALU.add))
                elif k == 1:
                    done(dve.tensor_tensor(pbase[:], pbase[:], drop[:], ALU.add))
                    done(dve.reciprocal(esum[:], esum[:]))
                    done(dve.tensor_tensor(macc[:], macc[:], msum[:], ALU.add))
                elif k == 2:
                    done(dve.tensor_tensor(pick[:], oh[:], pbase[:].unsqueeze(1).to_broadcast([P, 2, GT, E]),
                                           ALU.mult))
                    done(dve.tensor_tensor(gk[:], e12[:], esum[:].unsqueeze(1).to_broadcast([P, 2, GT]), ALU.mult))
                elif k == 3:
                    done(dve.tensor_reduce(slot[:], pick[:], AX_X, ALU.add))
                elif k == 4:
                    if gn >= 3:
                        dve.wait_ge(sent[1 - pg], 128 * ((it - 1) if pg == 0 else it))
                    done(dve.tensor_copy(sloti[:], slot[:]))
                    done(dve.scalar_tensor_tensor(gk[:], slot[:], BIG / 2, gk[:], ALU.is_lt, ALU.mult))
                elif k == 5:
                    done(dve.tensor_reduce(esum[:], gk[:].rearrange("p k t -> p t k"), AX_X, ALU.add))
                elif k == 6:
                    done(dve.tensor_scalar(esum[:], esum[:], 1e-6, None, ALU.add))
                elif k == 7:
                    done(dve.reciprocal(esum[:], esum[:]))
                elif k == 8:
                    row = Hrow[:, pg].rearrange("p t r -> p r t")
                    done(dve.tensor_tensor(row[:, D:D + 2, :], gk[:],
                                           esum[:].unsqueeze(1).to_broadcast([P, 2, GT]), ALU.mult))

            def place_ids(it, pg):
                row = Hrow[:, pg].rearrange("p t r -> p r t")
                dve.tensor_scalar(row[:, D + 3:D + 4, :], rk[:, 0:1, :], -1.0, float(E), ALU.mult, ALU.add)
                dve.tensor_copy(row[:, D + 2:D + 3, :], tokf[:].unsqueeze(1))
                dve.tensor_copy(row[:, D + 4:ROW, :],
                                bhot[:, bass.ds(halves(it, 1), 1), :].rearrange("p a k -> p k a")
                                .to_broadcast([P, PARTS * BATCH, GT]))

            def slot_(it, j, n):
                T = it * 8 + j
                G = it * 2 + j // 4
                gn, q, gp = n // 4, j % 4, (j // 4) % 2
                npar = 1 - gp
                tp = j % 2
                stage1 = group_ok(gn + 1)
                small = [0]
                hold = [gn == GROUPS]

                def between(from_q1=True):
                    if q == 1 and (not from_q1 or hold[0]):
                        return
                    k = small[0]
                    small[0] += 1
                    if group_ok(gn - 2):
                        if q == 1 and k < 13:
                            choose(G - 2, k)
                        if q == 3 and k < 9:
                            place(it, G - 2, gp, gn, k)

                if n == 1:
                    dve.wait_ge(mb_in, 32)
                if tile_ok(n):
                    masked_scores(T, 0, tp, n)
                    masked_scores(T, 1, tp, n)
                if q == 3 and group_ok(gn - 2):
                    if gn == GROUPS + 1:
                        dve.wait_ge(last_rows, 1)
                    place_ids(it, gp)
                between(False)
                if tile_ok(n - 1):
                    normalise_heads(T, between)
                between()
                if tile_ok(n + 1):
                    next_tile_lo(T, q, gp, tp, between)
                if tile_ok(n):
                    masked_scores(T, 2, tp, n)
                    between()
                    masked_scores(T, 3, tp, n)
                between()
                if tile_ok(n - 1):
                    attention_lo(T)
                between()
                if stage1 and q in (1, 2):
                    phi(G, 2 * (q - 1), npar)
                    between()
                if tile_ok(n):
                    state(it, T, j)
                between()
                if tile_ok(n - 1):
                    b = halves(it, 0 if j >= 1 else 1)
                    dve.wait_ge(op_full, T)
                    at_least(dve, x1_done, T - 1)
                    dve.tensor_tensor(og[:], MD[:, 0:D], MB[:, bass.ds(b, 1), 0, :].rearrange("p a d -> p (a d)"),
                                      ALU.mult).then_inc(og_done, 1)
                between()
                if tile_ok(n - 2):
                    dve.wait_ge(x1_done, T - 1)
                    dve.bn_stats(st2[:, (j - 2) % 4, :], X[:, bass.ds(T - 2, 1), :].rearrange("p a d -> p (a d)")
                                 ).then_inc(bn2, 1)
                if q == 1 and gn == GROUPS:
                    hold[0] = False
                    dve.wait_ge(bn2, 4 * G)
                    ln_tail(st2, mv2, vp2, nm2, ag2, vpe2, G)
                between()
                if q == 0:
                    if group_ok(gn + 2):
                        ln1_stats(it, G, gp)
                if q == 1:
                    if group_ok(gn - 1) and gn != GROUPS:
                        dve.wait_ge(bn2, 4 * G)
                    if group_ok(gn + 2):
                        dve.wait_ge(bn1, 4 * (G + 3))
                    if stage1:
                        phi(G, 1, npar)
                    if group_ok(gn + 2):
                        ln_tail(st1, mv1, vp1, nm1, ag1, vpe1, G + 3)
                    if group_ok(gn - 1) and gn != GROUPS:
                        ln_tail(st2, mv2, vp2, nm2, ag2, vpe2, G)
                if q == 2 and stage1:
                    phi(G, 3, npar)
                if q == 2 and gn == GROUPS:
                    for t in range(GT):
                        row = N1[:, t, :]
                        dve.wait_ge(n2_ready, 4 * (G - 1) + t + 1)
                        dve.tensor_tensor(row, row, MB[:, BATCH - 1, 2, :], ALU.mult).then_inc(h2_scaled, 1)
                        dve.wait_ge(h2_scaled, 4 * (G - 1) + t + 1)
                        dve.tensor_tensor(row, row, MB[:, BATCH - 1, 1, :], ALU.add).then_inc(h2_done, 1)
                while small[0] < 13:
                    between()
                if q == 0 and group_ok(gn - 3):
                    dve.tensor_scalar(tokf[:], tokf[:], float(GW), None, ALU.add).then_inc(dve_setup, 1)

            run_slots(dve, slot_, early)

            def slots_lo(S, par):
                dve.wait_ge(xt_hi, S + 1)
                dve.tensor_tensor(XT[par][:, 1].rearrange("p c n -> p (c n)"), PJ[par][:],
                                  XT[par][:, 0].rearrange("p c n -> p (c n)").bitcast(F32),
                                  ALU.subtract).then_inc(xt_lo, 1)

            def hidden_lo(S, par):
                for hh in range(2):
                    f = slice(2 * hh, 2 * hh + 2)
                    dve.wait_ge(hid_hi, 2 * S + hh + 1)
                    dve.tensor_tensor(hid[par][1][:, f, :], hid_raw[par][:, f, :],
                                      hid[par][0][:, f, :].bitcast(F32), ALU.subtract).then_inc(hid_lo, 1)

            def slot_meta(ep, s, n):
                S, par = ep * (2 * BS) + s, s % 2
                t = bs[par]
                first, other, wa, wb, w = (t[:, 2 * i:2 * i + 2].unsqueeze(2) for i in range(5))
                row = Xr[s % BS]
                eno = eid[:, bass.ds(ep * 2 + s // BS, 1)]
                dve.wait_ge(rows_in[s % BS], 16 * (ep * 2 + s // BS + 1))
                dve.tensor_scalar(first, row[:, :, D + 3:D + 4], eno, None, ALU.is_equal).then_inc(meta, 1)
                if n >= 2:
                    dve.wait_ge(y_sent[par], 32 * (ep * BS + s // 2))
                dve.tensor_copy(desti[par][:].unsqueeze(2), row[:, :, D + 2:D + 3]).then_inc(meta, 1)
                dve.wait_ge(meta, 5 * S + 1)
                dve.tensor_scalar(other, first, -1.0, 1.0, ALU.mult, ALU.add).then_inc(meta, 1)
                dve.tensor_tensor(wa, row[:, :, D:D + 1], first, ALU.mult)
                dve.wait_ge(meta, 5 * S + 3)
                dve.tensor_tensor(wb, row[:, :, D + 1:D + 2], other, ALU.mult).then_inc(meta, 1)
                dve.wait_ge(meta, 5 * S + 4)
                dve.tensor_tensor(w, wa, wb, ALU.add).then_inc(meta, 1)

            def weighted_rows(ep, s):
                S, par = ep * (2 * BS) + s, s % 2
                dve.wait_ge(gb_done, S + 1)
                dve.wait_ge(y_full, S + 1)
                dve.wait_ge(meta, 5 * S + 5)
                for a in range(2):
                    dve.scalar_tensor_tensor(Ys[par][:, a, :], (MA, MD)[par][:, a * D:(a + 1) * D],
                                             bs[par][:, 8 + a:9 + a], GB[par][:, a * D:(a + 1) * D],
                                             ALU.mult, ALU.mult).then_inc(ys_done, 1)

            def step_b(ep, s, n, last):
                if not (last and s + 2 >= 2 * BS):
                    slots_lo(ep * (2 * BS) + s + 2, s % 2)
                slot_meta(ep, s, n)
                if not (last and s + 1 >= 2 * BS):
                    hidden_lo(ep * (2 * BS) + s + 1, (s + 1) % 2)
                weighted_rows(ep, s)

            slots_lo(0, 0)
            slots_lo(1, 1)
            hidden_lo(0, 0)
            for s in range(2 * BS):
                step_b(0, s, s, False)
            with dve.Fori(1, E // 2 - 1) as ep:
                for s in range(2 * BS):
                    step_b(ep, s, 10, False)
            for s in range(2 * BS):
                step_b(E // 2 - 1, s, 10, True)

        @block.tensor
        def _(pe):
            mm = pe.matmul
            pe.wait_ge(c_silu, 1)
            for m in range(2 * DC):
                for k in range(DC):
                    last = mm(MA[:, m * BATCH:(m + 1) * BATCH], wmod_sb[:, k, m * P:(m + 1) * P], cS[:, k, 0:BATCH],
                              start=(k == 0), stop=(k == DC - 1))
            last.then_inc(mod_mm, 1)
            for hh in range(2):
                for k in range(DC):
                    last = mm(SC[hh][0:PARTS * BATCH, :], cS[:, k, :], wmod_sb[:, k, (2 + 2 * hh) * D:(4 + 2 * hh) * D],
                              start=(k == 0), stop=(k == DC - 1))
                last.then_inc(mod_mm, 1)
            pe.wait_ge(w_in, 64)
            pe.wait_ge(dve_setup, 2)
            pe.wait_ge(consts, N_CONST)

            def scores(T, tp, r):
                if isinstance(T, int) and T == 0 and r == 0:
                    pe.wait_ge(gate_fix, 3)
                if r == 0:
                    pe.wait_ge(q_lo, 2 * T + 2)
                    pe.wait_ge(k_lo, T + 1)
                at_least(pe, sm_done, 4 * T + r - 1)
                rows = slice(32 * r, 32 * r + 32)
                for cc in range(DC):
                    for i, (kp, qp) in enumerate(SPLIT):
                        last = mm(SC[r % 2][:, cc * 2 * P:(cc + 1) * 2 * P], KS[rows, tp, kp, cc, :],
                                  QS[rows, tp, qp, :, cc, :], start=(i == 0), stop=(i == len(SPLIT) - 1))
                last.then_inc(sc_full, 1)

            def head_rows(T, q):
                pe.wait_ge(ot_done, T)
                at_least(pe, og_done, T - 1)
                for i in range(4):
                    last = pe.transpose(MD[:, i * P:(i + 1) * P], OTs[:, i, :], ident[:])
                last.then_inc(on_full, 1)

            def key_rows(T, q, gp):
                at_least(pe, at_lo, T - 1)
                for cc in range(DC):
                    last = pe.transpose(MA[:, cc * P:(cc + 1) * P], KT[:, gp, cc, q * P:(q + 1) * P], ident[:])
                last.then_inc(knt_full, 1)

            def from_state(T, q, gp):
                at_least(pe, ot_done, T)
                at_least(pe, sbd_done, T)
                for i in range(4):
                    mm(OB[:, i * P:(i + 1) * P], Sbd[:, 4 * i:4 * i + 4, :].rearrange("p h w -> p (h w)"),
                       QT[:, gp, i // 2, q * P:(q + 1) * P], start=(i == 0), stop=False, skip_group_check=True)

            def from_tile(T, q, gp, tp, part):
                pe.wait_ge(sm_done, 4 * T + 2 + 2 * part)
                for i in (part, part + 2):
                    for a in range(4):
                        h = 4 * i + a
                        last = mm(OB[32 * a:32 * a + SW, i * P:(i + 1) * P], VA[:, gp, q, h, :], Sm[:, tp, h, :],
                                  start=False, stop=(part == 1), skip_group_check=True)
                if part == 1:
                    last.then_inc(av_done, 1)

            def add_to_state(T, q, gp, tp, j):
                pe.wait_ge(kn_done, T + 1)
                both = SB[:, 0:H * SW]
                if j == 0:
                    mm(both.rearrange("p (h w) -> p h w", h=H), ident[:], Sbd[:, :, 0:SW], start=True, stop=False,
                       skip_group_check=True)
                for cc in range(DC):
                    last = mm(SB[:, cc * HC * SW:(cc + 1) * HC * SW].rearrange("p (h w) -> p h w", h=HC),
                              Kn[:, tp, cc * P:(cc + 1) * P], VA[:, gp, q, cc * HC:(cc + 1) * HC, 0:SW],
                              start=False, stop=True, skip_group_check=True)
                last.then_inc(state_full, 1)

            def attention_columns(T, n):
                pe.wait_ge(an_done, T)
                if tile_ok(n):
                    pe.wait_ge(kn_done, T + 1)
                else:
                    pe.wait_ge(at_lo, T - 1)
                a = An[:].rearrange("p h e -> p (h e)")
                for cc in range(DC):
                    last = pe.transpose(MA[:, cc * P:(cc + 1) * P], a[:, cc * P:(cc + 1) * P], ident[:])
                last.then_inc(at_full, 1)

            def out_product(T):
                pe.wait_ge(at_lo, T)
                for cc in range(DC):
                    for i, (ap, wp) in enumerate(SPLIT):
                        last = mm(MD[:, 0:D], ATs[:, ap, cc, :], w_o[:, wp, cc, :], start=(cc + i == 0),
                                  stop=(cc == DC - 1 and i == len(SPLIT) - 1))
                last.then_inc(op_full, 1)

            def stage1_transposes(G, gn):
                N = G + 1
                pe.wait_ge(n1_ready, 4 * N + 4)
                at_least(pe, pj_read, 6 * N)
                if group_ok(gn - 2):
                    pe.wait_ge(h2t_done, 2 * (G - 2) + 2)
                for cc in range(DC):
                    for t in range(GT):
                        last = pe.transpose(PJ[cc][:, t * P:(t + 1) * P], N1[:, t, cc * P:(cc + 1) * P], ident[:])
                    last.then_inc(pj_full, 1)

            def stage1_qk(G, m):
                N = G + 1
                if isinstance(G, int) and N == 0 and m == 0:
                    pe.wait_ge(w_lo, 2)
                if m == 0:
                    pe.wait_ge(h_raw, 2 * N + 2)
                    pe.wait_ge(h_lo, 2 * N + 2)
                elif m >= 2:
                    pe.wait_ge(pj_read, 6 * N + m - 1)
                for cc in range(DC):
                    for i, (hp, wp) in enumerate(SPLIT):
                        last = mm(PJ[m % 2][:], w_qkv[:, wp, cc, m * P:(m + 1) * P], hT[:, hp, cc, :],
                                  start=(cc + i == 0), stop=(cc == DC - 1 and i == len(SPLIT) - 1))
                last.then_inc(pj_full, 1)

            def stage1_v(G, u):
                N = G + 1
                pe.wait_ge(pj_read, 6 * N + 3 + u)
                for t in range(2):
                    for cc in range(DC):
                        for i, (hp, wp) in enumerate(SPLIT):
                            last = mm(PJ[u][:, t * D:(t + 1) * D],
                                      hT[:, hp, cc, (2 * u + t) * P:(2 * u + t + 1) * P],
                                      w_qkv[:, wp, cc, 2 * D:3 * D], start=(cc + i == 0),
                                      stop=(cc == DC - 1 and i == len(SPLIT) - 1))
                last.then_inc(pj_full, 1)

            def h2_transposes(G, gn, hp):
                pe.wait_ge(h2_done, 4 * (G - 1))
                if group_ok(gn):
                    pe.wait_ge(pj_read, 6 * G + 6)
                else:
                    pe.wait_ge(h2t_done, 2 * (G - 2))
                for cc in range(DC):
                    for t in range(GT):
                        row = N1[:, t, :] if gn == GROUPS + 1 else Hrow[:, hp, t, 0:D]
                        last = pe.transpose(PJ[cc][:, t * P:(t + 1) * P], row[:, cc * P:(cc + 1) * P], ident[:])
                    last.then_inc(h2t_full, 1)

            def logits(G, stage1):
                if stage1:
                    pe.wait_ge(h_raw, 2 * (G + 1) + 2)
                pe.wait_ge(h2t_done, 2 * (G - 2) + 2)
                for cc in range(DC):
                    for t in range(GT):
                        last = mm(PJ[1][32 * t:32 * t + 32, 0:P], w_r[:, cc, :], h2T[:, cc, t * P:(t + 1) * P],
                                  start=(cc == 0), stop=(cc == DC - 1), skip_group_check=True)
                last.then_inc(lgt_full, 1)

            def logit_rows(G):
                pe.wait_ge(lgt_done, G - 1)
                pe.transpose(PJ[1][:, P:2 * P], lgT[:], ident[:]).then_inc(lg_full, 1)

            def positions(G, T, n):
                g = G - 2
                pe.wait_ge(route, NR * g + 13)
                at_least(pe, og_done, T - 1 if tile_ok(n - 2) else TILES)
                all_ = pos_ps
                mm(all_, before[:], mask[:], start=True, stop=True, skip_group_check=True)
                for t in range(GT - 1):
                    mm(all_[:, t + 1:GT, :], ones[:], mask[:, t:t + 1, :].to_broadcast([P, GT - 1 - t, E]),
                       start=False, stop=True, skip_group_check=True)
                mm(all_, ones[:], macc[:].unsqueeze(1).to_broadcast([P, GT, E]), start=False, stop=True,
                   skip_group_check=True).then_inc(pos_full, 1)

            def slot_(it, j, n):
                T = it * 8 + j
                G = it * 2 + j // 4
                gn, q, gp = n // 4, j % 4, (j // 4) % 2
                tp = j % 2
                stage1 = group_ok(gn + 1)
                for r in range(2):
                    if tile_ok(n):
                        scores(T, tp, r)
                    if r == 0 and q == 1 and group_ok(gn - 2):
                        logit_rows(G)
                    if r == 0 and q == 3 and group_ok(gn - 2):
                        positions(G, T, n)
                if q == 0 and group_ok(gn - 2):
                    h2_transposes(G, gn, gp)
                if tile_ok(n - 1):
                    if q == 3 and group_ok(gn - 2):
                        pe.wait_ge(taken, 2 * (G - 2) + 2)
                    head_rows(T, q)
                if tile_ok(n):
                    key_rows(T, q, gp)
                    from_state(T, q, gp)
                if stage1:
                    if q == 0:
                        stage1_transposes(G, gn)
                    elif q == 1:
                        stage1_qk(G, 0)
                    elif q == 2:
                        stage1_qk(G, 2)
                    else:
                        stage1_v(G, 0)
                if tile_ok(n):
                    scores(T, tp, 2)
                    scores(T, tp, 3)
                if tile_ok(n - 1):
                    attention_columns(T, n)
                if tile_ok(n):
                    from_tile(T, q, gp, tp, 0)
                    add_to_state(T, q, gp, tp, j)
                if stage1:
                    if q == 1:
                        if group_ok(gn - 2):
                            pe.wait_ge(taken, 2 * (G - 2) + 1)
                        stage1_qk(G, 1)
                    elif q == 2:
                        stage1_qk(G, 3)
                    elif q == 3:
                        stage1_v(G, 1)
                if q == 0 and group_ok(gn - 2):
                    logits(G, stage1)
                if tile_ok(n) and q == 0:
                    from_tile(T, q, gp, tp, 1)
                if tile_ok(n - 1):
                    out_product(T)
                if tile_ok(n) and q != 0:
                    from_tile(T, q, gp, tp, 1)

            run_slots(pe, slot_)

            pe.wait_ge(route, NR * GROUPS)
            pe.wait_ge(w_lo, 3)
            pe.wait_ge(gb_split, 8)

            def slot_columns(ep, s, n):
                S, par = ep * (2 * BS) + s, s % 2
                pe.wait_ge(rows_in[s % BS], 16 * (ep * 2 + s // BS + 1))
                if n >= 2:
                    pe.wait_ge(xt_lo, S - 1)
                for cc in range(DC):
                    for a in range(2):
                        last = pe.transpose(PJ[par][:, cc * BW + a * P:cc * BW + (a + 1) * P],
                                            Xr[s % BS][:, a, cc * P:(cc + 1) * P], ident[:])
                if n >= 1:
                    pe.wait_ge(oh_done, S)
                for a in range(2):
                    last = pe.transpose(OB[0:PARTS * BATCH, a * P:(a + 1) * P],
                                        Xr[s % BS][:, a, D + 4:ROW], ident[:])
                last.then_inc(xt_full, 1)

            def gate(ep, s, n):
                S, par = ep * (2 * BS) + s, s % 2
                if n >= 1:
                    pe.wait_ge(gb_done, S)
                pe.wait_ge(oh_done, S + 1)
                for a in range(2):
                    last = mm(SB[:, a * D:(a + 1) * D], ohT[par][:, a * P:(a + 1) * P], gbp[:], start=True, stop=True)
                last.then_inc(gb_full, 1)
                pe.wait_ge(xt_lo, S + 1)
                for hh in range(2):
                    if n >= 1:
                        pe.wait_ge(silu_done, 2 * (S - 1) + hh + 1)
                    for f in (2 * hh, 2 * hh + 1):
                        for cc in range(DC):
                            for i, (wp, xp) in enumerate(SPLIT):
                                last = mm(SC[hh][:, (f % 2) * BW:(f % 2 + 1) * BW],
                                          w_g[:, wp, cc, f * P:(f + 1) * P], XT[par][:, xp, cc, :],
                                          start=(cc + i == 0), stop=(cc == DC - 1 and i == len(SPLIT) - 1))
                    last.then_inc(gate_full, 1)

            def down(ep, s, n):
                S, par, k = ep * (2 * BS) + s, s % 2, s // BS
                if n >= 2:
                    pe.wait_ge(ys_done, 2 * (S - 1))
                pe.wait_ge(hid_lo, 2 * S + 2)
                if s % BS == 0:
                    pe.wait_ge(wd_lo, ep * 2 + k + 1)
                for a in range(2):
                    for f in range(FC):
                        for i, (hp, wp) in enumerate(SPLIT):
                            last = mm((MA, MD)[par][:, a * D:(a + 1) * D], hid[par][hp][:, f, a * P:(a + 1) * P],
                                      WD[k][wp][:, f, :], start=(f + i == 0),
                                      stop=(f == FC - 1 and i == len(SPLIT) - 1))
                last.then_inc(y_full, 1)

            def step_b(ep, s, n, last):
                for ahead, part in ((2, slot_columns), (1, gate)):
                    if not (last and s + ahead >= 2 * BS):
                        part(*((ep, s + ahead) if s + ahead < 2 * BS else (ep + 1, s + ahead - 2 * BS)), n + ahead)
                down(ep, s, n)

            slot_columns(0, 0, 0)
            slot_columns(0, 1, 1)
            gate(0, 0, 0)
            for s in range(2 * BS):
                step_b(0, s, s, False)
            with pe.Fori(1, E // 2 - 1) as ep:
                for s in range(2 * BS):
                    step_b(ep, s, 10, False)
            for s in range(2 * BS):
                step_b(E // 2 - 1, s, 10, True)


def kernel(L0_attn_x, L0_attn_w_qkv, L0_attn_w_out, L0_ffn_w_router, L0_ffn_w_gate, L0_ffn_w_down, L0_c, L0_wmod):
    import numpy as np
    import concourse.bacc as bacc
    from concourse.bass_utils import run_bass_kernel_spmd

    def chunked(a):
        a = np.asarray(a)
        return np.ascontiguousarray(a.reshape(DC, P, -1).transpose(1, 0, 2))

    wdn = np.asarray(L0_ffn_w_down).transpose(0, 2, 1).reshape(E, FC, P, D).transpose(0, 2, 1, 3)
    arrays = {
        "x": np.ascontiguousarray(np.asarray(L0_attn_x).reshape(TOK, D)),
        "wqkv": chunked(np.asarray(L0_attn_w_qkv).T),
        "wo": chunked(np.asarray(L0_attn_w_out).T),
        "wr": chunked(np.asarray(L0_ffn_w_router).T),
        "wg": chunked(np.asarray(L0_ffn_w_gate).T),
        "wd": np.ascontiguousarray(wdn.reshape(E * P, FC * D)),
        "c": chunked(np.asarray(L0_c).T),
        "wmod": chunked(L0_wmod),
    }
    nc = bacc.Bacc("TRN2", target_bir_lowering=False, num_devices=1)
    ins = [nc.dram_tensor(k, a.shape, F32, kind="ExternalInput").ap() for k, a in arrays.items()]
    out = nc.dram_tensor("out", (TOK, D), F32, kind="ExternalOutput").ap()
    xe = nc.dram_tensor("slot_rows", (SLOTS, ROW), F32, kind="Internal").ap()
    mod_rows = nc.dram_tensor("mod_rows", (BATCH, 3 * D), F32, kind="Internal").ap()
    adaln_block(nc, *ins, out, xe, mod_rows)
    r = run_bass_kernel_spmd(nc, [arrays], core_ids=[0])
    return np.asarray(r.results[0]["out"]).reshape(BATCH, SEQ, D)
```
